# Optimizing a Trainium2 kernel written in Bass

```python
import numpy as np
import jax
import jax.numpy as jnp

def _softmax(x, axis=-1):
    return jax.nn.softmax(x, axis=axis)

def _gelu(x):
    return jax.nn.gelu(x, approximate=True)

def _silu(x):
    return jax.nn.silu(x)

def _sigmoid(x):
    return jax.nn.sigmoid(x)

def _layernorm(x, axis=-1, eps=1e-05):
    m = jnp.mean(x, axis=axis, keepdims=True)
    v = jnp.var(x, axis=axis, keepdims=True)
    return (x - m) / jnp.sqrt(v + eps)

def _scatter_add(tgt, idx, src, axis=0):
    return tgt.at[idx].add(src)

def _segment_sum(src, seg, n):
    return jax.ops.segment_sum(src, seg, n)
kernel_name = 'mk_vit_tower_postln_d1_tok_img768_r4_a96de0'

def setup_inputs(seed: int=0):
    np.random.seed(seed)
    _w = jnp.asarray

    def _rec_inputs():
        import jax
        import jax.numpy as jnp
        _rk = jax.random.key(seed)
        x = 7.57192e-06 + 1.00007 * jax.random.normal(jax.random.fold_in(_rk, 1), (64, 3, 518, 518), jnp.float32)
        return x
    x = _rec_inputs()

    def _L0_tok_setup():
        import jax, jax.numpy as jnp
        import numpy as np
        IMAGE_SIZE = 224
        NUM_CHANNELS = 3
        NUM_BINS = 16
        EMBED_DIM = 192
        FILTER_SIZE = 96
        CROP = 2 * FILTER_SIZE
        BIN_SIZE = CROP * CROP // NUM_BINS
        IN_FEATURES = NUM_CHANNELS * BIN_SIZE
        SEQ_LEN = NUM_BINS + 1

        def _sorted_radial_indices(H, W):
            y, x = np.meshgrid(np.arange(H), np.arange(W), indexing='ij')
            d = np.sqrt((x - W / 2.0) ** 2 + (y - H / 2.0) ** 2).reshape(-1)
            return jnp.asarray(np.argsort(d, kind='stable'))

        def _sinusoidal_pe(seq_len, d):
            pos = np.arange(seq_len)[:, None].astype(np.float32)
            div = np.exp(np.arange(0, d, 2).astype(np.float32) * (-np.log(10000.0) / d))
            pe = np.zeros((seq_len, d), dtype=np.float32)
            pe[:, 0::2] = np.sin(pos * div)
            pe[:, 1::2] = np.cos(pos * div)
            return jnp.asarray(pe)
        key = jax.random.key(seed)
        k1, k2, k3 = jax.random.split(key, 3)
        images = jax.random.normal(k1, (64, NUM_CHANNELS, IMAGE_SIZE, IMAGE_SIZE), dtype=jnp.float32)
        cls_token = jax.random.normal(k2, (1, 1, EMBED_DIM), dtype=jnp.float32)
        W = jax.random.normal(k3, (EMBED_DIM, IN_FEATURES), dtype=jnp.float32) * 0.02
        b = jnp.zeros((EMBED_DIM,), dtype=jnp.float32)
        return {'images': images, 'cls_token': cls_token, 'W': W, 'b': b}
    _L0_tok_all = _L0_tok_setup()
    _L0_tok_in = {k: v for k, v in _L0_tok_all.items() if k in ('cls_token', 'W', 'b')}
    del _L0_tok_all

    def _L0_attn_setup():
        import jax, jax.numpy as jnp
        import numpy as np
        NUM_HEADS = 12

        def _split_heads(x, N, S):
            return x.reshape(N, S, NUM_HEADS, -1).transpose(0, 2, 1, 3)
        key = jax.random.key(seed)
        ks = jax.random.split(key, 12)
        N, S, E, R, RM = (8, 256, 192, 96, 64)
        hd = E // NUM_HEADS
        s = 0.02
        return {'hidden_states': jax.random.normal(ks[0], (N, S, E), dtype=jnp.float32), 'U_Q': jax.random.normal(ks[1], (R, E), dtype=jnp.float32) * s, 'V_Q': jax.random.normal(ks[2], (E, R), dtype=jnp.float32) * s, 'U_K': jax.random.normal(ks[3], (R, E), dtype=jnp.float32) * s, 'V_K': jax.random.normal(ks[4], (E, R), dtype=jnp.float32) * s, 'U_V': jax.random.normal(ks[5], (R, E), dtype=jnp.float32) * s, 'V_V': jax.random.normal(ks[6], (E, R), dtype=jnp.float32) * s, 'bias_q': jax.random.normal(ks[7], (E,), dtype=jnp.float32) * s, 'bias_k': jax.random.normal(ks[8], (E,), dtype=jnp.float32) * s, 'bias_v': jax.random.normal(ks[9], (E,), dtype=jnp.float32) * s, 'M_U': jax.random.normal(ks[10], (hd, RM), dtype=jnp.float32) * 0.1, 'M_V': jax.random.normal(ks[11], (RM, hd), dtype=jnp.float32) * 0.1}
    _L0_attn_all = _L0_attn_setup()
    _L0_attn_in = {k: v for k, v in _L0_attn_all.items() if k in ('U_Q', 'V_Q', 'U_K', 'V_K', 'U_V', 'V_V', 'bias_q', 'bias_k', 'bias_v', 'M_U', 'M_V')}
    del _L0_attn_all

    def _L0_ffn_setup():
        import jax, jax.numpy as jnp
        import numpy as np
        N_EXPERTS = 8
        TOPK = 2
        B, S, H, F = (8, 512, 192, 768)
        key = jax.random.key(seed)
        ks = jax.random.split(key, 4)
        return {'hidden_states': jax.random.normal(ks[0], (B, S, H), dtype=jnp.float32), 'Wr': jax.random.normal(ks[1], (H, N_EXPERTS), dtype=jnp.float32) * 0.02, 'br': jnp.zeros((N_EXPERTS,), dtype=jnp.float32), 'Wfc': jax.random.normal(ks[2], (N_EXPERTS, H, F), dtype=jnp.float32) * 0.02, 'bfc': jnp.zeros((N_EXPERTS, F), dtype=jnp.float32), 'Wproj': jax.random.normal(ks[3], (N_EXPERTS, F, H), dtype=jnp.float32) * 0.02, 'bproj': jnp.zeros((N_EXPERTS, H), dtype=jnp.float32)}
    _L0_ffn_all = _L0_ffn_setup()
    _L0_ffn_in = {k: v for k, v in _L0_ffn_all.items() if k in ('Wr', 'br', 'Wfc', 'bfc', 'Wproj', 'bproj')}
    del _L0_ffn_all
    return {'x': x, 'L0_tok_cls_token': _L0_tok_in['cls_token'], 'L0_tok_W': _L0_tok_in['W'], 'L0_tok_b': _L0_tok_in['b'], 'L0_attn_U_Q': _L0_attn_in['U_Q'], 'L0_attn_V_Q': _L0_attn_in['V_Q'], 'L0_attn_U_K': _L0_attn_in['U_K'], 'L0_attn_V_K': _L0_attn_in['V_K'], 'L0_attn_U_V': _L0_attn_in['U_V'], 'L0_attn_V_V': _L0_attn_in['V_V'], 'L0_attn_bias_q': _L0_attn_in['bias_q'], 'L0_attn_bias_k': _L0_attn_in['bias_k'], 'L0_attn_bias_v': _L0_attn_in['bias_v'], 'L0_attn_M_U': _L0_attn_in['M_U'], 'L0_attn_M_V': _L0_attn_in['M_V'], 'L0_ffn_Wr': _L0_ffn_in['Wr'], 'L0_ffn_br': _L0_ffn_in['br'], 'L0_ffn_Wfc': _L0_ffn_in['Wfc'], 'L0_ffn_bfc': _L0_ffn_in['bfc'], 'L0_ffn_Wproj': _L0_ffn_in['Wproj'], 'L0_ffn_bproj': _L0_ffn_in['bproj']}

def reference(x, L0_tok_cls_token, L0_tok_W, L0_tok_b, L0_attn_U_Q, L0_attn_V_Q, L0_attn_U_K, L0_attn_V_K, L0_attn_U_V, L0_attn_V_V, L0_attn_bias_q, L0_attn_bias_k, L0_attn_bias_v, L0_attn_M_U, L0_attn_M_V, L0_ffn_Wr, L0_ffn_br, L0_ffn_Wfc, L0_ffn_bfc, L0_ffn_Wproj, L0_ffn_bproj):
    import jax
    import jax.numpy as jnp

    def _L0_tok_ref(images, cls_token, W, b):
        import jax, jax.numpy as jnp
        import numpy as np
        IMAGE_SIZE = 224
        NUM_CHANNELS = 3
        NUM_BINS = 16
        EMBED_DIM = 192
        FILTER_SIZE = 96
        CROP = 2 * FILTER_SIZE
        BIN_SIZE = CROP * CROP // NUM_BINS
        IN_FEATURES = NUM_CHANNELS * BIN_SIZE
        SEQ_LEN = NUM_BINS + 1

        def _sorted_radial_indices(H, W):
            y, x = np.meshgrid(np.arange(H), np.arange(W), indexing='ij')
            d = np.sqrt((x - W / 2.0) ** 2 + (y - H / 2.0) ** 2).reshape(-1)
            return jnp.asarray(np.argsort(d, kind='stable'))

        def _sinusoidal_pe(seq_len, d):
            pos = np.arange(seq_len)[:, None].astype(np.float32)
            div = np.exp(np.arange(0, d, 2).astype(np.float32) * (-np.log(10000.0) / d))
            pe = np.zeros((seq_len, d), dtype=np.float32)
            pe[:, 0::2] = np.sin(pos * div)
            pe[:, 1::2] = np.cos(pos * div)
            return jnp.asarray(pe)
        B, C, H, Wd = images.shape
        f = jnp.fft.fftshift(jnp.fft.fft2(images))
        y, x = jnp.meshgrid(jnp.arange(H), jnp.arange(Wd), indexing='ij')
        mask = (jnp.abs(x - Wd // 2) <= FILTER_SIZE) & (jnp.abs(y - H // 2) <= FILTER_SIZE)
        f = f * mask.astype(f.dtype)
        cy, cx = (H // 2, Wd // 2)
        f = f[:, :, cy - FILTER_SIZE:cy + FILTER_SIZE, cx - FILTER_SIZE:cx + FILTER_SIZE]
        power = jnp.abs(f).astype(jnp.float32)
        idx = _sorted_radial_indices(CROP, CROP)
        power_sorted = power.reshape(B, C, CROP * CROP)[:, :, idx]
        ps = power_sorted.reshape(B, C, NUM_BINS, BIN_SIZE)
        tokens = ps.transpose(0, 2, 1, 3).reshape(B, NUM_BINS, C * BIN_SIZE)
        tokens = jnp.einsum('bnf,ef->bne', tokens, W) + b
        cls = jnp.broadcast_to(cls_token, (B, 1, EMBED_DIM))
        tokens = jnp.concatenate([cls, tokens], axis=1)
        tokens = tokens + _sinusoidal_pe(SEQ_LEN, EMBED_DIM)[None]
        return tokens

    def _L0_attn_ref(hidden_states, U_Q, V_Q, U_K, V_K, U_V, V_V, bias_q, bias_k, bias_v, M_U, M_V):
        import jax, jax.numpy as jnp
        import numpy as np
        NUM_HEADS = 12

        def _split_heads(x, N, S):
            return x.reshape(N, S, NUM_HEADS, -1).transpose(0, 2, 1, 3)
        N, S, E = hidden_states.shape
        hd = E // NUM_HEADS
        scale = 1.0 / jnp.sqrt(jnp.asarray(hd, hidden_states.dtype))
        q = hidden_states @ V_Q @ U_Q + bias_q
        k = hidden_states @ V_K @ U_K + bias_k
        v = hidden_states @ V_V @ U_V + bias_v
        q = _split_heads(q, N, S)
        k = _split_heads(k, N, S)
        v = _split_heads(v, N, S)
        qm = jnp.einsum('bhsd,dr->bhsr', q, M_U)
        km = jnp.einsum('rd,bhtd->bhrt', M_V, k)
        attn = jnp.einsum('bhsr,bhrt->bhst', qm, km) * scale
        attn = jax.nn.softmax(attn, axis=-1)
        out = jnp.einsum('bhst,bhtd->bhsd', attn, v)
        out = out.transpose(0, 2, 1, 3).reshape(N, S, E)
        return out

    def _L0_ffn_ref(hidden_states, Wr, br, Wfc, bfc, Wproj, bproj):
        import jax, jax.numpy as jnp
        import numpy as np
        N_EXPERTS = 8
        TOPK = 2
        B, S, H, F = (8, 512, 192, 768)
        b, s, h = hidden_states.shape
        x = hidden_states.reshape(-1, h)
        logits = x @ Wr + br
        probs = jax.nn.softmax(logits, axis=-1)
        topk_w, topk_i = jax.lax.top_k(probs, TOPK)
        topk_w = topk_w / jnp.sum(topk_w, axis=-1, keepdims=True)
        out = jnp.zeros_like(x)
        for e in range(N_EXPERTS):
            w = jnp.sum(jnp.where(topk_i == e, topk_w, 0.0), axis=-1)
            he = jax.nn.gelu(x @ Wfc[e] + bfc[e], approximate=True) @ Wproj[e] + bproj[e]
            out = out + w[:, None] * he
        return out.reshape(b, s, h)
    h = _L0_tok_ref(x, L0_tok_cls_token, L0_tok_W, L0_tok_b)
    h = _layernorm(h + _L0_attn_ref(h, L0_attn_U_Q, L0_attn_V_Q, L0_attn_U_K, L0_attn_V_K, L0_attn_U_V, L0_attn_V_V, L0_attn_bias_q, L0_attn_bias_k, L0_attn_bias_v, L0_attn_M_U, L0_attn_M_V), axis=-1)
    h = _layernorm(h + _L0_ffn_ref(h, L0_ffn_Wr, L0_ffn_br, L0_ffn_Wfc, L0_ffn_bfc, L0_ffn_Wproj, L0_ffn_bproj), axis=-1)
    return h

_drawn_inputs = setup_inputs


def setup_inputs(seed=0):
    import zlib

    import numpy as np

    out = dict(_drawn_inputs(seed))
    spreads = {'L0_tok_b': (0.0, 2.0),
     'L0_ffn_br': (0.0, 0.1),
     'L0_ffn_bfc': (0.0, 0.4),
     'L0_ffn_bproj': (0.0, 0.1)}
    factors = {'L0_tok_cls_token': 3.532,
     'L0_attn_bias_q': 8.0,
     'L0_attn_bias_k': 200.0,
     'L0_attn_bias_v': 200.0}
    for name, (base, spread) in spreads.items():
        noise = np.random.default_rng([zlib.crc32(name.encode()), seed]).standard_normal(out[name].shape)
        drawn = base * np.exp(spread * noise) if base else spread * noise
        out[name] = jnp.asarray(drawn.astype(out[name].dtype))
    for name, factor in factors.items():
        out[name] = (out[name] * factor).astype(out[name].dtype)
    return out
```

```python
from contextlib import ExitStack

import numpy as np

import concourse.bass as bass
from concourse import mybir

F32 = mybir.dt.float32
I32 = mybir.dt.int32
ALU = mybir.AluOpType
ACT = mybir.ActivationFunctionType
AXX = mybir.AxisListType.X

P = 128
N = 518
HALF = N // 2
KEEP = 96
NE = KEEP // 2 + 1
U = 4 * NE
V = 2 * NE
NL = 6
LEFT = [0, 129, 130, HALF, 388, 389]
FOLD = np.arange(1, P + 1)
FOLDED = [FOLD, HALF - FOLD, HALF + FOLD, N - FOLD]
B, C, E = 64, 3, 192
IMAGES = B * C
STAGE = 48
ROWS = V * 2 * V
BINS, BINSZ = 16, 2304
JC = BINSZ // P
EH = E // 2
S = BINS + 1
T = S * B
HEADS, HD, RANK, RM = 12, 16, 96, 64
HH = HEADS // 2
EXPERTS, FF = 8, 768
FC = FF // P
GT = 2 * B
TILES = (S + 1) // 2
EPS = 1e-5


def trig(pos):
    a = 2 * np.pi / N * np.asarray(pos, np.float64)[:, None]
    fe, fo = 2 * np.arange(NE), 2 * np.arange(NE) + 1
    t = np.stack([np.cos(a * fe), np.cos(a * fo), np.sin(a * fe), np.sin(a * fo)], 1)
    t[:, 1::2, NE - 1] = 0
    return t.reshape(-1, U).astype(np.float32)


def folded_trig():
    t = trig(FOLD).reshape(P, 4, NE)
    out = np.stack([t[:, 0], t[:, 2], t[:, 0], -t[:, 2], t[:, 1], t[:, 3], -t[:, 1], t[:, 3]], 1)
    return np.ascontiguousarray(out.reshape(P, 4, V))


def radial_rows():
    side = 2 * KEEP
    y, x = np.meshgrid(np.arange(side), np.arange(side), indexing="ij")
    d = np.sqrt((x - side / 2.0) ** 2 + (y - side / 2.0) ** 2).reshape(-1)
    idx = np.argsort(d, kind="stable")
    fy, fx = idx // side - KEEP, idx % side - KEEP
    v, u = np.abs(fy), np.where(fy < 0, -fx, fx)
    place = lambda f: (f % 2) * NE + f // 2
    row = (place(v) * 2 + (u < 0)) * V + place(np.abs(u))
    row = row.reshape(BINS, JC, P).transpose(2, 1, 0)
    return np.ascontiguousarray(row.reshape(P, JC * BINS).astype(np.int32))


def position_code():
    pos = np.arange(S)[:, None].astype(np.float32)
    div = np.exp(np.arange(0, E, 2).astype(np.float32) * (-np.log(10000.0) / E))
    pe = np.zeros((S, E), np.float32)
    pe[:, 0::2], pe[:, 1::2] = np.sin(pos * div), np.cos(pos * div)
    return np.ascontiguousarray(pe.T.reshape(2, EH, S).transpose(1, 0, 2))


def dft_phase(nc, d, scratch):
    LB = IMAGES * NL // P
    PRE = 3
    XB = 4
    assert LB % PRE == 0 and IMAGES % XB == 0 and STAGE % XB == 0
    STEPS = STAGE // XB
    STAGES = IMAGES // STAGE
    with ExitStack() as ctx:
        sb = lambda n, s: ctx.enter_context(nc.sbuf_tensor(n, s, F32))
        ps = lambda n: ctx.enter_context(nc.psum_tensor(n, [P, 512], F32))
        sem = lambda n: ctx.enter_context(nc.semaphore(n))
        image = sb("image", [P, XB, 4, 512])
        fold_y = sb("fold_y", [P, 2, 4, 512])
        high = sb("high", [P, 2, 2 * U])
        fold_x = sb("fold_x", [P, 2, 4, U])
        second = sb("second", [V, 2, U])
        parts = sb("parts", [V, 2, 2, U])
        squares = sb("squares", [V, 2, 2, U])
        power2 = sb("power2", [V, 2, 2 * V])
        mags = sb("mags", [V, 2 * V, 2 * STAGE])
        ktab = sb("ktab", [P, 4, V])
        full = sb("full", [P, 4, U])
        left = sb("left", [NL, U])
        low = sb("low", [2 * NL, XB, 2, U])
        pre_c = sb("pre_c", [P, PRE, 4, P])
        pre_r = sb("pre_r", [P, PRE, 4, P])
        pre_k = sb("pre_k", [NL, PRE, P])
        pre_o = sb("pre_o", [P, PRE, 2, U])
        rows_ps = [[ps(f"rows{i}{h}") for h in range(2)] for i in range(2)]
        cols_ps = [ps(f"cols{i}") for i in range(2)]
        pre_ps = [ps(f"pre{i}") for i in range(2)]

        tables_in = sem("tables_in")
        pre_in = [sem(f"pre_in{i}") for i in range(PRE)]
        pre_done = sem("pre_done")
        pre_copied = sem("pre_copied")
        pre_out = [sem(f"pre_out{i}") for i in range(PRE)]
        image_in = [sem(f"image_in{i}") for i in range(XB)]
        low_in = [sem(f"low_in{i}") for i in range(XB)]
        folded_y = sem("folded_y")
        rows_high = sem("rows_high")
        rows_low = sem("rows_low")
        high_copied = sem("high_copied")
        folded_x = sem("folded_x")
        cols_done = sem("cols_done")
        second_copied = sem("second_copied")
        parts_done = sem("parts_done")
        squared = sem("squared")
        added = sem("added")
        rooted = sem("rooted")
        stage_out = [sem(f"stage_out{i}") for i in range(2)]
        block = ctx.enter_context(nc.Block())

        @block.sync
        def _(sp):
            for dst, src in ((ktab[:], d["ktab"]), (full[:], d["full"]), (left[:], d["left"])):
                sp.dma_start(dst, src).then_inc(tables_in, 16)
            for i in range(XB):
                sp.dma_start(low[NL:, i, 0, :], d["left"]).then_inc(tables_in, 16)
                sp.dma_start(low[0:NL, i, 1, :], d["left"]).then_inc(tables_in, 16)

            def load_pre(m, i):
                sp.dma_start(pre_c[:, i], d["x_cols"][m]).then_inc(pre_in[i], 16)
                sp.dma_start(pre_r[:, i], d["x_rows"][m]).then_inc(pre_in[i], 16)
                sp.dma_start(pre_k[:, i], d["x_corner"][m]).then_inc(pre_in[i], 16)

            def load_image(n, i):
                sp.dma_start(image[:, i], d["x"][n]).then_inc(image_in[i], 16)

            def load_low(n, i):
                rows = bass.ds(n, 1) if not isinstance(n, int) else slice(n, n + 1)
                sp.dma_start(low[0:NL, i, 0, :], scratch["left_cols"][rows].rearrange("a l u -> (a l) u"))\
                    .then_inc(low_in[i], 16)
                sp.dma_start(low[NL:, i, 1, :], scratch["left_rows"][rows].rearrange("a l u -> (a l) u"))\
                    .then_inc(low_in[i], 16)

            for i in range(PRE):
                load_pre(i, i)
            for i in range(XB):
                load_image(i, i)
            for m in range(LB):
                i = m % PRE
                sp.wait_ge(pre_copied, m + 1)
                for side, name in enumerate(("left_cols", "left_rows")):
                    sp.dma_start(scratch[name].rearrange("a l u -> (a l) u")[m * P:(m + 1) * P],
                                 pre_o[:, i, side]).then_inc(pre_out[i], 16)
                if m + PRE < LB:
                    load_pre(m + PRE, i)
            for i in range(PRE):
                sp.wait_ge(pre_out[i], 32 * (LB // PRE))
            for i in range(XB):
                load_low(i, i)

            def flush(s):
                sp.dma_start(scratch["power"].rearrange("(v r) (s i) -> s v r i", v=V, i=STAGE)[s],
                             mags[:, :, (s % 2) * STAGE:(s % 2 + 1) * STAGE]).then_inc(stage_out[s % 2], 16)

            for s in range(STAGES):
                last = s == STAGES - 1
                with sp.Fori(0, STEPS - last) as k:
                    for i in range(XB):
                        n = sp.snap(k * XB + (s * STAGE + i + XB))
                        done = sp.snap(k * XB + (s * STAGE + i + 1))
                        sp.wait_ge(folded_y, done)
                        sp.dma_start(image[:, i], d["x"][bass.ds(n, 1)].rearrange("a p r x -> (a p) r x"))\
                            .then_inc(image_in[i], 16)
                        sp.wait_ge(cols_done, done)
                        load_low(n, i)
                sp.wait_ge(rooted, (s + 1) * STAGE)
                flush(s)
            for i in range(2):
                sp.wait_ge(stage_out[i], 16 * (STAGES // 2))

        @block.tensor
        def _(pe):
            pe.wait_ge(tables_in, 16 * (3 + 2 * XB))
            for m in range(LB):
                i, o = m % PRE, pre_ps[m % 2]
                pe.wait_ge(pre_in[i], 48 * (m // PRE + 1))
                if m >= 2:
                    pe.wait_ge(pre_copied, m - 1)
                for q in range(4):
                    nc.tensor.matmul(o[:, 0:U], pre_c[:, i, q], full[:, q], start=q == 0, stop=q == 3)
                for q in range(4):
                    nc.tensor.matmul(o[:, U:2 * U], pre_r[:, i, q], full[:, q], start=q == 0, stop=False)
                nc.tensor.matmul(o[:, U:2 * U], pre_k[:, i], left[:], start=False, stop=True)\
                    .then_inc(pre_done, 1)

            def parity(a, g):
                return a.rearrange("p (t g f) -> p t g f", t=2, g=2)[:, :, g]

            def row_transform(n, i, peeled):
                pe.wait_ge(folded_y, n + 1)
                if not peeled:
                    pe.wait_ge(folded_x, n - 1)
                for h in (1, 0):
                    for j in range(2):
                        q = 2 * h + j
                        for g in range(2):
                            for a in range(2):
                                mm = nc.tensor.matmul(
                                    parity(rows_ps[i][h][:, j * U:(j + 1) * U], g),
                                    fold_y[:, i, 2 * g + a, q * P:(q + 1) * P], ktab[:, 2 * g + a],
                                    start=a == 0, stop=a == 1)
                    mm.then_inc(rows_high if h else rows_low, 1)

            def steps(base, peeled):
                for j in range(XB):
                    row_transform(base + j, j % 2, peeled and j < 2)
                    if peeled and j == 0:
                        continue
                    columns(base, j - 1, peeled)

            def columns(base, j, peeled):
                i, slot, n = j % 2, j % XB, base + j
                pe.wait_ge(folded_x, n + 1)
                if not peeled or j >= 2:
                    pe.wait_ge(parts_done, n - 1)
                pe.wait_ge(low_in[slot], 8 * (base + j - slot) + 32)
                for t in range(2):
                    o = cols_ps[i][0:V, t * U:(t + 1) * U]
                    part = slice(t * V, (t + 1) * V)
                    nc.tensor.matmul(o, low[:, slot, 0, part], low[:, slot, 1], start=True, stop=False,
                                     skip_group_check=True)
                    for g in range(2):
                        for a in range(2):
                            mm = nc.tensor.matmul(parity(o, g), fold_x[:, i, 2 * g + a, part],
                                                  ktab[:, 2 * g + a], start=False, stop=g == 1 and a == 1,
                                                  skip_group_check=True)
                mm.then_inc(cols_done, 1)

            steps(0, True)
            with pe.Fori(XB, IMAGES, XB) as base:
                steps(base, False)
            columns(IMAGES - XB, XB - 1, False)

        @block.vector
        def _(dve):
            def fold_rows(n, j, peeled):
                i, s = j % 2, j % XB
                dve.wait_ge(image_in[s], 4 * (n - s) + 16)
                if not peeled:
                    dve.wait_ge(rows_low, n - 1)
                a, b = image[:, s, 0:2], image[:, s, 2:4]
                nc.vector.tensor_tensor(fold_y[:, i, 0:2], a, b, ALU.add)
                nc.vector.tensor_tensor(fold_y[:, i, 2:4], a, b, ALU.subtract).then_inc(folded_y, 1)

            def fold_columns(n, j, peeled):
                i = j % 2
                dve.wait_ge(rows_low, n + 1)
                dve.wait_ge(high_copied, n + 1)
                if not peeled:
                    dve.wait_ge(cols_done, n - 1)
                a, b = rows_ps[i][0][:, 0:2 * U], high[:, i]
                for k, op in ((0, ALU.add), (1, ALU.subtract)):
                    ins = nc.vector.tensor_tensor(
                        fold_x[:, i, 2 * k:2 * k + 2].rearrange("p a u -> p (a u)"), a, b, op)
                ins.then_inc(folded_x, 1)

            def combine(n, j, peeled):
                i = j % 2
                dve.wait_ge(second_copied, n + 1)
                if not peeled:
                    dve.wait_ge(squared, n - 1)
                a, b = cols_ps[i][0:V, 0:U], second[:, i]
                nc.vector.tensor_tensor(parts[:, i, 0], a, b, ALU.subtract)
                nc.vector.tensor_tensor(parts[:, i, 1], a, b, ALU.add).then_inc(parts_done, 1)

            def steps(base, peeled, last):
                for j in range(XB):
                    if not (last and j == XB - 1):
                        fold_rows(base + j + 1, j + 1, peeled and j + 1 < 2)
                    fold_columns(base + j, j, peeled and j < 2)
                    if not (peeled and j == 0):
                        combine(base + j - 1, j - 1, peeled and j - 1 < 2)

            fold_rows(0, 0, True)
            steps(0, True, False)
            with dve.Fori(XB, IMAGES - XB, XB) as base:
                steps(base, False, False)
            steps(IMAGES - XB, False, True)
            combine(IMAGES - 1, XB - 1, False)

        @block.scalar
        def _(act):
            for m in range(LB):
                i = m % PRE
                act.wait_ge(pre_done, m + 1)
                if m >= PRE:
                    act.wait_ge(pre_out[i], 32 * (m // PRE))
                nc.scalar.copy(pre_o[:, i].rearrange("p a u -> p (a u)"), pre_ps[m % 2][:, 0:2 * U])\
                    .then_inc(pre_copied, 1)

            def copy_high(n, j, peeled):
                i = j % 2
                act.wait_ge(rows_high, n + 1)
                if not peeled:
                    act.wait_ge(folded_x, n - 1)
                nc.scalar.copy(high[:, i], rows_ps[i][1][:, 0:2 * U]).then_inc(high_copied, 1)

            def copy_second(n, j, peeled):
                i = j % 2
                act.wait_ge(cols_done, n + 1)
                if not peeled:
                    act.wait_ge(parts_done, n - 1)
                src = cols_ps[i][0:V, U:2 * U].rearrange("p (t v) -> p t v", t=2)
                nc.scalar.copy(second[:, i].rearrange("p (t v) -> p t v", t=2), src[:, ::-1])\
                    .then_inc(second_copied, 1)

            def square(n, j, peeled):
                i = j % 2
                act.wait_ge(parts_done, n + 1)
                if not peeled:
                    act.wait_ge(added, n - 1)
                nc.scalar.activation(squares[:, i].rearrange("p w u -> p (w u)"),
                                     parts[:, i].rearrange("p w u -> p (w u)"), ACT.Square)\
                    .then_inc(squared, 1)

            def root(n, j, at):
                dst = mags[:, :, bass.ds(at, 1)] if not isinstance(at, int) else mags[:, :, at:at + 1]
                nc.scalar.activation(dst.rearrange("p r a -> p (r a)"), power2[:, j % 2], ACT.Sqrt)\
                    .then_inc(rooted, 1)

            def steps(base, peeled, entry=None, at=None):
                for j in range(XB):
                    if not (peeled and j < 2):
                        act.wait_ge(added, base + j - 1)
                    copy_high(base + j, j, peeled and j < 2)
                    if not (peeled and j < 2):
                        if entry is not None and j == 2 and entry >= 2:
                            act.wait_ge(stage_out[entry % 2], 16 * (entry // 2))
                        root(base + j - 2, j - 2, at(j - 2))
                    if not (peeled and j == 0):
                        copy_second(base + j - 1, j - 1, peeled and j - 1 < 2)
                        square(base + j - 1, j - 1, peeled and j - 1 < 2)

            for s in range(STAGES):
                first = s * STAGE
                place = lambda j, f=first: (f + j) % (2 * STAGE)
                steps(first, s == 0, s, place)
                with act.Fori(1, STEPS) as k:
                    off = k * XB + (s % 2) * STAGE
                    steps(k * XB + first, False, None, lambda j, o=off: o + j)
            n = IMAGES
            act.wait_ge(added, n - 1)
            root(n - 2, 0, (n - 2) % (2 * STAGE))
            copy_second(n - 1, 1, False)
            square(n - 1, 1, False)
            act.wait_ge(added, n)
            root(n - 1, 1, (n - 1) % (2 * STAGE))

        @block.gpsimd
        def _(pool):
            def add(n, j, peeled):
                i = j % 2
                pool.wait_ge(squared, n + 1)
                if not peeled:
                    pool.wait_ge(rooted, n - 1)
                ins = nc.gpsimd.tensor_tensor(power2[:, i].rearrange("p (w v) -> p w v", w=2),
                                              squares[:, i, :, 0:V], squares[:, i, ::-1, V:U], ALU.add)
                ins.then_inc(added, 1)

            for j in range(XB):
                add(j, j, j < 2)
            with pool.Fori(XB, IMAGES, XB) as base:
                for j in range(XB):
                    add(base + j, j, False)


def token_phase(nc, d, scratch, tokens):
    GB = 3
    NH = BINS // 2
    assert JC % GB == 0 and NH * B == 512
    with ExitStack() as ctx:
        sb = lambda n, s, t=F32: ctx.enter_context(nc.sbuf_tensor(n, s, t))
        sem = lambda n: ctx.enter_context(nc.semaphore(n))
        gathered = sb("gathered", [P, GB, BINS, IMAGES])
        weight = sb("weight", [P, JC, C, E])
        rows = sb("rows", [P, JC * BINS], I32)
        rows_now = sb("rows_now", [P, GB, BINS], I32)
        code = sb("code", [EH, 2, S])
        bias = sb("bias", [EH, 2])
        cls = sb("cls", [EH, 2])
        shift = sb("shift", [EH, 2, S])
        acc = [[ctx.enter_context(nc.psum_tensor(f"token{h}{b}", [P, 512], F32)) for b in range(2)]
               for h in range(2)]
        weight_in, rows_in, small_in = sem("weight_in"), sem("rows_in"), sem("small_in")
        rows_copied, chunks_begun = sem("rows_copied"), sem("chunks_begun")
        chunk_in = [sem(f"chunk_in{i}") for i in range(GB)]
        chunk_used = sem("chunk_used")
        shift_done = sem("shift_done")
        tokens_done = sem("tokens_done")
        block = ctx.enter_context(nc.Block())

        @block.sync
        def _(sp):
            sp.dma_start(rows[:], d["rows"]).then_inc(rows_in, 16)
            sp.dma_start(weight[:], d["tok_w"]).then_inc(weight_in, 16)
            for dst, src in ((code, "code"), (bias, "tok_b"), (cls, "cls")):
                sp.dma_start(dst[:], d[src]).then_inc(small_in, 16)

        @block.gpsimd
        def _(pool):
            def chunk(jc, i, peeled):
                if not peeled:
                    pool.wait_ge(chunk_used, jc - (GB - 1))
                src = rows[:, i * BINS:(i + 1) * BINS] if peeled else rows[:, bass.ds(jc * BINS, BINS)]
                nc.gpsimd.tensor_copy(rows_now[:, i], src).then_inc(rows_copied, 1)
                pool.wait_ge(rows_copied, jc + 1)
                pool.sem_inc(chunks_begun, 1)
                for n in range(BINS):
                    nc.gpsimd.indirect_dma_start(
                        gathered[:, i, n], None, scratch["power"],
                        bass.IndirectOffsetOnAxis(ap=rows_now[:, i, n:n + 1], axis=0))\
                        .then_inc(chunk_in[i], 16)

            pool.wait_ge(rows_in, 16)
            for i in range(GB):
                chunk(i, i, True)
            with pool.Fori(1, JC // GB) as k:
                for i in range(GB):
                    chunk(k * GB + i, i, False)

        @block.tensor
        def _(pe):
            pe.wait_ge(weight_in, 16)
            for jc in range(JC):
                i = jc % GB
                pe.wait_ge(chunk_in[i], 16 * BINS * (jc // GB + 1))
                for c in range(C):
                    for h in range(2):
                        for b in range(2):
                            mm = nc.tensor.matmul(
                                acc[h][b][0:EH, :], weight[:, jc, c, h * EH:(h + 1) * EH],
                                gathered[:, i, b * NH:(b + 1) * NH, c * B:(c + 1) * B],
                                start=jc == 0 and c == 0, stop=jc == JC - 1 and c == C - 1)
                mm.then_inc(chunk_used, 1)

        @block.vector
        def _(dve):
            dve.wait_ge(small_in, 48)
            for h in range(2):
                nc.vector.tensor_scalar(shift[:, h, 1:S], code[:, h, 1:S], bias[:, h:h + 1], None, ALU.add)
                nc.vector.tensor_scalar(shift[:, h, 0:1], code[:, h, 0:1], cls[:, h:h + 1], None, ALU.add)\
                    .then_inc(shift_done, 1)
            dve.wait_ge(shift_done, 2)
            nc.vector.tensor_copy(tokens[:, :, 0, :], shift[:, :, 0:1].to_broadcast([EH, 2, B]))
            dve.wait_ge(chunk_used, JC)
            for h in range(2):
                for b in range(2):
                    s = slice(1 + b * NH, 1 + (b + 1) * NH)
                    nc.vector.tensor_tensor(
                        tokens[:, h, s, :], acc[h][b][0:EH, :].rearrange("p (n b) -> p n b", b=B),
                        shift[:, h, s].rearrange("p (n o) -> p n o", o=1).to_broadcast([EH, NH, B]), ALU.add)\
                        .then_inc(tokens_done, 1)
            dve.wait_ge(tokens_done, 4)


CHUNKS = [(0, 6), (6, 12), (12, S)]
GB = 16
GROUPS = 2 * (B // GB)
HS = HH * S


def head_masks():
    f, r = np.arange(EH) // HD, np.arange(HS) // S
    of_head = (f[:, None] == np.arange(HH)).astype(np.float32)
    feat_feat = (f[:, None] == f).astype(np.float32)
    row_row = (r[:, None] == r).astype(np.float32)
    row_feat = (r[:, None] == f).astype(np.float32)
    minus_same = -(np.arange(HS)[:, None] % S == np.arange(S)).astype(np.float32)
    return of_head, feat_feat, row_row, row_feat, minus_same


def attention_phase(nc, d, tokens, h1):
    with ExitStack() as ctx:
        sb = lambda n, s: ctx.enter_context(nc.sbuf_tensor(n, s, F32))
        sem = lambda n: ctx.enter_context(nc.semaphore(n))
        down = sb("down", [EH, 3, 2, RANK])
        up = sb("up", [RANK, 3, E])
        bias = sb("bias3", [EH, 3, 2])
        m_u = sb("m_u", [RM, EH])
        m_v = sb("m_v", [RM, EH])
        of_head = sb("of_head", [EH, HH])
        feat_feat = sb("feat_feat", [EH, EH])
        row_row = sb("row_row", [HS, HS])
        row_feat = sb("row_feat", [HS, EH])
        minus_same = sb("minus_same", [HS, S])
        mixer = sb("mixer", [EH, EH])
        bias_heads = sb("bias_heads", [EH, 2, HH])
        low = sb("low_rank", [RANK, 2, S, B])
        q = sb("q", [EH, 2, S, B])
        qm = q
        qm_heads = sb("qm_heads", [EH, 2, B, HH, S])
        low_v = qm_heads[:, 0]
        k = sb("k", [EH, 2, S, B])
        k_heads = sb("k_heads", [EH, 2, B, HH, S])
        v_heads = sb("v_heads", [HS, B, 2, EH])
        top = sb("top", [HS, GROUPS, GB])
        shift = sb("score_shift", [HS, 2, GB, S])
        expd = sb("expd", [HS, 2, GB, S])
        rden = sb("rden", [EH, 2, GB, S])
        att = rden
        ones = sb("ones", [EH, EH])
        spare = low[:].rearrange("p x s b -> p (x s b)")
        sq = spare[:, 0:1024].rearrange("p (h n) -> p h n", h=2)
        var = spare[:, 1024:2048].rearrange("p (h n) -> p h n", h=2)
        bank = [ctx.enter_context(nc.psum_tensor(f"bank{i}", [P, 512], F32)) for i in range(8)]
        (weights_in, mixer_mm, mixer_done, low_mm, low_copied, q_mm, q_copied, k_mm, k_copied, qm_mm,
         qm_copied, v_mm, v_copied, score_mm, top_done, shifted, turned_mm, exp_done, out_mm, rden_done,
         att_done, out_read, bias_done, mean_mm, centred, sq_done, var_mm, var_eps, std_done, rstd_done,
         normed, ones_done) = [sem(n) for n in (
             "weights_in mixer_mm mixer_done low_mm low_copied q_mm q_copied k_mm k_copied qm_mm "
             "qm_copied v_mm v_copied score_mm top_done shifted turned_mm exp_done out_mm rden_done "
             "att_done out_read bias_done mean_mm centred sq_done var_mm var_eps std_done rstd_done "
             "normed ones_done").split()]
        loads = [(down, "down"), (up, "up"), (bias, "bias"), (m_u, "m_u"), (m_v, "m_v"),
                 (of_head, "of_head"), (feat_feat, "feat_feat"), (row_row, "row_row"),
                 (row_feat, "row_feat"), (minus_same, "minus_same")]
        tiles = [(h, c) for h in range(2) for c in range(len(CHUNKS))]
        cols = lambda c: (CHUNKS[c][1] - CHUNKS[c][0]) * B
        at = lambda c: slice(*CHUNKS[c])
        flat = lambda a: a.rearrange("p s b -> p (s b)")
        wide = lambda a: a.rearrange("p (s b) -> p s b", b=B)
        GC = GB * S
        group = lambda g: (g // (B // GB), slice(g % (B // GB) * GB, (g % (B // GB) + 1) * GB))
        block = ctx.enter_context(nc.Block())

        @block.sync
        def _(sp):
            for dst, src in loads:
                sp.dma_start(dst[:], d[src]).then_inc(weights_in, 16)

        @block.tensor
        def _(pe):
            pe.wait_ge(weights_in, 16 * len(loads))
            nc.tensor.matmul(bank[6][0:EH, 0:EH], m_u[:], m_v[:], start=True, stop=True).then_inc(mixer_mm, 1)
            for n in range(3 * len(CHUNKS)):
                x, c = divmod(n, len(CHUNKS))
                if n >= 2:
                    pe.wait_ge(low_copied, n - 1)
                for h in range(2):
                    mm = nc.tensor.matmul(bank[n % 2][0:RANK, 0:cols(c)], down[:, x, h], flat(tokens[:, h, at(c)]),
                                          start=h == 0, stop=h == 1)
                mm.then_inc(low_mm, 1)

            def up_tile(x, n, mm_sem, copied, first):
                h, c = tiles[n]
                if n >= 2:
                    pe.wait_ge(copied, n - 1)
                nc.tensor.matmul(bank[first + n % 2][0:EH, 0:cols(c)], up[:, x, h * EH:(h + 1) * EH],
                                 flat(low[:, x, at(c)]), start=True, stop=True).then_inc(mm_sem, 1)

            pe.wait_ge(low_copied, 3 * len(CHUNKS))
            for b in range(B):
                n = b // 2
                if b % 2 == 0 and n >= 2:
                    pe.wait_ge(v_copied, n - 1)
                mm = nc.tensor.matmul(bank[n % 2][0:HS, b % 2 * E:(b % 2 + 1) * E],
                                      low_v[:, b].rearrange("p h s -> p (h s)"), up[:, 2],
                                      start=True, stop=True)
                if b % 2:
                    mm.then_inc(v_mm, 1)
                if b % 10 == 0 and b // 10 < len(tiles):
                    up_tile(1, b // 10, k_mm, k_copied, 4)
            for n in range(len(tiles)):
                up_tile(0, n, q_mm, q_copied, 2)
            pe.wait_ge(mixer_done, 1)
            for n, (h, c) in enumerate(tiles):
                pe.wait_ge(q_copied, n + 1)
                if n >= 2:
                    pe.wait_ge(qm_copied, n - 1)
                nc.tensor.matmul(bank[6 + n % 2][0:EH, 0:cols(c)], mixer[:], flat(q[:, h, at(c)]),
                                 start=True, stop=True).then_inc(qm_mm, 1)

            def scores(g):
                h, bs = group(g)
                if g == 0:
                    pe.wait_ge(qm_copied, len(tiles))
                    pe.wait_ge(k_copied, len(tiles))
                if g >= 2:
                    pe.wait_ge(top_done, g - 1)
                for i, b in enumerate(range(bs.start, bs.stop)):
                    mm = nc.tensor.matmul(bank[2 + g % 2][0:HS, i * S:(i + 1) * S],
                                          qm_heads[:, h, b].rearrange("p h s -> p (h s)"), k[:, h, :, b],
                                          start=True, stop=True)
                mm.then_inc(score_mm, 1)

            def turned(g):
                h, bs = group(g)
                pe.wait_ge(shifted, g + 1)
                if g >= 2:
                    pe.wait_ge(exp_done, g - 1)
                o = bank[4 + g % 2][0:HS, 0:GC]
                nc.tensor.matmul(o, row_row[:], flat(shift[:, g % 2]), start=True, stop=False,
                                 skip_group_check=True)
                for i, b in enumerate(range(bs.start, bs.stop)):
                    mm = nc.tensor.matmul(o[:, i * S:(i + 1) * S],
                                          k_heads[:, h, b].rearrange("p h s -> p (h s)"), qm[:, h, :, b],
                                          start=False, stop=i == GB - 1, skip_group_check=True)
                mm.then_inc(turned_mm, 1)

            def weighted(g):
                h, bs = group(g)
                if g == 0:
                    pe.wait_ge(v_copied, B // 2)
                pe.wait_ge(exp_done, g + 1)
                if g >= 2:
                    pe.wait_ge(out_read, g - 1)
                nc.tensor.matmul(bank[g % 2][0:EH, 0:GC], row_feat[:], flat(expd[:, g % 2]), start=True, stop=True)
                for i, b in enumerate(range(bs.start, bs.stop)):
                    mm = nc.tensor.matmul(bank[6 + g % 2][0:EH, i * S:(i + 1) * S], v_heads[:, b, h],
                                          expd[:, g % 2, i], start=True, stop=True)
                mm.then_inc(out_mm, 1)

            scores(0)
            for g in range(GROUPS):
                if g + 1 < GROUPS:
                    scores(g + 1)
                turned(g)
                if g:
                    weighted(g - 1)
            weighted(GROUPS - 1)
            pe.wait_ge(att_done, GROUPS)
            pe.wait_ge(ones_done, 2)
            for c in range(len(CHUNKS)):
                for h in range(2):
                    mm = nc.tensor.matmul(bank[c][0:EH, 0:cols(c)], ones[:], flat(tokens[:, h, at(c)]),
                                          start=h == 0, stop=h == 1)
                mm.then_inc(mean_mm, 1)
            for c in range(len(CHUNKS)):
                pe.wait_ge(sq_done, c + 1)
                for h in range(2):
                    mm = nc.tensor.matmul(bank[3 + c][0:EH, 0:cols(c)], ones[:], sq[:, h, 0:cols(c)],
                                          start=h == 0, stop=h == 1)
                mm.then_inc(var_mm, 1)

        @block.scalar
        def _(act):
            for n in range(3 * len(CHUNKS)):
                x, c = divmod(n, len(CHUNKS))
                act.wait_ge(low_mm, n + 1)
                src = wide(bank[n % 2][0:RANK, 0:cols(c)])
                if x < 2:
                    nc.scalar.copy(low[:, x, at(c)], src).then_inc(low_copied, 1)
                else:
                    for h in range(HH):
                        ins = nc.scalar.copy(low_v[:, :, h, at(c)].rearrange("p b s -> p s b"), src)
                    ins.then_inc(low_copied, 1)
            act.wait_ge(bias_done, 1)
            for n, (h, c) in enumerate(tiles):
                act.wait_ge(k_mm, n + 1)
                src = wide(bank[4 + n % 2][0:EH, 0:cols(c)])
                nc.scalar.activation(k[:, h, at(c)], src, ACT.Identity, bias=bias[:, 1, h:h + 1])
                for m in range(HH):
                    ins = nc.scalar.activation(k_heads[:, h, :, m, at(c)].rearrange("p b s -> p s b"), src,
                                               ACT.Identity, scale=of_head[:, m:m + 1],
                                               bias=bias_heads[:, h, m:m + 1])
                ins.then_inc(k_copied, 1)
            for g in range(GROUPS):
                act.wait_ge(turned_mm, g + 1)
                if g >= 2:
                    act.wait_ge(out_mm, g - 1)
                nc.scalar.activation(flat(expd[:, g % 2]), bank[4 + g % 2][0:HS, 0:GC], ACT.Exp)\
                    .then_inc(exp_done, 1)
            for c in range(len(CHUNKS)):
                act.wait_ge(centred, c + 1)
                if c:
                    act.wait_ge(var_mm, c)
                for h in range(2):
                    ins = nc.scalar.activation(sq[:, h, 0:cols(c)], flat(h1[:, h, at(c)]), ACT.Square)
                ins.then_inc(sq_done, 1)
            for c in range(len(CHUNKS)):
                act.wait_ge(var_eps, c + 1)
                nc.scalar.activation(var[:, c % 2, 0:cols(c)], var[:, c % 2, 0:cols(c)], ACT.Sqrt)\
                    .then_inc(std_done, 1)

        @block.vector
        def _(dve):
            nc.vector.memset(ones[:], 1.0 / E).then_inc(ones_done, 1)
            nc.vector.memset(h1[:, :, S], 0.0).then_inc(ones_done, 1)
            dve.wait_ge(weights_in, 16 * len(loads))
            for h in range(2):
                ins = nc.vector.tensor_scalar(bias_heads[:, h], of_head[:], bias[:, 1, h:h + 1], None, ALU.mult)
            ins.then_inc(bias_done, 1)
            dve.wait_ge(mixer_mm, 1)
            nc.vector.scalar_tensor_tensor(out=mixer[:], in0=bank[6][0:EH, 0:EH], scalar=float(HD) ** -0.5,
                                           in1=feat_feat[:], op0=ALU.mult, op1=ALU.mult).then_inc(mixer_done, 1)
            for n in range(B // 2):
                dve.wait_ge(v_mm, n + 1)
                mask = row_feat[:].rearrange("p (o f) -> p o f", o=1).to_broadcast([HS, 4, EH])
                nc.vector.tensor_tensor(v_heads[:, 2 * n:2 * n + 2].rearrange("p b h f -> p (b h) f"),
                                        bank[n % 2][0:HS, 0:2 * E].rearrange("p (a f) -> p a f", a=4),
                                        mask, ALU.mult).then_inc(v_copied, 1)
            for n, (h, c) in enumerate(tiles):
                dve.wait_ge(q_mm, n + 1)
                nc.vector.tensor_scalar(q[:, h, at(c)], wide(bank[2 + n % 2][0:EH, 0:cols(c)]),
                                        bias[:, 0, h:h + 1], None, ALU.add).then_inc(q_copied, 1)
            for n, (h, c) in enumerate(tiles):
                dve.wait_ge(qm_mm, n + 1)
                src = wide(bank[6 + n % 2][0:EH, 0:cols(c)])
                nc.vector.tensor_copy(qm[:, h, at(c)], src)
                for m in range(HH):
                    ins = nc.vector.tensor_scalar(qm_heads[:, h, :, m, at(c)].rearrange("p b s -> p s b"), src,
                                                  of_head[:, m:m + 1], None, ALU.mult)
                ins.then_inc(qm_copied, 1)
            def shift_of(g):
                dve.wait_ge(score_mm, g + 1)
                nc.vector.tensor_reduce(top[:, g], bank[2 + g % 2][0:HS, 0:GC].rearrange("p (b s) -> p b s", s=S),
                                        AXX, ALU.max).then_inc(top_done, 1)
                dve.wait_ge(top_done, g + 1)
                if g >= 2:
                    dve.wait_ge(turned_mm, g - 1)
                nc.vector.tensor_tensor(shift[:, g % 2],
                                        top[:, g].rearrange("p (b o) -> p b o", o=1).to_broadcast([HS, GB, S]),
                                        minus_same[:].rearrange("p (o s) -> p o s", o=1).to_broadcast([HS, GB, S]),
                                        ALU.mult).then_inc(shifted, 1)

            def residual(g):
                h, bs = group(g)
                dve.wait_ge(out_mm, g + 1)
                nc.vector.reciprocal(flat(rden[:, g % 2]), bank[g % 2][0:EH, 0:GC]).then_inc(rden_done, 1)
                dve.wait_ge(rden_done, g + 1)
                nc.vector.tensor_tensor(flat(att[:, g % 2]), bank[6 + g % 2][0:EH, 0:GC], flat(rden[:, g % 2]),
                                        ALU.mult).then_inc(out_read, 1)
                dve.wait_ge(out_read, g + 1)
                t = tokens[:, h, :, bs].rearrange("p s b -> p b s")
                nc.vector.scalar_tensor_tensor(out=t, in0=att[:, g % 2], scalar=bias[:, 2, h:h + 1], in1=t,
                                               op0=ALU.add, op1=ALU.add).then_inc(att_done, 1)

            shift_of(0)
            for g in range(GROUPS):
                if g + 1 < GROUPS:
                    shift_of(g + 1)
                if g:
                    residual(g - 1)
            residual(GROUPS - 1)
            dve.wait_ge(att_done, GROUPS)
            for c in range(len(CHUNKS)):
                dve.wait_ge(mean_mm, c + 1)
                for h in range(2):
                    ins = nc.vector.tensor_tensor(flat(h1[:, h, at(c)]), flat(tokens[:, h, at(c)]),
                                                  bank[c][0:EH, 0:cols(c)], ALU.subtract)
                ins.then_inc(centred, 1)
            for c in range(len(CHUNKS)):
                w = var[:, c % 2, 0:cols(c)]
                dve.wait_ge(var_mm, c + 1)
                if c >= 2:
                    dve.wait_ge(normed, c - 1)
                nc.vector.tensor_scalar(w, bank[3 + c][0:EH, 0:cols(c)], EPS, None, ALU.add).then_inc(var_eps, 1)
                dve.wait_ge(std_done, c + 1)
                nc.vector.reciprocal(w, w).then_inc(rstd_done, 1)
                dve.wait_ge(rstd_done, c + 1)
                for h in range(2):
                    x = flat(h1[:, h, at(c)])
                    ins = nc.vector.tensor_tensor(x, x, w, ALU.mult)
                ins.then_inc(normed, 1)


def expert_phase(nc, d, h1, out):
    tile_rows = [min(P, T - t * P) for t in range(TILES)]
    with ExitStack() as ctx:
        sb = lambda n, s: ctx.enter_context(nc.sbuf_tensor(n, s, F32))
        sem = lambda n: ctx.enter_context(nc.semaphore(n))
        w_router = sb("w_router", [EH, 2, EXPERTS])
        b_router = sb("b_router", [1, EXPERTS])
        one_row = sb("one_row", [1, P])
        ident = sb("ident", [P, P])
        counts = sb("counts", [P, TILES, EXPERTS])
        b_fc = sb("b_fc", [P, 2, FC])
        b_proj = sb("b_proj", [EXPERTS, E])
        w_fc = sb("w_fc", [EH, 2, 2, FF])
        w_proj = sb("w_proj", [P, 2, FC, E])
        act_out = sb("act_out", [P, 2, FC, T])
        acc = sb("acc", [P, TILES, E])
        gate = sb("gate", [P, TILES, EXPERTS])
        gate_t = sb("gate_t", [EXPERTS, TILES, P])
        RT = [P, TILES, EXPERTS]
        (probs, far, first, second, rest, picked) = [sb(n, RT) for n in
                                                     "probs far best_one next_one rest picked".split()]
        stat = sb("stat", [P, 8, TILES])
        square = sb("square", [P, TILES, E])
        bank = [ctx.enter_context(nc.psum_tensor(f"ebank{i}", [P, 512], F32)) for i in range(8)]
        (small_in, logits_mm, exp_in, exp_done, routed, turn_mm, turned, base_mm, base_copied, fc_mm,
         fc_act, proj_mm, proj_added, chain, std_in, std_done, out_ready, out_left, ones_set) = [
             sem("e_" + n) for n in (
                 "small_in logits_mm exp_in exp_done routed turn_mm turned base_mm base_copied fc_mm "
                 "fc_act proj_mm proj_added chain std_in std_done out_ready out_left ones_set").split()]
        w_in = [sem(f"e_w_in{i}") for i in range(2)]
        small = [(w_router, "w_router"), (b_router, "b_router"), (ident, "ident"), (counts, "counts"),
                 (b_proj, "b_proj")]
        block = ctx.enter_context(nc.Block())
        NC = len(CHUNKS)
        cols = [slice(a * B, b * B) for a, b in CHUNKS]
        hid = h1[:].rearrange("p h s b -> p h (s b)")
        act_flat = act_out[:]

        @block.sync
        def _(sp):
            for dst, src in small:
                sp.dma_start(dst[:], d[src]).then_inc(small_in, 16)

            def load(e, i):
                one = bass.ds(e, 1) if not isinstance(e, int) else slice(e, e + 1)
                sp.dma_start(w_fc[:, i], d["w_fc"][one].rearrange("a p h f -> (a p) h f")).then_inc(w_in[i], 16)
                sp.dma_start(b_fc[:, i], d["b_fc"][one].rearrange("a p f -> (a p) f")).then_inc(w_in[i], 16)
                sp.dma_start(w_proj[:, i], d["w_proj"][one].rearrange("a p c f -> (a p) c f"))\
                    .then_inc(w_in[i], 16)

            for i in range(2):
                load(i, i)
            with sp.Fori(1, EXPERTS // 2) as k:
                for i in range(2):
                    e = sp.snap(2 * k + i)
                    used = sp.snap(TILES * (2 * k + i - 1))
                    sp.wait_ge(proj_mm, used)
                    load(e, i)
            sp.wait_ge(out_ready, 1)
            for s in range(S):
                sp.dma_start(out[:, s, :], acc[s % 2 * B:(s % 2 + 1) * B, s // 2, :]).then_inc(out_left, 16)
            sp.wait_ge(out_left, 16 * S)

        @block.tensor
        def _(pe):
            pe.wait_ge(small_in, 16 * len(small))
            pe.wait_ge(ones_set, 1)
            for t in range(TILES):
                o = bank[0][:, t * EXPERTS:(t + 1) * EXPERTS]
                for h in range(2):
                    nc.tensor.matmul(o, hid[:, h, t * P:(t + 1) * P], w_router[:, h], start=h == 0, stop=False)
                mm = nc.tensor.matmul(o, one_row[:], b_router[:], start=False, stop=True)
            mm.then_inc(logits_mm, 1)

            def gate_turn():
                pe.wait_ge(routed, 1)
                for t in range(TILES):
                    if t >= 1:
                        pe.wait_ge(turned, t)
                    nc.tensor.transpose(bank[0][0:EXPERTS, 0:P], gate[:, t], ident[:]).then_inc(turn_mm, 1)

            def base(t):
                if t >= 1:
                    pe.wait_ge(base_copied, t)
                o = bank[1][:, 0:E]
                nc.tensor.matmul(o, gate_t[:, t], b_proj[:], start=True, stop=False, skip_group_check=True)
                for h in range(2):
                    mm = nc.tensor.matmul(o[:, h * EH:(h + 1) * EH], hid[:, h, t * P:(t + 1) * P],
                                          ident[0:EH, 0:EH], start=False, stop=h == 1, skip_group_check=True)
                mm.then_inc(base_mm, 1)

            def up(e, i, used):
                pe.wait_ge(w_in[i], 24 * (e - i) + 48)
                for n in range(FC * NC):
                    f, c = divmod(n, NC)
                    if used is None and n >= 3:
                        pe.wait_ge(fc_act, n - 2)
                    if used is not None:
                        pe.wait_ge(fc_act, used + n - 2)
                    o = bank[2 + n % 3][:, 0:cols[c].stop - cols[c].start]
                    for h in range(2):
                        mm = nc.tensor.matmul(o, w_fc[:, i, h, f * P:(f + 1) * P], hid[:, h, cols[c]],
                                              start=h == 0, stop=h == 1)
                    mm.then_inc(fc_mm, 1)

            def down(e, i, peeled):
                pe.wait_ge(fc_act, (e + 1) * FC * NC)
                for t in range(TILES):
                    if not (peeled and t < 3):
                        pe.wait_ge(proj_added, e * TILES + t - 2)
                    for f in range(FC):
                        mm = nc.tensor.matmul(bank[5 + t % 3][0:tile_rows[t], 0:E],
                                              act_flat[:, i, f, t * P:t * P + tile_rows[t]],
                                              w_proj[:, i, f], start=f == 0, stop=f == FC - 1)
                    mm.then_inc(proj_mm, 1)

            up(0, 0, None)
            gate_turn()
            pe.wait_ge(turned, TILES)
            for t in range(TILES):
                base(t)
            up(1, 1, FC * NC)
            down(0, 0, True)
            with pe.Fori(1, EXPERTS // 2) as k:
                up(2 * k, 0, FC * NC * 2 * k)
                down(2 * k - 1, 1, False)
                up(2 * k + 1, 1, FC * NC * (2 * k + 1))
                down(2 * k, 0, False)
            down(EXPERTS - 1, 1, False)

        @block.scalar
        def _(act):
            act.wait_ge(exp_in, 1)
            nc.scalar.activation(probs[:], probs[:], ACT.Exp).then_inc(exp_done, 1)

            def gelu(e, i, peeled):
                for n in range(FC * NC):
                    f, c = divmod(n, NC)
                    act.wait_ge(fc_mm, e * FC * NC + n + 1)
                    if n == 0 and not peeled:
                        act.wait_ge(proj_mm, TILES * (e - 1))
                    width = cols[c].stop - cols[c].start
                    nc.scalar.activation(act_out[:, i, f, cols[c]], bank[2 + n % 3][:, 0:width],
                                         ACT.Gelu_apprx_tanh, bias=b_fc[:, i, f:f + 1]).then_inc(fc_act, 1)

            for i in range(2):
                gelu(i, i, True)
            with act.Fori(1, EXPERTS // 2) as k:
                for i in range(2):
                    gelu(2 * k + i, i, False)
            act.wait_ge(std_in, 1)
            nc.scalar.activation(stat[:, 5], stat[:, 4], ACT.Sqrt).then_inc(std_done, 1)

        @block.vector
        def _(dve):
            step = [0]

            def then(ins):
                step[0] += 1
                ins.then_inc(chain, 1)
                dve.wait_ge(chain, step[0])

            spread = lambda a, w=EXPERTS: a.rearrange("p (t o) -> p t o", o=1).to_broadcast([P, TILES, w])
            nc.vector.memset(one_row[:], 1.0).then_inc(ones_set, 1)
            dve.wait_ge(small_in, 16 * len(small))
            dve.wait_ge(logits_mm, 1)
            logits = bank[0][:, 0:TILES * EXPERTS].rearrange("p (t e) -> p t e", e=EXPERTS)
            then(nc.vector.tensor_reduce(stat[:, 0], logits, AXX, ALU.max))
            nc.vector.tensor_tensor(probs[:], logits, spread(stat[:, 0]), ALU.subtract).then_inc(exp_in, 1)
            dve.wait_ge(exp_done, 1)
            then(nc.vector.tensor_reduce(stat[:, 1], probs[:], AXX, ALU.add))
            then(nc.vector.reciprocal(stat[:, 1], stat[:, 1]))
            then(nc.vector.tensor_tensor(probs[:], probs[:], spread(stat[:, 1]), ALU.mult))

            def best(src, onehot, value):
                then(nc.vector.tensor_reduce(value, src, AXX, ALU.max))
                then(nc.vector.tensor_tensor(far[:], src, spread(value), ALU.is_lt))
                then(nc.vector.scalar_tensor_tensor(out=far[:], in0=far[:], scalar=float(EXPERTS), in1=counts[:],
                                                    op0=ALU.mult, op1=ALU.add))
                then(nc.vector.tensor_reduce(stat[:, 6], far[:], AXX, ALU.min))
                then(nc.vector.tensor_tensor(onehot[:], counts[:], spread(stat[:, 6]), ALU.is_equal))

            best(probs[:], first, stat[:, 2])
            then(nc.vector.scalar_tensor_tensor(out=rest[:], in0=first[:], scalar=-2.0, in1=probs[:],
                                                op0=ALU.mult, op1=ALU.add))
            best(rest[:], second, stat[:, 3])
            then(nc.vector.tensor_tensor(picked[:], first[:], second[:], ALU.add))
            then(nc.vector.tensor_tensor(picked[:], picked[:], probs[:], ALU.mult))
            then(nc.vector.tensor_tensor(stat[:, 7], stat[:, 2], stat[:, 3], ALU.add))
            then(nc.vector.reciprocal(stat[:, 7], stat[:, 7]))
            nc.vector.tensor_tensor(gate[:], picked[:], spread(stat[:, 7]), ALU.mult).then_inc(routed, 1)
            for t in range(TILES):
                dve.wait_ge(turn_mm, t + 1)
                nc.vector.tensor_copy(gate_t[:, t], bank[0][0:EXPERTS, 0:P]).then_inc(turned, 1)
            for t in range(TILES):
                dve.wait_ge(base_mm, t + 1)
                nc.vector.tensor_copy(acc[:, t], bank[1][:, 0:E]).then_inc(base_copied, 1)
            dve.wait_ge(routed, 1)
            dve.wait_ge(base_copied, TILES)

            def add(e, first_expert):
                for t in range(TILES):
                    r = tile_rows[t]
                    dve.wait_ge(proj_mm, e * TILES + t + 1)
                    if not first_expert:
                        dve.wait_ge(proj_added, (e - 1) * TILES + t + 1)
                    g = gate[0:r, t, e:e + 1] if isinstance(e, int) else gate[0:r, t, bass.ds(e, 1)]
                    nc.vector.scalar_tensor_tensor(out=acc[0:r, t], in0=bank[5 + t % 3][0:r, 0:E], scalar=g,
                                                   in1=acc[0:r, t], op0=ALU.mult, op1=ALU.add)\
                        .then_inc(proj_added, 1)

            add(0, True)
            with dve.Fori(1, EXPERTS) as e:
                add(e, False)
            dve.wait_ge(proj_added, EXPERTS * TILES)
            then(nc.vector.tensor_reduce(stat[:, 0], acc[:], AXX, ALU.add))
            then(nc.vector.tensor_scalar(stat[:, 0], stat[:, 0], 1.0 / E, None, ALU.mult))
            then(nc.vector.tensor_tensor(acc[:], acc[:], spread(stat[:, 0], E), ALU.subtract))
            then(nc.vector.tensor_tensor(square[:], acc[:], acc[:], ALU.mult))
            then(nc.vector.tensor_reduce(stat[:, 1], square[:], AXX, ALU.add))
            nc.vector.tensor_scalar(stat[:, 4], stat[:, 1], 1.0 / E, EPS, ALU.mult, ALU.add).then_inc(std_in, 1)
            dve.wait_ge(std_done, 1)
            then(nc.vector.reciprocal(stat[:, 5], stat[:, 5]))
            nc.vector.tensor_tensor(acc[:], acc[:], spread(stat[:, 5], E), ALU.mult).then_inc(out_ready, 1)


def vit_tower(nc, d, out):
    scratch = {
        "power": nc.dram_tensor("power", [ROWS, IMAGES], F32).ap(),
        "left_cols": nc.dram_tensor("left_cols", [IMAGES, NL, U], F32).ap(),
        "left_rows": nc.dram_tensor("left_rows", [IMAGES, NL, U], F32).ap(),
    }
    with ExitStack() as ctx:
        dft_phase(nc, d, scratch)
        tokens = ctx.enter_context(nc.sbuf_tensor("tokens", [EH, 2, S, B], F32))
        h1 = ctx.enter_context(nc.sbuf_tensor("h1", [EH, 2, S + 1, B], F32))
        token_phase(nc, d, scratch, tokens)
        attention_phase(nc, d, tokens, h1)
        expert_phase(nc, d, h1, out)


def layout(x, L0_tok_cls_token, L0_tok_W, L0_tok_b, **w):
    x = np.asarray(x)
    order = [((b - B // 2) % B, (c - C // 2) % C) for c in range(C) for b in range(B)]
    flat = x.reshape(B * C, N, N)
    src = np.array([b * C + c for b, c in order])
    rows = np.concatenate(FOLDED)
    main = np.empty((IMAGES, P, 4, 4 * P), np.float32)
    cols = np.empty((IMAGES, NL, 4, P), np.float32)
    for n, k in enumerate(src):
        image = flat[k]
        picked = image[rows]
        main[n] = picked[:, rows].reshape(4, P, 4 * P).transpose(1, 0, 2)
        cols[n] = picked[:, LEFT].T.reshape(NL, 4, P)
    left = flat[src][:, LEFT]
    chunks = lambda a: np.ascontiguousarray(
        a.reshape(-1, P, 4, P).transpose(0, 3, 2, 1))
    corner = left[:, :, LEFT].reshape(-1, P, NL).transpose(0, 2, 1)
    per_half = lambda a: np.ascontiguousarray(
        np.asarray(a).reshape(2, EH, -1).transpose(1, 0, 2))
    w = {name: np.asarray(a) for name, a in w.items()}
    of_head, feat_feat, row_row, row_feat, minus_same = head_masks()
    tab = trig(np.concatenate(FOLDED)).reshape(4, P, U).transpose(1, 0, 2)
    return {
        "x": main,
        "x_cols": chunks(cols),
        "x_rows": chunks(left[:, :, rows].reshape(IMAGES, NL, 4, P)),
        "x_corner": np.ascontiguousarray(corner),
        "ktab": folded_trig(), "full": np.ascontiguousarray(tab), "left": trig(LEFT),
        "rows": radial_rows(), "code": position_code(),
        "tok_w": np.ascontiguousarray(np.asarray(L0_tok_W).reshape(E, C, JC, P).transpose(3, 2, 1, 0)),
        "tok_b": per_half(np.asarray(L0_tok_b))[:, :, 0],
        "cls": per_half(np.asarray(L0_tok_cls_token).reshape(E))[:, :, 0],
        "down": np.ascontiguousarray(np.stack([per_half(w["L0_attn_V_" + n]) for n in "QKV"], 1)),
        "up": np.ascontiguousarray(np.stack([w["L0_attn_U_" + n] for n in "QKV"], 1)),
        "bias": np.ascontiguousarray(np.stack([per_half(w["L0_attn_bias_" + n])[:, :, 0] for n in "qkv"], 1)),
        "m_u": np.ascontiguousarray(np.tile(np.asarray(w["L0_attn_M_U"]).T, (1, HH))),
        "m_v": np.ascontiguousarray(np.tile(w["L0_attn_M_V"], (1, HH))),
        "of_head": of_head, "feat_feat": feat_feat, "row_row": row_row, "row_feat": row_feat,
        "minus_same": minus_same,
        "w_router": per_half(w["L0_ffn_Wr"]),
        "b_router": np.asarray(w["L0_ffn_br"]).reshape(1, EXPERTS),
        "ident": np.eye(P, dtype=np.float32),
        "counts": np.ascontiguousarray(
            np.broadcast_to(np.arange(EXPERTS, dtype=np.float32), (P, TILES, EXPERTS))),
        "b_fc": np.ascontiguousarray(np.asarray(w["L0_ffn_bfc"]).reshape(EXPERTS, FC, P).transpose(0, 2, 1)),
        "b_proj": np.asarray(w["L0_ffn_bproj"]),
        "w_fc": np.ascontiguousarray(np.asarray(w["L0_ffn_Wfc"]).reshape(EXPERTS, 2, EH, FF).transpose(0, 2, 1, 3)),
        "w_proj": np.ascontiguousarray(
            np.asarray(w["L0_ffn_Wproj"]).reshape(EXPERTS, FC, P, E).transpose(0, 2, 1, 3)),
    }


def kernel(**inputs):
    import concourse.bacc as bacc
    from concourse.bass_utils import run_bass_kernel_spmd as run

    nc = bacc.Bacc("TRN2", target_bir_lowering=False, num_devices=1)
    arrays, aps = {}, {}
    for name, a in layout(**inputs).items():
        a = np.ascontiguousarray(a)
        arrays[f"in_{name}"] = a
        aps[name] = nc.dram_tensor(f"in_{name}", list(a.shape), mybir.dt.from_np(a.dtype),
                                   kind="ExternalInput").ap()
    out = nc.dram_tensor("tokens_out", [B, S, E], F32, kind="ExternalOutput").ap()
    vit_tower(nc, aps, out)
    return run(nc, [arrays], core_ids=[0]).results[0]["tokens_out"]
```

```python
from contextlib import ExitStack

import numpy as np

import concourse.bass as bass
from concourse import mybir

F32 = mybir.dt.float32
I32 = mybir.dt.int32
ALU = mybir.AluOpType
ACT = mybir.ActivationFunctionType
AXX = mybir.AxisListType.X

P = 128
N = 518
HALF = N // 2
KEEP = 96
NE = KEEP // 2 + 1
U = 4 * NE
V = 2 * NE
NL = 6
LEFT = [0, 129, 130, HALF, 388, 389]
FOLD = np.arange(1, P + 1)
FOLDED = [FOLD, HALF - FOLD, HALF + FOLD, N - FOLD]
B, C, E = 64, 3, 192
IMAGES = B * C
STAGE = 48
ROWS = V * 2 * V
BINS, BINSZ = 16, 2304
JC = BINSZ // P
EH = E // 2
S = BINS + 1
T = S * B
HEADS, HD, RANK, RM = 12, 16, 96, 64
HH = HEADS // 2
EXPERTS, FF = 8, 768
FC = FF // P
GT = 2 * B
TILES = (S + 1) // 2
EPS = 1e-5


def trig(pos):
    a = 2 * np.pi / N * np.asarray(pos, np.float64)[:, None]
    fe, fo = 2 * np.arange(NE), 2 * np.arange(NE) + 1
    t = np.stack([np.cos(a * fe), np.cos(a * fo), np.sin(a * fe), np.sin(a * fo)], 1)
    t[:, 1::2, NE - 1] = 0
    return t.reshape(-1, U).astype(np.float32)


def folded_trig():
    t = trig(FOLD).reshape(P, 4, NE)
    out = np.stack([t[:, 0], t[:, 2], t[:, 0], -t[:, 2], t[:, 1], t[:, 3], -t[:, 1], t[:, 3]], 1)
    return np.ascontiguousarray(out.reshape(P, 4, V))


def radial_rows():
    side = 2 * KEEP
    y, x = np.meshgrid(np.arange(side), np.arange(side), indexing="ij")
    d = np.sqrt((x - side / 2.0) ** 2 + (y - side / 2.0) ** 2).reshape(-1)
    idx = np.argsort(d, kind="stable")
    fy, fx = idx // side - KEEP, idx % side - KEEP
    v, u = np.abs(fy), np.where(fy < 0, -fx, fx)
    place = lambda f: (f % 2) * NE + f // 2
    row = (place(v) * 2 + (u < 0)) * V + place(np.abs(u))
    row = row.reshape(BINS // 2, 2, JC, P).transpose(3, 0, 2, 1)
    return np.ascontiguousarray(row.reshape(P, BINS * JC).astype(np.int32))


def position_code():
    pos = np.arange(S)[:, None].astype(np.float32)
    div = np.exp(np.arange(0, E, 2).astype(np.float32) * (-np.log(10000.0) / E))
    pe = np.zeros((S, E), np.float32)
    pe[:, 0::2], pe[:, 1::2] = np.sin(pos * div), np.cos(pos * div)
    return np.ascontiguousarray(pe.T.reshape(2, EH, S).transpose(1, 0, 2))


def dft_phase(nc, d, scratch, weight, rows, ident):
    LB = IMAGES * NL // P
    PRE = 3
    XB = 4
    assert LB % PRE == 0 and IMAGES % XB == 0 and STAGE % XB == 0
    STEPS = STAGE // XB
    STAGES = IMAGES // STAGE
    PARTS = 2 * V // NE
    with ExitStack() as ctx:
        sb = lambda n, s: ctx.enter_context(nc.sbuf_tensor(n, s, F32))
        ps = lambda n: ctx.enter_context(nc.psum_tensor(n, [P, 512], F32))
        sem = lambda n: ctx.enter_context(nc.semaphore(n))
        image = sb("image", [P, XB, 4, 512])
        fold_y = sb("fold_y", [P, 2, 4, 512])
        high = sb("high", [P, 2, 2 * U])
        fold_x = sb("fold_x", [P, 2, 4, U])
        second = sb("second", [V, 2, U])
        parts = sb("parts", [V, 2, 2, U])
        squares = sb("squares", [V, 2, 2, U])
        power2 = sb("power2", [V, 2, 2 * V])
        mags = sb("mags", [P, 2 * V, 2 * STAGE])
        ktab = sb("ktab", [P, 4, V])
        full = sb("full", [P, 4, U])
        left = sb("left", [NL, U])
        low = sb("low", [2 * NL, XB, 2, U])
        spare = mags[:].rearrange("p r i -> p (r i)")
        space = {}
        for name, size in (("c", 4 * P), ("r", 4 * P), ("k", P), ("o", 2 * U)):
            space[name], spare = spare[:, 0:PRE * size], spare[:, PRE * size:]
        pre_c = space["c"].rearrange("p (i q n) -> p i q n", i=PRE, q=4)
        pre_r = space["r"].rearrange("p (i q n) -> p i q n", i=PRE, q=4)
        pre_k = space["k"].rearrange("p (i n) -> p i n", i=PRE)[0:NL]
        pre_o = space["o"].rearrange("p (i a u) -> p i a u", i=PRE, a=2)
        rows_ps = [[ps(f"rows{i}{h}") for h in range(2)] for i in range(2)]
        cols_ps = [ps(f"cols{i}") for i in range(2)]
        pre_ps = [ps(f"pre{i}") for i in range(2)]

        tables_in = sem("tables_in")
        pre_in = [sem(f"pre_in{i}") for i in range(PRE)]
        pre_done = sem("pre_done")
        pre_copied = sem("pre_copied")
        pre_out = [sem(f"pre_out{i}") for i in range(PRE)]
        image_in = [sem(f"image_in{i}") for i in range(XB)]
        low_in = [sem(f"low_in{i}") for i in range(XB)]
        folded_y = sem("folded_y")
        rows_high = sem("rows_high")
        rows_low = sem("rows_low")
        high_copied = sem("high_copied")
        folded_x = sem("folded_x")
        cols_done = sem("cols_done")
        second_copied = sem("second_copied")
        parts_done = sem("parts_done")
        squared = sem("squared")
        added = sem("added")
        rooted = sem("rooted")
        preloaded = sem("preloaded")
        stage_out = [sem(f"stage_out{i}") for i in range(2)]
        block = ctx.enter_context(nc.Block())

        @block.sync
        def _(sp):
            for dst, src in ((ktab[:], d["ktab"]), (full[:], d["full"]), (left[:], d["left"])):
                sp.dma_start(dst, src).then_inc(tables_in, 16)
            for i in range(XB):
                sp.dma_start(low[NL:, i, 0, :], d["left"]).then_inc(tables_in, 16)
                sp.dma_start(low[0:NL, i, 1, :], d["left"]).then_inc(tables_in, 16)

            def load_pre(m, i):
                sp.dma_start(pre_c[:, i], d["x_cols"][m]).then_inc(pre_in[i], 16)
                sp.dma_start(pre_r[:, i], d["x_rows"][m]).then_inc(pre_in[i], 16)
                sp.dma_start(pre_k[:, i], d["x_corner"][m]).then_inc(pre_in[i], 16)

            def load_image(n, i):
                sp.dma_start(image[:, i], d["x"][n]).then_inc(image_in[i], 16)

            def load_low(n, i):
                rows = bass.ds(n, 1) if not isinstance(n, int) else slice(n, n + 1)
                sp.dma_start(low[0:NL, i, 0, :], scratch["left_cols"][rows].rearrange("a l u -> (a l) u"))\
                    .then_inc(low_in[i], 16)
                sp.dma_start(low[NL:, i, 1, :], scratch["left_rows"][rows].rearrange("a l u -> (a l) u"))\
                    .then_inc(low_in[i], 16)

            for i in range(PRE):
                load_pre(i, i)
            for i in range(XB):
                load_image(i, i)
            for m in range(LB):
                i = m % PRE
                sp.wait_ge(pre_copied, m + 1)
                for side, name in enumerate(("left_cols", "left_rows")):
                    sp.dma_start(scratch[name].rearrange("a l u -> (a l) u")[m * P:(m + 1) * P],
                                 pre_o[:, i, side]).then_inc(pre_out[i], 16)
                if m + PRE < LB:
                    load_pre(m + PRE, i)
            for i in range(PRE):
                sp.wait_ge(pre_out[i], 32 * (LB // PRE))
            for i in range(XB):
                load_low(i, i)

            def flush(s, k):
                part = bass.ds((k - 1) * NE, NE)
                sp.dma_start(scratch["power"].rearrange("(v r) (s i) -> s v r i", v=V, i=STAGE)[s][:, part],
                             mags[0:V, part, (s % 2) * STAGE:(s % 2 + 1) * STAGE])\
                    .then_inc(stage_out[s % 2], 16)

            for dst, src in ((rows, "rows"), (ident, "ident")):
                sp.dma_start(dst[:], d[src]).then_inc(preloaded, 16)
            piece = JC * C * E // STEPS
            for s in range(STAGES):
                def refill(k, s=s):
                    for i in range(XB):
                        n = k * XB + (s * STAGE + i + XB)
                        done = k * XB + (s * STAGE + i + 1)
                        if not isinstance(k, int):
                            n, done = sp.snap(n), sp.snap(done)
                        one = bass.ds(n, 1) if not isinstance(n, int) else slice(n, n + 1)
                        sp.wait_ge(folded_y, done)
                        sp.dma_start(image[:, i], d["x"][one].rearrange("a p r x -> (a p) r x"))\
                            .then_inc(image_in[i], 16)
                        sp.wait_ge(cols_done, done)
                        load_low(n, i)
                    if s == 0:
                        part = bass.ds(k * piece, piece) if not isinstance(k, int) else slice(0, piece)
                        sp.dma_start(weight[:].rearrange("p j c e -> p (j c e)")[:, part],
                                     d["tok_w"].rearrange("p j c e -> p (j c e)")[:, part])\
                            .then_inc(preloaded, 16)

                refill(0)
                if s:
                    sp.wait_ge(rooted, s * STAGE)
                with sp.Fori(1, PARTS + 1) as k:
                    if s:
                        flush(s - 1, k)
                    refill(k)
                with sp.Fori(PARTS + 1, STEPS - (s == STAGES - 1)) as k:
                    refill(k)
            sp.wait_ge(rooted, IMAGES)
            for k in range(PARTS):
                flush(STAGES - 1, k + 1)
            for i in range(2):
                sp.wait_ge(stage_out[i], 16 * PARTS * (STAGES // 2))
            sp.wait_ge(preloaded, 16 * (2 + STEPS))

        @block.tensor
        def _(pe):
            pe.wait_ge(tables_in, 16 * (3 + 2 * XB))
            for m in range(LB):
                i, o = m % PRE, pre_ps[m % 2]
                pe.wait_ge(pre_in[i], 48 * (m // PRE + 1))
                if m >= 2:
                    pe.wait_ge(pre_copied, m - 1)
                for q in range(4):
                    nc.tensor.matmul(o[:, 0:U], pre_c[:, i, q], full[:, q], start=q == 0, stop=q == 3)
                for q in range(4):
                    nc.tensor.matmul(o[:, U:2 * U], pre_r[:, i, q], full[:, q], start=q == 0, stop=False)
                nc.tensor.matmul(o[:, U:2 * U], pre_k[:, i], left[:], start=False, stop=True)\
                    .then_inc(pre_done, 1)

            def parity(a, g):
                return a.rearrange("p (t g f) -> p t g f", t=2, g=2)[:, :, g]

            def row_transform(n, i, peeled):
                pe.wait_ge(folded_y, n + 1)
                if not peeled:
                    pe.wait_ge(folded_x, n - 1)
                for h in (1, 0):
                    for j in range(2):
                        q = 2 * h + j
                        for g in range(2):
                            for a in range(2):
                                mm = nc.tensor.matmul(
                                    parity(rows_ps[i][h][:, j * U:(j + 1) * U], g),
                                    fold_y[:, i, 2 * g + a, q * P:(q + 1) * P], ktab[:, 2 * g + a],
                                    start=a == 0, stop=a == 1)
                    mm.then_inc(rows_high if h else rows_low, 1)

            def steps(base, peeled):
                for j in range(XB):
                    row_transform(base + j, j % 2, peeled and j < 2)
                    if peeled and j == 0:
                        continue
                    columns(base, j - 1, peeled)

            def columns(base, j, peeled):
                i, slot, n = j % 2, j % XB, base + j
                pe.wait_ge(folded_x, n + 1)
                if not peeled or j >= 2:
                    pe.wait_ge(parts_done, n - 1)
                pe.wait_ge(low_in[slot], 8 * (base + j - slot) + 32)
                for t in range(2):
                    o = cols_ps[i][0:V, t * U:(t + 1) * U]
                    part = slice(t * V, (t + 1) * V)
                    nc.tensor.matmul(o, low[:, slot, 0, part], low[:, slot, 1], start=True, stop=False,
                                     skip_group_check=True)
                    for g in range(2):
                        for a in range(2):
                            mm = nc.tensor.matmul(parity(o, g), fold_x[:, i, 2 * g + a, part],
                                                  ktab[:, 2 * g + a], start=False, stop=g == 1 and a == 1,
                                                  skip_group_check=True)
                mm.then_inc(cols_done, 1)

            steps(0, True)
            with pe.Fori(XB, IMAGES, XB) as base:
                steps(base, False)
            columns(IMAGES - XB, XB - 1, False)

        @block.vector
        def _(dve):
            def fold_rows(n, j, peeled):
                i, s = j % 2, j % XB
                dve.wait_ge(image_in[s], 4 * (n - s) + 16)
                if not peeled:
                    dve.wait_ge(rows_low, n - 1)
                a, b = image[:, s, 0:2], image[:, s, 2:4]
                nc.vector.tensor_tensor(fold_y[:, i, 0:2], a, b, ALU.add)
                nc.vector.tensor_tensor(fold_y[:, i, 2:4], a, b, ALU.subtract).then_inc(folded_y, 1)

            def fold_columns(n, j, peeled):
                i = j % 2
                dve.wait_ge(rows_low, n + 1)
                dve.wait_ge(high_copied, n + 1)
                if not peeled:
                    dve.wait_ge(cols_done, n - 1)
                a, b = rows_ps[i][0][:, 0:2 * U], high[:, i]
                for k, op in ((0, ALU.add), (1, ALU.subtract)):
                    ins = nc.vector.tensor_tensor(
                        fold_x[:, i, 2 * k:2 * k + 2].rearrange("p a u -> p (a u)"), a, b, op)
                ins.then_inc(folded_x, 1)

            def combine(n, j, peeled):
                i = j % 2
                dve.wait_ge(second_copied, n + 1)
                if not peeled:
                    dve.wait_ge(squared, n - 1)
                a, b = cols_ps[i][0:V, 0:U], second[:, i]
                nc.vector.tensor_tensor(parts[:, i, 0], a, b, ALU.subtract)
                nc.vector.tensor_tensor(parts[:, i, 1], a, b, ALU.add).then_inc(parts_done, 1)

            def steps(base, peeled, last):
                for j in range(XB):
                    if not (last and j == XB - 1):
                        fold_rows(base + j + 1, j + 1, peeled and j + 1 < 2)
                    fold_columns(base + j, j, peeled and j < 2)
                    if not (peeled and j == 0):
                        combine(base + j - 1, j - 1, peeled and j - 1 < 2)

            fold_rows(0, 0, True)
            steps(0, True, False)
            with dve.Fori(XB, IMAGES - XB, XB) as base:
                steps(base, False, False)
            steps(IMAGES - XB, False, True)
            combine(IMAGES - 1, XB - 1, False)

        @block.scalar
        def _(act):
            for m in range(LB):
                i = m % PRE
                act.wait_ge(pre_done, m + 1)
                if m >= PRE:
                    act.wait_ge(pre_out[i], 32 * (m // PRE))
                nc.scalar.copy(pre_o[:, i].rearrange("p a u -> p (a u)"), pre_ps[m % 2][:, 0:2 * U])\
                    .then_inc(pre_copied, 1)

            def copy_high(n, j, peeled):
                i = j % 2
                act.wait_ge(rows_high, n + 1)
                if not peeled:
                    act.wait_ge(folded_x, n - 1)
                nc.scalar.copy(high[:, i], rows_ps[i][1][:, 0:2 * U]).then_inc(high_copied, 1)

            def copy_second(n, j, peeled):
                i = j % 2
                act.wait_ge(cols_done, n + 1)
                if not peeled:
                    act.wait_ge(parts_done, n - 1)
                src = cols_ps[i][0:V, U:2 * U].rearrange("p (t v) -> p t v", t=2)
                nc.scalar.copy(second[:, i].rearrange("p (t v) -> p t v", t=2), src[:, ::-1])\
                    .then_inc(second_copied, 1)

            def square(n, j, peeled):
                i = j % 2
                act.wait_ge(parts_done, n + 1)
                if not peeled:
                    act.wait_ge(added, n - 1)
                nc.scalar.activation(squares[:, i].rearrange("p w u -> p (w u)"),
                                     parts[:, i].rearrange("p w u -> p (w u)"), ACT.Square)\
                    .then_inc(squared, 1)

            def root(n, j, at):
                dst = mags[0:V, :, bass.ds(at, 1)] if not isinstance(at, int) else mags[0:V, :, at:at + 1]
                nc.scalar.activation(dst.rearrange("p r a -> p (r a)"), power2[:, j % 2], ACT.Sqrt)\
                    .then_inc(rooted, 1)

            def steps(base, peeled, entry=None, at=None):
                for j in range(XB):
                    if not (peeled and j < 2):
                        act.wait_ge(added, base + j - 1)
                    copy_high(base + j, j, peeled and j < 2)
                    if not (peeled and j < 2):
                        if entry is not None and j == 2 and entry >= 2:
                            act.wait_ge(stage_out[entry % 2], 16 * PARTS * (entry // 2))
                        root(base + j - 2, j - 2, at(j - 2))
                    if not (peeled and j == 0):
                        copy_second(base + j - 1, j - 1, peeled and j - 1 < 2)
                        square(base + j - 1, j - 1, peeled and j - 1 < 2)

            for s in range(STAGES):
                first = s * STAGE
                place = lambda j, f=first: (f + j) % (2 * STAGE)
                steps(first, s == 0, s, place)
                with act.Fori(1, STEPS) as k:
                    off = k * XB + (s % 2) * STAGE
                    steps(k * XB + first, False, None, lambda j, o=off: o + j)
            n = IMAGES
            act.wait_ge(added, n - 1)
            root(n - 2, 0, (n - 2) % (2 * STAGE))
            copy_second(n - 1, 1, False)
            square(n - 1, 1, False)
            act.wait_ge(added, n)
            root(n - 1, 1, (n - 1) % (2 * STAGE))

        @block.gpsimd
        def _(pool):
            def add(n, j, peeled):
                i = j % 2
                pool.wait_ge(squared, n + 1)
                if not peeled:
                    pool.wait_ge(rooted, n - 1)
                ins = nc.gpsimd.tensor_tensor(power2[:, i].rearrange("p (w v) -> p w v", w=2),
                                              squares[:, i, :, 0:V], squares[:, i, ::-1, V:U], ALU.add)
                ins.then_inc(added, 1)

            for j in range(XB):
                add(j, j, j < 2)
            with pool.Fori(XB, IMAGES, XB) as base:
                for j in range(XB):
                    add(base + j, j, False)




GB = 16
NBG = B // GB
GROUPS = 2 * NBG
HS = HH * S
QP = 32
QI = P // QP
PAIRS = BINS // 2
SLICES = 3
SJ = JC // SLICES


def head_masks():
    f, r = np.arange(EH) // HD, np.arange(HS) // S
    of_head = (f[:, None] == np.arange(HH)).astype(np.float32)
    feat_feat = (f[:, None] == f).astype(np.float32)
    row_feat = (r[:, None] == f).astype(np.float32)
    return of_head, feat_feat, row_feat


def token_attention_phase(nc, d, scratch, weight, rows, ident, h1):
    with ExitStack() as ctx:
        sb = lambda n, s, t=F32: ctx.enter_context(nc.sbuf_tensor(n, s, t))
        sem = lambda n: ctx.enter_context(nc.semaphore(n))
        gathered = sb("gathered", [P, JC, 2 * IMAGES])
        rows_now = sb("rows_now", [P, SLICES, 2 * SJ], I32)
        code = sb("code", [EH, 2, S])
        tok_bias = sb("tok_bias", [EH, 2])
        cls = sb("cls", [EH, 2])
        offset = sb("offset", [EH, 2, S])
        pair_rows = sb("pair_rows", [P, E])
        tokens = sb("tokens", [EH, 2, S, B])
        down = sb("down", [EH, 3, 2, RANK])
        up = sb("up", [RANK, 3, E])
        bias = sb("bias3", [EH, 3, 2])
        m_u = sb("m_u", [RM, EH])
        m_v = sb("m_v", [RM, EH])
        of_head = sb("of_head", [EH, HH])
        feat_feat = sb("feat_feat", [EH, EH])
        row_feat = sb("row_feat", [HS, EH])
        mixer = sb("mixer", [EH, EH])
        low_qk = sb("low_qk", [RANK, 2, P])
        low_v = sb("low_v", [RANK, S, B])
        q = sb("q", [EH, 2, P])
        qm = sb("qm", [EH, 2, B * S + QP])
        k = sb("k", [EH, 2, B, S])
        k_heads = sb("k_heads", [EH, 2, GB, HH, S])
        low_heads = sb("low_heads", [RANK, 2, GB, HH, S])
        v_heads = sb("v_heads", [HS, 2, GB, 2, EH])
        top = sb("top", [P, GROUPS, GB // QI, HH])
        total = sb("total", [P, GROUPS, GB // QI, HH])
        probs = sb("head_probs", [P, 2, GB // QI, HH, S])
        probs_t = sb("head_probs_t", [HS, 2, GB // QI, QI, QP])
        ones = sb("ones", [EH, EH])
        sq = sb("sq", [EH, 2, S, GB])
        rstd = sb("rstd", [EH, NBG, S, GB])
        bank = [ctx.enter_context(nc.psum_tensor(f"bank{i}", [P, 512], F32)) for i in range(8)]
        value_bank = (bank[0], bank[1], bank[6])
        names = ("weights_in rows_copied slices_begun chunk_used offset_done pair_mm pair_copied turn_mm "
                 "tokens_done mixer_mm mixer_done low_mm low_qk_copied low_v_copied up_mm up_copied qm_mm "
                 "qm_copied k_spread low_spread v_mm v_copied score_mm top_done shifted turned_mm "
                 "exp_done summed inverted weights_done probs_copied out_mm pad_set residual_done mean_mm centred sq_done var_mm var_read rooted rstd_done "
                 "normed ones_set").split()
        (weights_in, rows_copied, slices_begun, chunk_used, offset_done, pair_mm, pair_copied, turn_mm,
         tokens_done, mixer_mm, mixer_done, low_mm, low_qk_copied, low_v_copied, up_mm, up_copied, qm_mm,
         qm_copied, k_spread, low_spread, v_mm, v_copied, score_mm, top_done, shifted, turned_mm,
         exp_done, summed, inverted, weights_done, probs_copied, out_mm, pad_set, residual_done, mean_mm, centred, sq_done, var_mm, var_read, rooted, rstd_done,
         normed, ones_set) = [sem(n) for n in names]
        chunk_in = [sem(f"chunk_in{j}") for j in range(JC)]
        loads = [(code, "code"), (tok_bias, "tok_b"), (cls, "cls"), (down, "down"), (up, "up"),
                 (bias, "bias"), (m_u, "m_u"), (m_v, "m_v"), (of_head, "of_head"),
                 (feat_feat, "feat_feat"), (row_feat, "row_feat")]
        width = lambda c: B if c == 0 else P
        at = lambda c: slice(0, 1) if c == 0 else slice(2 * c - 1, 2 * c + 1)
        flat = lambda a: a.rearrange("p s b -> p (s b)")
        wide = lambda a: a.rearrange("p (s b) -> p s b", b=B)
        GC = GB * S
        images = lambda bg: slice(bg * GB, (bg + 1) * GB)
        block = ctx.enter_context(nc.Block())

        @block.sync
        def _(sp):
            for dst, src in loads:
                sp.dma_start(dst[:], d[src]).then_inc(weights_in, 16)

        @block.gpsimd
        def _(pool):
            def pair(p, peeled):
                for c in range(SLICES):
                    if not peeled:
                        pool.wait_ge(chunk_used, (p - 1) * JC + (c + 1) * SJ)
                    src = rows[:, c * 2 * SJ:(c + 1) * 2 * SJ] if peeled else \
                        rows[:, bass.ds(p * (2 * JC) + c * 2 * SJ, 2 * SJ)]
                    nc.gpsimd.tensor_copy(rows_now[:, c], src).then_inc(rows_copied, 1)
                    pool.wait_ge(rows_copied, p * SLICES + c + 1)
                    pool.sem_inc(slices_begun, 1)
                    for j in range(SJ):
                        for n in range(2):
                            nc.gpsimd.indirect_dma_start(
                                gathered[:, c * SJ + j, n * IMAGES:(n + 1) * IMAGES], None, scratch["power"],
                                bass.IndirectOffsetOnAxis(ap=rows_now[:, c, 2 * j + n:2 * j + n + 1], axis=0))\
                                .then_inc(chunk_in[c * SJ + j], 16)

            pair(0, True)
            with pool.Fori(1, PAIRS) as p:
                pair(p, False)

        @block.tensor
        def _(pe):
            def multiply(p, j, acc):
                pe.wait_ge(chunk_in[j], 32 * p + 32)
                by_channel = gathered[:, j].rearrange("p (m c) -> p c m", c=C)
                for c in range(C):
                    mm = nc.tensor.matmul(acc, by_channel[:, c], weight[:, j, c], start=j == 0 and c == 0,
                                          stop=j == JC - 1 and c == C - 1)
                mm.then_inc(chunk_used, 1)
                return mm

            def turn(c):
                pe.wait_ge(pair_copied, c)
                for h in range(2):
                    mm = nc.tensor.matmul(bank[1][0:EH, h * P:(h + 1) * P], pair_rows[:, h * EH:(h + 1) * EH],
                                          ident[:], start=True, stop=True)
                mm.then_inc(turn_mm, 1)

            def low(c, first):
                n = width(0) if first else P
                pe.wait_ge(tokens_done, c + 1)
                if not first:
                    pe.wait_ge(low_v_copied, c)
                for x in range(3):
                    for h in range(2):
                        src = flat(tokens[:, h, 0:1]) if first else \
                            tokens[:, h].rearrange("p s b -> p (s b)")[:, bass.ds(c * P - B, P)]
                        mm = nc.tensor.matmul(bank[2][0:RANK, x * P:x * P + n], down[:, x, h], src,
                                              start=h == 0, stop=h == 1)
                mm.then_inc(low_mm, 1)

            def up_both(c, first):
                n = width(0) if first else P
                pe.wait_ge(low_qk_copied, c + 1)
                if not first:
                    pe.wait_ge(up_copied, c)
                for x in range(2):
                    for h in range(2):
                        mm = nc.tensor.matmul(bank[3][0:EH, (2 * x + h) * P:(2 * x + h) * P + n],
                                              up[:, x, h * EH:(h + 1) * EH], low_qk[:, x, 0:n],
                                              start=True, stop=True)
                mm.then_inc(up_mm, 1)

            def mix(c, first):
                n = width(0) if first else P
                pe.wait_ge(up_copied, c + 1)
                if not first:
                    pe.wait_ge(qm_copied, c)
                for h in range(2):
                    mm = nc.tensor.matmul(bank[4][0:EH, h * P:h * P + n], mixer[:], q[:, h, 0:n],
                                          start=True, stop=True)
                mm.then_inc(qm_mm, 1)

            def pair(p, first):
                acc = bank[0][:, 0:E]
                if not first:
                    pe.wait_ge(pair_copied, p)
                for j in range(JC):
                    mm = multiply(p, j, acc)
                    if j == 2 and not first:
                        turn(p)
                    if j == 5:
                        low(p, first)
                    if j == 8:
                        up_both(p, first)
                    if j == 11:
                        mix(p, first)

            pe.wait_ge(weights_in, 16 * len(loads))
            nc.tensor.matmul(bank[5][0:EH, 0:EH], m_u[:], m_v[:], start=True, stop=True).then_inc(mixer_mm, 1)
            pe.wait_ge(mixer_done, 1)
            pair(0, True)
            with pe.Fori(1, PAIRS) as p:
                pair(p, False)
            turn(PAIRS)
            low(PAIRS, False)
            up_both(PAIRS, False)
            mix(PAIRS, False)

            def values(v):
                bg = v // 2
                pe.wait_ge(low_spread, bg + 1)
                for i in range(v % 2 * (GB // 2), (v % 2 + 1) * (GB // 2)):
                    n = bg * (GB // 2) + i // 2
                    if i % 2 == 0 and n >= 3:
                        pe.wait_ge(v_copied, n - 2)
                    mm = nc.tensor.matmul(value_bank[n % 3][0:HS, i % 2 * E:(i % 2 + 1) * E],
                                          low_heads[:, bg % 2, i].rearrange("p h s -> p (h s)"), up[:, 2],
                                          start=True, stop=True)
                    if i % 2:
                        mm.then_inc(v_mm, 1)

            def scores(g):
                bg, h = divmod(g, 2)
                pe.wait_ge(k_spread, g + 1)
                if g:
                    pe.wait_ge(shifted, g)
                for i in range(GB):
                    at_q, at_k = i % QI * QP, i // QI * HS
                    mm = nc.tensor.matmul(bank[2][at_q:at_q + QP, at_k:at_k + HS],
                                          qm[:, h, (bg * GB + i) * S:(bg * GB + i) * S + QP],
                                          k_heads[:, g % 2, i].rearrange("p h s -> p (h s)"),
                                          start=True, stop=True)
                mm.then_inc(score_mm, 1)

            def turned(g):
                pe.wait_ge(weights_done, g + 1)
                if g:
                    pe.wait_ge(probs_copied, g)
                for c in range(GB // QI):
                    mm = nc.tensor.matmul(bank[3][0:HS, c * P:(c + 1) * P],
                                          probs[:, g % 2, c].rearrange("p h s -> p (h s)"), ident[:],
                                          start=True, stop=True)
                mm.then_inc(turned_mm, 1)

            def weighted(g):
                bg, h = divmod(g, 2)
                pe.wait_ge(v_copied, (bg + 1) * (GB // 2))
                pe.wait_ge(probs_copied, g + 1)
                if g:
                    pe.wait_ge(residual_done, g)
                for i in range(GB):
                    mm = nc.tensor.matmul(bank[4][0:EH, i * S:(i + 1) * S], v_heads[:, bg % 2, i, h],
                                          probs_t[:, g % 2, i // QI, i % QI, 0:S], start=True, stop=True)
                mm.then_inc(out_mm, 1)

            def mean(bg):
                pe.wait_ge(ones_set, 1)
                pe.wait_ge(residual_done, 2 * bg + 2)
                if bg:
                    pe.wait_ge(var_read, bg)
                for h in range(2):
                    mm = nc.tensor.matmul(bank[7][0:EH, 0:GC], ones[:], tokens[:, h, :, images(bg)],
                                          start=h == 0, stop=h == 1)
                mm.then_inc(mean_mm, 1)

            def variance(bg):
                pe.wait_ge(centred, bg + 1)
                pe.wait_ge(sq_done, bg + 1)
                for h in range(2):
                    mm = nc.tensor.matmul(bank[7][0:EH, 0:GC], ones[:], flat(sq[:, h]),
                                          start=h == 0, stop=h == 1)
                mm.then_inc(var_mm, 1)

            pe.wait_ge(pad_set, 1)
            pe.wait_ge(qm_copied, PAIRS + 1)
            scores(0)
            values(0)
            for g in range(GROUPS + 3):
                if g + 1 < GROUPS:
                    scores(g + 1)
                    values(g + 1)
                if g < GROUPS:
                    turned(g)
                if 1 <= g <= GROUPS:
                    weighted(g - 1)
                if g >= 3 and g % 2:
                    mean((g - 3) // 2)
                if g >= 4 and g % 2 == 0:
                    variance((g - 4) // 2)

        @block.scalar
        def _(act):
            def square(bg):
                act.wait_ge(centred, bg + 1)
                if bg:
                    act.wait_ge(var_mm, bg)
                for h in range(2):
                    ins = nc.scalar.activation(sq[:, h], h1[:, h, 0:S, images(bg)], ACT.Square)
                ins.then_inc(sq_done, 1)

            for c in range(PAIRS + 1):
                if c:
                    act.wait_ge(chunk_used, c * JC)
                    if c >= 2:
                        act.wait_ge(turn_mm, c - 1)
                    nc.scalar.copy(pair_rows[:], bank[0][:, 0:E]).then_inc(pair_copied, 1)
                n = width(c)
                act.wait_ge(low_mm, c + 1)
                if c:
                    act.wait_ge(up_mm, c)
                nc.scalar.copy(low_qk[:, :, 0:n],
                               bank[2][0:RANK, 0:2 * P].rearrange("p (x n) -> p x n", x=2)[:, :, 0:n])\
                    .then_inc(low_qk_copied, 1)
            def spread_low(bg):
                if bg >= 2:
                    act.wait_ge(v_mm, (bg - 1) * (GB // 2))
                src = low_v[:, :, images(bg)].rearrange("p (o s) b -> p b o s", o=1)
                nc.scalar.copy(low_heads[:, bg % 2], src.to_broadcast([RANK, GB, HH, S]))\
                    .then_inc(low_spread, 1)

            def exp(g):
                act.wait_ge(shifted, g + 1)
                x = probs[:, g % 2].rearrange("p c h s -> p (c h s)")
                nc.scalar.activation(x, x, ACT.Exp).then_inc(exp_done, 1)

            act.wait_ge(low_v_copied, PAIRS + 1)
            spread_low(0)
            exp(0)
            for g in range(GROUPS):
                if g + 1 < GROUPS:
                    exp(g + 1)
                act.wait_ge(turned_mm, g + 1)
                if g >= 2:
                    act.wait_ge(out_mm, g - 1)
                nc.scalar.copy(probs_t[:, g % 2].rearrange("p c a q -> p (c a q)"), bank[3][0:HS, :])\
                    .then_inc(probs_copied, 1)
                if g % 2 == 0 and g // 2 + 1 < NBG:
                    spread_low(g // 2 + 1)
                if g >= 4 and g % 2 == 0:
                    square((g - 4) // 2)
            square(NBG - 2)
            for bg in range(NBG):
                if bg == NBG - 1:
                    square(bg)
                act.wait_ge(var_read, bg + 1)
                v = rstd[:, bg].rearrange("p s b -> p (s b)")
                nc.scalar.activation(v, v, ACT.Sqrt).then_inc(rooted, 1)

        @block.vector
        def _(dve):
            V_ = nc.vector
            V_.memset(ones[:], 1.0 / E).then_inc(ones_set, 1)
            V_.memset(h1[:, :, S], 0.0)
            V_.memset(qm[:, :, B * S:], 0.0).then_inc(pad_set, 1)
            by_position = lambda a: a.rearrange("p (b s) -> p s b", s=S)
            dve.wait_ge(weights_in, 16 * len(loads))
            for h in range(2):
                V_.tensor_scalar(offset[:, h, 1:S], code[:, h, 1:S], tok_bias[:, h:h + 1], None, ALU.add)
                ins = V_.tensor_scalar(offset[:, h, 0:1], code[:, h, 0:1], cls[:, h:h + 1], None, ALU.add)
            ins.then_inc(offset_done, 1)
            dve.wait_ge(mixer_mm, 1)
            V_.scalar_tensor_tensor(out=mixer[:], in0=bank[5][0:EH, 0:EH], scalar=float(HD) ** -0.5,
                                    in1=feat_feat[:], op0=ALU.mult, op1=ALU.mult).then_inc(mixer_done, 1)
            dve.wait_ge(offset_done, 1)
            V_.tensor_copy(tokens[:, :, 0, :], offset[:, :, 0:1].to_broadcast([EH, 2, B])).then_inc(tokens_done, 1)
            for c in range(PAIRS + 1):
                n = width(c)
                if c:
                    dve.wait_ge(turn_mm, c)
                    for h in range(2):
                        o = offset[:, h, at(c)].rearrange("p (s o) -> p s o", o=1).to_broadcast([EH, 2, B])
                        ins = V_.tensor_tensor(tokens[:, h, at(c)], wide(bank[1][0:EH, h * P:(h + 1) * P]), o,
                                               ALU.add)
                    ins.then_inc(tokens_done, 1)
                dve.wait_ge(low_qk_copied, c + 1)
                V_.tensor_copy(low_v[:, at(c)], wide(bank[2][0:RANK, 2 * P:2 * P + n])).then_inc(low_v_copied, 1)
                dve.wait_ge(up_mm, c + 1)
                if c:
                    dve.wait_ge(qm_mm, c)
                for h in range(2):
                    V_.tensor_scalar(q[:, h, 0:n], bank[3][0:EH, h * P:h * P + n], bias[:, 0, h:h + 1], None,
                                     ALU.add)
                    ins = V_.tensor_scalar(k[:, h].rearrange("p b s -> p s b")[:, at(c)], wide(bank[3][0:EH, (2 + h) * P:(2 + h) * P + n]),
                                           bias[:, 1, h:h + 1], None, ALU.add)
                ins.then_inc(up_copied, 1)
                dve.wait_ge(qm_mm, c + 1)
                for h in range(2):
                    ins = V_.tensor_copy(by_position(qm[:, h, 0:B * S])[:, at(c)], wide(bank[4][0:EH, h * P:h * P + n]))
                ins.then_inc(qm_copied, 1)

            by_head = of_head[:].rearrange("p (o h q) -> p o h q", o=1, q=1).to_broadcast([EH, GB, HH, S])

            def spread_k(g):
                bg, h = divmod(g, 2)
                if g >= 2:
                    dve.wait_ge(score_mm, g - 1)
                v = k[:, h, images(bg)].rearrange("p b (o s) -> p b o s", o=1)
                V_.tensor_tensor(k_heads[:, g % 2], v.to_broadcast([EH, GB, HH, S]), by_head, ALU.mult)\
                    .then_inc(k_spread, 1)

            per_head = [P, GB // QI, HH, S]
            along = lambda a: a.rearrange("p c (h o) -> p c h o", o=1).to_broadcast(per_head)

            def less_top(g):
                dve.wait_ge(score_mm, g + 1)
                x = bank[2][:, 0:GB // QI * HS].rearrange("p (c h s) -> p c h s", c=GB // QI, h=HH)
                V_.tensor_reduce(top[:, g], x, AXX, ALU.max).then_inc(top_done, 1)
                dve.wait_ge(top_done, g + 1)
                if g >= 2:
                    dve.wait_ge(turned_mm, g - 1)
                V_.tensor_tensor(probs[:, g % 2], x, along(top[:, g]), ALU.subtract).then_inc(shifted, 1)

            def weights(g):
                dve.wait_ge(exp_done, g + 1)
                V_.tensor_reduce(total[:, g], probs[:, g % 2], AXX, ALU.add).then_inc(summed, 1)
                dve.wait_ge(summed, g + 1)
                V_.reciprocal(total[:, g], total[:, g]).then_inc(inverted, 1)
                dve.wait_ge(inverted, g + 1)
                V_.tensor_tensor(probs[:, g % 2], probs[:, g % 2], along(total[:, g]), ALU.mult)\
                    .then_inc(weights_done, 1)

            def value_rows(v):
                bg = v // 2
                for i in range(v % 2 * (GB // 4), (v % 2 + 1) * (GB // 4)):
                    n = bg * (GB // 2) + i
                    dve.wait_ge(v_mm, n + 1)
                    if i == 0 and bg >= 2:
                        dve.wait_ge(out_mm, 2 * bg - 2)
                    mask = row_feat[:].rearrange("p (o f) -> p o f", o=1).to_broadcast([HS, 4, EH])
                    V_.tensor_tensor(v_heads[:, bg % 2, 2 * i:2 * i + 2].rearrange("p b h f -> p (b h) f"),
                                     value_bank[n % 3][0:HS, 0:2 * E].rearrange("p (a f) -> p a f", a=4),
                                     mask, ALU.mult).then_inc(v_copied, 1)

            def residual(g):
                bg, h = divmod(g, 2)
                dve.wait_ge(out_mm, g + 1)
                t = tokens[:, h, :, images(bg)].rearrange("p s b -> p b s")
                V_.scalar_tensor_tensor(out=t, in0=bank[4][0:EH, 0:GC].rearrange("p (b s) -> p b s", s=S),
                                        scalar=bias[:, 2, h:h + 1], in1=t, op0=ALU.add, op1=ALU.add)\
                    .then_inc(residual_done, 1)

            def centre(bg):
                dve.wait_ge(mean_mm, bg + 1)
                dve.wait_ge(residual_done, 2 * bg + 2)
                for h in range(2):
                    ins = V_.tensor_tensor(h1[:, h, 0:S, images(bg)], tokens[:, h, :, images(bg)],
                                           bank[7][0:EH, 0:GC].rearrange("p (s b) -> p s b", b=GB), ALU.subtract)
                ins.then_inc(centred, 1)

            def variance(bg):
                dve.wait_ge(var_mm, bg + 1)
                V_.tensor_scalar(rstd[:, bg].rearrange("p s b -> p (s b)"), bank[7][0:EH, 0:GC], EPS, None,
                                 ALU.add).then_inc(var_read, 1)

            def norm(bg):
                dve.wait_ge(rooted, bg + 1)
                dve.wait_ge(centred, bg + 1)
                V_.reciprocal(rstd[:, bg], rstd[:, bg]).then_inc(rstd_done, 1)
                dve.wait_ge(rstd_done, bg + 1)
                for h in range(2):
                    x = h1[:, h, 0:S, images(bg)]
                    ins = V_.tensor_tensor(x, x, rstd[:, bg], ALU.mult)
                ins.then_inc(normed, 1)

            dve.wait_ge(qm_copied, PAIRS + 1)
            spread_k(0)
            spread_k(1)
            less_top(0)
            value_rows(0)
            weights(0)
            for g in range(GROUPS + 3):
                if 2 <= g < GROUPS + 2:
                    residual(g - 2)
                if g >= 4 and g % 2 == 0:
                    centre((g - 4) // 2)
                if g >= 5 and g % 2:
                    variance((g - 5) // 2)
                if g + 1 < GROUPS:
                    less_top(g + 1)
                    value_rows(g + 1)
                if g + 2 < GROUPS:
                    spread_k(g + 2)
                if g + 1 < GROUPS:
                    weights(g + 1)
            for bg in range(NBG):
                if bg == NBG - 1:
                    variance(bg)
                norm(bg)
            dve.wait_ge(normed, NBG)


NT = (2 * T - EXPERTS) // P + EXPERTS
SLOTS = NT * P
TG = 3


def routing_tables():
    before = np.triu(np.ones((P, P), np.float32), 1)
    count = np.arange(EXPERTS, dtype=np.float32)
    rows = {
        "counts": np.broadcast_to(count, (TILES, EXPERTS)),
        "limits": np.broadcast_to(P * np.arange(TILES, dtype=np.float32), (EXPERTS, TILES)),
        "upto": np.tril(np.ones((EXPERTS, EXPERTS), np.float32)),
        "tile_no": np.broadcast_to(np.arange(NT, dtype=np.float32)[:, None], (NT, EXPERTS)),
    }
    out = {n: np.ascontiguousarray(np.broadcast_to(a, (P,) + a.shape)) for n, a in rows.items()}
    valid = (np.arange(TILES)[None] * P + np.arange(P)[:, None] < T).astype(np.float32)
    out["valid"] = np.ascontiguousarray(np.repeat(valid[:, :, None], EXPERTS, 2))
    out["before"] = before
    return out


def expert_phase(nc, d, h1, ident, scratch, out):
    XT = 4
    assert NT % XT == 0 and TILES % TG == 0
    tile_rows = [min(P, T - t * P) for t in range(TILES)]
    RT = [P, TILES, EXPERTS]
    with ExitStack() as ctx:
        sb = lambda n, s, t=F32: ctx.enter_context(nc.sbuf_tensor(n, s, t))
        sem = lambda n: ctx.enter_context(nc.semaphore(n))
        w_router = sb("w_router", [EH, 2, EXPERTS])
        b_router = sb("b_router", [1, EXPERTS])
        one_row = sb("one_row", [1, P])
        all_ones = sb("all_ones", [P, P])
        before = sb("before", [P, P])
        counts = sb("counts", RT)
        limits = sb("limits", [P, EXPERTS, TILES])
        upto = sb("upto", [P, EXPERTS, EXPERTS])
        tile_no = sb("tile_no", [P, NT, EXPERTS])
        valid = sb("valid", RT)
        b_proj = sb("b_proj", [EXPERTS, E])
        zero = sb("zero", [P, NT * E])
        rows = sb("token_rows", [P, TILES, E])
        acc = sb("acc", [P, TILES, E])
        square = sb("square", [P, TG, E])
        results = sb("results", [P, TILES, 2, E])
        (probs, far, best_one, next_one, rest, picked, gate, slot_of, of_slot) = [sb(n, RT) for n in (
            "probs far best_one next_one rest picked gate slot_of of_slot").split()]
        ahead = sb("ahead", [P, TILES + 1, EXPERTS])
        need = sb("need", [P, EXPERTS, TILES])
        tri = sb("tri", [P, EXPERTS, EXPERTS])
        past = sb("past", [P, NT, EXPERTS])
        per_expert = sb("per_expert", [P, 3, EXPERTS])
        gate_t = sb("gate_t", [EXPERTS, TILES, P])
        stat = sb("stat", [P, 10, TILES])
        slots = sb("slots", [P, 2, TILES], I32)
        owner_f = sb("owner_f", [P, NT])
        owner = sb("owner", [P, NT], I32)
        w_fc = sb("w_fc", [EH, XT, 2, FF])
        w_proj = sb("w_proj", [P, XT, FC, E])
        b_fc = sb("b_fc", [P, XT, FC])
        slot_rows = sb("slot_rows", [P, XT, E])
        features = sb("features", [EH, 2, 2, P])
        hidden = sb("hidden", [P, 2, FC, P])
        result = sb("result", [P, XT, E])
        bank = [ctx.enter_context(nc.psum_tensor(f"ebank{i}", [P, 512], F32)) for i in range(8)]
        (small_in, zero_set, zeroed, logits_mm, exp_in, exp_done, routed, rank_mm, placed, rows_mm,
         rows_copied, turn_mm, turned, base_mm, based, scattered, feat_mm, feat_copied, fc_mm, fc_act,
         proj_mm, proj_copied, chain, std_in, std_done, out_ready, out_left, ones_set, added) = [
             sem("e_" + n) for n in (
                 "small_in zero_set zeroed logits_mm exp_in exp_done routed rank_mm placed rows_mm "
                 "rows_copied turn_mm turned base_mm based scattered feat_mm feat_copied fc_mm fc_act "
                 "proj_mm proj_copied chain std_in std_done out_ready out_left ones_set added").split()]
        w_in = [sem(f"e_w_in{i}") for i in range(XT)]
        x_in = [sem(f"e_x_in{i}") for i in range(XT)]
        y_out = [sem(f"e_y_out{i}") for i in range(XT)]
        y_in = [sem(f"e_y_in{i}") for i in range(TILES // TG)]
        small = [(w_router, "w_router"), (b_router, "b_router"), (before, "before"),
                 (counts, "counts"), (limits, "limits"), (upto, "upto"), (tile_no, "tile_no"),
                 (valid, "valid"), (b_proj, "b_proj")]
        block = ctx.enter_context(nc.Block())
        hid = h1[:].rearrange("p h s b -> p h (s b)")

        @block.sync
        def _(sp):
            for dst, src in small:
                sp.dma_start(dst[:], d[src]).then_inc(small_in, 16)
            sp.wait_ge(zero_set, 1)
            sp.dma_start(scratch["slots"].rearrange("(n p) e -> p n e", p=P),
                         zero[:].rearrange("p (n e) -> p n e", e=E)).then_inc(zeroed, 16)

            def load(j, i):
                at = bass.ds(j, 1) if not isinstance(j, int) else slice(j, j + 1)
                e = sp.value_load(owner[0:1, at], min_val=0, max_val=EXPERTS - 1)
                one = bass.ds(e, 1)
                sp.dma_start(w_fc[:, i], d["w_fc"][one].rearrange("a p h f -> (a p) h f")).then_inc(w_in[i], 16)
                sp.dma_start(b_fc[:, i], d["b_fc"][one].rearrange("a p f -> (a p) f")).then_inc(w_in[i], 16)
                sp.dma_start(w_proj[:, i], d["w_proj"][one].rearrange("a p c f -> (a p) c f"))\
                    .then_inc(w_in[i], 16)

            def load_rows(j, i):
                at = bass.ds(j, 1) if not isinstance(j, int) else slice(j, j + 1)
                src = scratch["slots"].rearrange("(n p) e -> n p e", p=P)[at]
                sp.dma_start(slot_rows[:, i], src.rearrange("a p e -> (a p) e")).then_inc(x_in[i], 16)

            def store(j, i):
                at = bass.ds(j, 1) if not isinstance(j, int) else slice(j, j + 1)
                dst = scratch["results"].rearrange("(n p) e -> n p e", p=P)[at]
                sp.dma_start(dst.rearrange("a p e -> (a p) e"), result[:, i]).then_inc(y_out[i], 16)

            sp.wait_ge(placed, 1)
            for i in range(XT):
                load(i, i)
            sp.wait_ge(scattered, 32 * TILES)
            for i in range(XT):
                load_rows(i, i)
            with sp.Fori(0, NT // XT - 1) as k:
                for i in range(XT):
                    j = sp.snap(k * XT + i)
                    done = sp.snap(j + 1)
                    following = sp.snap(j + XT)
                    sp.wait_ge(proj_mm, done)
                    load_rows(following, i)
                    load(following, i)
                    sp.wait_ge(proj_copied, done)
                    store(j, i)
            for i in range(XT):
                sp.wait_ge(proj_copied, NT - XT + i + 1)
                store(NT - XT + i, i)
            for s in range(S):
                if s % (2 * TG) == 0:
                    sp.wait_ge(out_ready, s // (2 * TG) + 1)
                sp.dma_start(out[:, s, :], acc[s % 2 * B:(s % 2 + 1) * B, s // 2, :]).then_inc(out_left, 16)
            sp.wait_ge(out_left, 16 * S)

        @block.gpsimd
        def _(pool):
            nc.gpsimd.memset(zero[:], 0.0).then_inc(zero_set, 1)
            pool.wait_ge(placed, 1)
            pool.wait_ge(zeroed, 16)
            for t in range(TILES):
                r = tile_rows[t]
                pool.wait_ge(rows_copied, t + 1)
                for k in range(2):
                    nc.gpsimd.indirect_dma_start(
                        scratch["slots"], bass.IndirectOffsetOnAxis(ap=slots[0:r, k, t:t + 1], axis=0),
                        rows[0:r, t], None).then_inc(scattered, 16)
            for i in range(XT):
                pool.wait_ge(y_out[i], 16 * (NT // XT))
            for t in range(TILES):
                r = tile_rows[t]
                for k in range(2):
                    nc.gpsimd.indirect_dma_start(
                        results[0:r, t, k], None, scratch["results"],
                        bass.IndirectOffsetOnAxis(ap=slots[0:r, k, t:t + 1], axis=0))\
                        .then_inc(y_in[t // TG], 16)

        @block.tensor
        def _(pe):
            pe.wait_ge(small_in, 16 * len(small))
            pe.wait_ge(ones_set, 2)
            for t in range(TILES):
                o = bank[0][:, t * EXPERTS:(t + 1) * EXPERTS]
                for h in range(2):
                    nc.tensor.matmul(o, hid[:, h, t * P:(t + 1) * P], w_router[:, h], start=h == 0, stop=False)
                mm = nc.tensor.matmul(o, one_row[:], b_router[:], start=False, stop=True)
            mm.then_inc(logits_mm, 1)
            for t in range(TILES):
                if t >= 2:
                    pe.wait_ge(rows_copied, t - 1)
                for h in range(2):
                    mm = nc.tensor.matmul(bank[2 + t % 2][:, h * EH:(h + 1) * EH], hid[:, h, t * P:(t + 1) * P],
                                          ident[0:EH, 0:EH], start=True, stop=True)
                mm.then_inc(rows_mm, 1)
            pe.wait_ge(routed, 1)
            both = picked[:].rearrange("p t e -> p (t e)")
            nc.tensor.matmul(bank[1][:, 0:TILES * EXPERTS], before[:], both, start=True, stop=True)
            nc.tensor.matmul(bank[1][:, 256:256 + TILES * EXPERTS], all_ones[:], both, start=True, stop=True)\
                .then_inc(rank_mm, 1)
            pe.wait_ge(routed, 2)
            for t in range(TILES):
                if t >= 2:
                    pe.wait_ge(turned, t - 1)
                nc.tensor.transpose(bank[4 + t % 2][0:EXPERTS, 0:P], gate[:, t], ident[:]).then_inc(turn_mm, 1)
            for t in range(TILES):
                pe.wait_ge(turned, t + 1)
                if t >= 2:
                    pe.wait_ge(based, t - 1)
                nc.tensor.matmul(bank[6 + t % 2][:, 0:E], gate_t[:, t], b_proj[:], start=True, stop=True)\
                    .then_inc(base_mm, 1)
            pe.wait_ge(based, TILES)

            def turn(j, i, q, peeled):
                pe.wait_ge(x_in[i], 4 * (j - i) + 16)
                if not peeled:
                    pe.wait_ge(feat_copied, j - 1)
                for h in range(2):
                    mm = nc.tensor.matmul(bank[q][0:EH, h * P:(h + 1) * P], slot_rows[:, i, h * EH:(h + 1) * EH],
                                          ident[:], start=True, stop=True)
                mm.then_inc(feat_mm, 1)

            def up(j, i, q, peeled):
                pe.wait_ge(w_in[i], 12 * (j - i) + 48)
                pe.wait_ge(feat_copied, j + 1)
                if not peeled:
                    pe.wait_ge(fc_act, FC * (j - 1))
                for f in range(FC):
                    o = bank[2 + 2 * q + f // 3][:, f % 3 * P:(f % 3 + 1) * P]
                    for h in range(2):
                        mm = nc.tensor.matmul(o, w_fc[:, i, h, f * P:(f + 1) * P], features[:, q, h],
                                              start=h == 0, stop=h == 1)
                    if f % 3 == 2:
                        mm.then_inc(fc_mm, 1)

            def down(j, i, q, peeled):
                pe.wait_ge(fc_act, FC * (j + 1))
                if not peeled:
                    pe.wait_ge(proj_copied, j - 1)
                for f in range(FC):
                    mm = nc.tensor.matmul(bank[6 + q][:, 0:E], hidden[:, q, f], w_proj[:, i, f],
                                          start=f == 0, stop=f == FC - 1)
                mm.then_inc(proj_mm, 1)

            def step(base, i, peeled):
                turn(base + i, i, i % 2, peeled and i < 2)
                up(base + i, i, i % 2, peeled and i < 2)
                if not (peeled and i == 0):
                    down(base + i - 1, (i - 1) % XT, (i - 1) % 2, peeled and i - 1 < 2)

            for i in range(XT):
                step(0, i, True)
            with pe.Fori(1, NT // XT) as k:
                for i in range(XT):
                    step(k * XT, i, False)
            down(NT - 1, XT - 1, 1, False)

        @block.scalar
        def _(act):
            act.wait_ge(exp_in, 1)
            nc.scalar.activation(probs[:], probs[:], ACT.Exp).then_inc(exp_done, 1)
            for t in range(TILES):
                act.wait_ge(rows_mm, t + 1)
                nc.scalar.copy(rows[:, t], bank[2 + t % 2][:, 0:E]).then_inc(rows_copied, 1)

            def gelu(j, i, peeled):
                q = i % 2
                if not peeled:
                    act.wait_ge(proj_mm, j - 1)
                for f in range(FC):
                    if f % 3 == 0:
                        act.wait_ge(fc_mm, 2 * j + f // 3 + 1)
                    nc.scalar.activation(hidden[:, q, f], bank[2 + 2 * q + f // 3][:, f % 3 * P:(f % 3 + 1) * P],
                                         ACT.Gelu_apprx_tanh, bias=b_fc[:, i, f:f + 1]).then_inc(fc_act, 1)

            for i in range(XT):
                gelu(i, i, i < 2)
            with act.Fori(1, NT // XT) as k:
                for i in range(XT):
                    gelu(k * XT + i, i, False)
            for g in range(TILES // TG):
                act.wait_ge(std_in, g + 1)
                v = stat[:, 8, g * TG:(g + 1) * TG]
                nc.scalar.activation(v, v, ACT.Sqrt).then_inc(std_done, 1)

        @block.vector
        def _(dve):
            step = [0]

            def then(ins):
                step[0] += 1
                ins.then_inc(chain, 1)
                dve.wait_ge(chain, step[0])

            def spread(a, n, w):
                return a.rearrange("p (t o) -> p t o", o=1).to_broadcast([P, n, w])

            def repeat(a, n, w):
                return a.rearrange("p (o t) -> p o t", o=1).to_broadcast([P, n, w])

            tok = lambda a: spread(a, TILES, EXPERTS)
            V_ = nc.vector
            V_.memset(one_row[:], 1.0).then_inc(ones_set, 1)
            V_.memset(all_ones[:], 1.0).then_inc(ones_set, 1)
            then(V_.memset(ahead[:, 0], 0.0))
            dve.wait_ge(small_in, 16 * len(small))
            dve.wait_ge(logits_mm, 1)
            logits = bank[0][:, 0:TILES * EXPERTS].rearrange("p (t e) -> p t e", e=EXPERTS)
            then(V_.tensor_reduce(stat[:, 0], logits, AXX, ALU.max))
            V_.tensor_tensor(probs[:], logits, tok(stat[:, 0]), ALU.subtract).then_inc(exp_in, 1)
            dve.wait_ge(exp_done, 1)
            then(V_.tensor_reduce(stat[:, 1], probs[:], AXX, ALU.add))
            then(V_.reciprocal(stat[:, 1], stat[:, 1]))
            then(V_.tensor_tensor(probs[:], probs[:], tok(stat[:, 1]), ALU.mult))

            def best(src, onehot, value):
                then(V_.tensor_reduce(value, src, AXX, ALU.max))
                then(V_.tensor_tensor(far[:], src, tok(value), ALU.is_lt))
                then(V_.scalar_tensor_tensor(out=far[:], in0=far[:], scalar=float(EXPERTS), in1=counts[:],
                                             op0=ALU.mult, op1=ALU.add))
                then(V_.tensor_reduce(stat[:, 6], far[:], AXX, ALU.min))
                then(V_.tensor_tensor(onehot[:], counts[:], tok(stat[:, 6]), ALU.is_equal))

            best(probs[:], best_one, stat[:, 2])
            then(V_.scalar_tensor_tensor(out=rest[:], in0=best_one[:], scalar=-2.0, in1=probs[:],
                                         op0=ALU.mult, op1=ALU.add))
            best(rest[:], next_one, stat[:, 3])
            then(V_.tensor_tensor(rest[:], best_one[:], next_one[:], ALU.add))
            V_.tensor_tensor(picked[:], rest[:], valid[:], ALU.mult).then_inc(routed, 1)
            then(V_.tensor_tensor(stat[:, 7], stat[:, 2], stat[:, 3], ALU.add))
            then(V_.reciprocal(stat[:, 7], stat[:, 7]))
            for k in range(2):
                then(V_.tensor_tensor(stat[:, 4 + k], stat[:, 2 + k], stat[:, 7], ALU.mult))
            then(V_.tensor_tensor(gate[:], best_one[:], tok(stat[:, 4]), ALU.mult))
            then(V_.tensor_tensor(rest[:], next_one[:], tok(stat[:, 5]), ALU.mult))
            V_.tensor_tensor(gate[:], gate[:], rest[:], ALU.add).then_inc(routed, 1)
            dve.wait_ge(rank_mm, 1)
            total = bank[1][:, 256:256 + TILES * EXPERTS].rearrange("p (t e) -> p t e", e=EXPERTS)
            for t in range(TILES):
                then(V_.tensor_tensor(ahead[:, t + 1], total[:, t], ahead[:, t], ALU.add))
            then(V_.tensor_tensor(need[:], spread(ahead[:, TILES], EXPERTS, TILES), limits[:], ALU.is_gt))
            then(V_.tensor_reduce(per_expert[:, 0], need[:], AXX, ALU.add))
            then(V_.tensor_tensor(tri[:], repeat(per_expert[:, 0], EXPERTS, EXPERTS), upto[:], ALU.mult))
            then(V_.tensor_reduce(per_expert[:, 1], tri[:], AXX, ALU.add))
            then(V_.tensor_tensor(past[:], repeat(per_expert[:, 1], NT, EXPERTS), tile_no[:], ALU.is_le))
            then(V_.tensor_reduce(owner_f[:], past[:], AXX, ALU.add))
            then(V_.tensor_scalar(owner[:], owner_f[:], float(EXPERTS - 1), None, ALU.min))
            then(V_.tensor_tensor(per_expert[:, 2], per_expert[:, 1], per_expert[:, 0], ALU.subtract))
            then(V_.tensor_scalar(per_expert[:, 2], per_expert[:, 2], float(P), None, ALU.mult))
            rank = bank[1][:, 0:TILES * EXPERTS].rearrange("p (t e) -> p t e", e=EXPERTS)
            then(V_.tensor_tensor(slot_of[:], rank, ahead[:, 0:TILES], ALU.add))
            then(V_.tensor_tensor(slot_of[:], slot_of[:], repeat(per_expert[:, 2], TILES, EXPERTS), ALU.add))
            for k, onehot in enumerate((best_one, next_one)):
                then(V_.tensor_tensor(of_slot[:], slot_of[:], onehot[:], ALU.mult))
                then(V_.tensor_reduce(stat[:, 6 + k], of_slot[:], AXX, ALU.add))
            V_.tensor_copy(slots[:], stat[:, 6:8]).then_inc(placed, 1)
            for t in range(TILES):
                dve.wait_ge(turn_mm, t + 1)
                V_.tensor_copy(gate_t[:, t], bank[4 + t % 2][0:EXPERTS, 0:P]).then_inc(turned, 1)
            for t in range(TILES):
                dve.wait_ge(base_mm, t + 1)
                dve.wait_ge(rows_copied, t + 1)
                V_.tensor_tensor(acc[:, t], bank[6 + t % 2][:, 0:E], rows[:, t], ALU.add).then_inc(based, 1)

            def copy_features(j, q, peeled):
                dve.wait_ge(feat_mm, j + 1)
                if not peeled:
                    dve.wait_ge(fc_mm, 2 * (j - 1))
                V_.tensor_copy(features[:, q].rearrange("p h n -> p (h n)"), bank[q][0:EH, 0:2 * P])\
                    .then_inc(feat_copied, 1)

            def copy_result(j, i, peeled):
                dve.wait_ge(proj_mm, j + 1)
                if not peeled:
                    dve.wait_ge(y_out[i], 4 * (j - i))
                V_.tensor_copy(result[:, i], bank[6 + i % 2][:, 0:E]).then_inc(proj_copied, 1)

            for i in range(XT):
                copy_features(i, i % 2, i < 2)
                if i:
                    copy_result(i - 1, i - 1, True)
            copy_features(XT, 0, False)
            copy_result(XT - 1, XT - 1, True)
            for i in range(1, XT):
                copy_features(XT + i, i % 2, False)
                copy_result(XT + i - 1, i - 1, False)
            with dve.Fori(2, NT // XT) as k:
                for i in range(XT):
                    copy_features(k * XT + i, i % 2, False)
                    copy_result(k * XT + i - 1, (i - 1) % XT, False)
            copy_result(NT - 1, XT - 1, False)

            for g in range(TILES // TG):
                ts = slice(g * TG, (g + 1) * TG)
                a = acc[:, ts]
                wide = lambda v: spread(v[:, ts], TG, E)
                dve.wait_ge(y_in[g], 32 * TG)
                for t in range(g * TG, (g + 1) * TG):
                    r = tile_rows[t]
                    for k in range(2):
                        n = 2 * t + k
                        if k:
                            dve.wait_ge(added, n)
                        ins = V_.scalar_tensor_tensor(out=acc[0:r, t], in0=results[0:r, t, k],
                                                      scalar=stat[0:r, 4 + k, t:t + 1], in1=acc[0:r, t],
                                                      op0=ALU.mult, op1=ALU.add)
                        ins.then_inc(added, 1)
                dve.wait_ge(added, 2 * TG * (g + 1))
                then(V_.tensor_reduce(stat[:, 9, ts], a, AXX, ALU.add))
                then(V_.tensor_scalar(stat[:, 9, ts], stat[:, 9, ts], 1.0 / E, None, ALU.mult))
                then(V_.tensor_tensor(a, a, wide(stat[:, 9]), ALU.subtract))
                then(V_.tensor_tensor(square[:], a, a, ALU.mult))
                then(V_.tensor_reduce(stat[:, 8, ts], square[:], AXX, ALU.add))
                v = stat[:, 8, ts]
                V_.tensor_scalar(v, v, 1.0 / E, EPS, ALU.mult, ALU.add).then_inc(std_in, 1)
                dve.wait_ge(std_done, g + 1)
                then(V_.reciprocal(v, v))
                V_.tensor_tensor(a, a, wide(stat[:, 8]), ALU.mult).then_inc(out_ready, 1)




def vit_tower(nc, d, out):
    scratch = {
        "power": nc.dram_tensor("power", [ROWS, IMAGES], F32).ap(),
        "left_cols": nc.dram_tensor("left_cols", [IMAGES, NL, U], F32).ap(),
        "left_rows": nc.dram_tensor("left_rows", [IMAGES, NL, U], F32).ap(),
        "slots": nc.dram_tensor("slot_rows_dram", [SLOTS, E], F32).ap(),
        "results": nc.dram_tensor("results_dram", [SLOTS, E], F32).ap(),
    }
    with ExitStack() as ctx:
        ident = ctx.enter_context(nc.sbuf_tensor("ident", [P, P], F32))
        h1 = ctx.enter_context(nc.sbuf_tensor("h1", [EH, 2, S + 1, B], F32))
        with ExitStack() as until_tokens:
            weight = until_tokens.enter_context(nc.sbuf_tensor("weight", [P, JC, C, E], F32))
            rows = until_tokens.enter_context(nc.sbuf_tensor("rows", [P, BINS * JC], I32))
            dft_phase(nc, d, scratch, weight, rows, ident)
            token_attention_phase(nc, d, scratch, weight, rows, ident, h1)
        expert_phase(nc, d, h1, ident, scratch, out)



def layout(x, L0_tok_cls_token, L0_tok_W, L0_tok_b, **w):
    x = np.asarray(x)
    order = [((b - B // 2) % B, (c - C // 2) % C) for b in range(B) for c in range(C)]
    flat = x.reshape(B * C, N, N)
    src = np.array([b * C + c for b, c in order])
    rows = np.concatenate(FOLDED)
    main = np.empty((IMAGES, P, 4, 4 * P), np.float32)
    cols = np.empty((IMAGES, NL, 4, P), np.float32)
    for n, k in enumerate(src):
        image = flat[k]
        picked = image[rows]
        main[n] = picked[:, rows].reshape(4, P, 4 * P).transpose(1, 0, 2)
        cols[n] = picked[:, LEFT].T.reshape(NL, 4, P)
    left = flat[src][:, LEFT]
    chunks = lambda a: np.ascontiguousarray(
        a.reshape(-1, P, 4, P).transpose(0, 3, 2, 1))
    corner = left[:, :, LEFT].reshape(-1, P, NL).transpose(0, 2, 1)
    per_half = lambda a: np.ascontiguousarray(
        np.asarray(a).reshape(2, EH, -1).transpose(1, 0, 2))
    w = {name: np.asarray(a) for name, a in w.items()}
    of_head, feat_feat, row_feat = head_masks()
    tab = trig(np.concatenate(FOLDED)).reshape(4, P, U).transpose(1, 0, 2)
    return {
        "x": main,
        "x_cols": chunks(cols),
        "x_rows": chunks(left[:, :, rows].reshape(IMAGES, NL, 4, P)),
        "x_corner": np.ascontiguousarray(corner),
        "ktab": folded_trig(), "full": np.ascontiguousarray(tab), "left": trig(LEFT),
        "rows": radial_rows(), "code": position_code(),
        "tok_w": np.ascontiguousarray(np.asarray(L0_tok_W).reshape(E, C, JC, P).transpose(3, 2, 1, 0)),
        "tok_b": per_half(np.asarray(L0_tok_b))[:, :, 0],
        "cls": per_half(np.asarray(L0_tok_cls_token).reshape(E))[:, :, 0],
        "down": np.ascontiguousarray(np.stack([per_half(w["L0_attn_V_" + n]) for n in "QKV"], 1)),
        "up": np.ascontiguousarray(np.stack([w["L0_attn_U_" + n] for n in "QKV"], 1)),
        "bias": np.ascontiguousarray(np.stack([per_half(w["L0_attn_bias_" + n])[:, :, 0] for n in "qkv"], 1)),
        "m_u": np.ascontiguousarray(np.tile(np.asarray(w["L0_attn_M_U"]).T, (1, HH))),
        "m_v": np.ascontiguousarray(np.tile(w["L0_attn_M_V"], (1, HH))),
        "of_head": of_head, "feat_feat": feat_feat, "row_feat": row_feat,
        "w_router": per_half(w["L0_ffn_Wr"]),
        "b_router": np.asarray(w["L0_ffn_br"]).reshape(1, EXPERTS),
        "ident": np.eye(P, dtype=np.float32),
        **routing_tables(),
        "b_fc": np.ascontiguousarray(np.asarray(w["L0_ffn_bfc"]).reshape(EXPERTS, FC, P).transpose(0, 2, 1)),
        "b_proj": np.asarray(w["L0_ffn_bproj"]),
        "w_fc": np.ascontiguousarray(np.asarray(w["L0_ffn_Wfc"]).reshape(EXPERTS, 2, EH, FF).transpose(0, 2, 1, 3)),
        "w_proj": np.ascontiguousarray(
            np.asarray(w["L0_ffn_Wproj"]).reshape(EXPERTS, FC, P, E).transpose(0, 2, 1, 3)),
    }


def kernel(**inputs):
    import concourse.bacc as bacc
    from concourse.bass_utils import run_bass_kernel_spmd as run

    nc = bacc.Bacc("TRN2", target_bir_lowering=False, num_devices=1)
    arrays, aps = {}, {}
    for name, a in layout(**inputs).items():
        a = np.ascontiguousarray(a)
        arrays[f"in_{name}"] = a
        aps[name] = nc.dram_tensor(f"in_{name}", list(a.shape), mybir.dt.from_np(a.dtype),
                                   kind="ExternalInput").ap()
    out = nc.dram_tensor("tokens_out", [B, S, E], F32, kind="ExternalOutput").ap()
    vit_tower(nc, aps, out)
    return run(nc, [arrays], core_ids=[0]).results[0]["tokens_out"]
```

```python
from contextlib import ExitStack

import numpy as np

import concourse.bass as bass
from concourse import mybir

F32 = mybir.dt.float32
I32 = mybir.dt.int32
ALU = mybir.AluOpType
ACT = mybir.ActivationFunctionType
AXX = mybir.AxisListType.X

P = 128
N = 518
HALF = N // 2
KEEP = 96
NE = KEEP // 2 + 1
U = 4 * NE
V = 2 * NE
NL = 6
LEFT = [0, 129, 130, HALF, 388, 389]
FOLD = np.arange(1, P + 1)
FOLDED = [FOLD, HALF - FOLD, HALF + FOLD, N - FOLD]
B, C, E = 64, 3, 192
IMAGES = B * C
STAGE = 48
ROWS = V * 2 * V
BINS, BINSZ = 16, 2304
JC = BINSZ // P
EH = E // 2
S = BINS + 1
T = S * B
HEADS, HD, RANK, RM = 12, 16, 96, 64
HH = HEADS // 2
EXPERTS, FF = 8, 768
FC = FF // P
TILES = -(-T // P)
EPS = 1e-5


def trig(pos):
    a = 2 * np.pi / N * np.asarray(pos, np.float64)[:, None]
    fe, fo = 2 * np.arange(NE), 2 * np.arange(NE) + 1
    t = np.stack([np.cos(a * fe), np.cos(a * fo), np.sin(a * fe), np.sin(a * fo)], 1)
    t[:, 1::2, NE - 1] = 0
    return t.reshape(-1, U).astype(np.float32)


def folded_trig():
    t = trig(FOLD).reshape(P, 4, NE)
    out = np.stack([t[:, 0], t[:, 2], t[:, 0], -t[:, 2], t[:, 1], t[:, 3], -t[:, 1], t[:, 3]], 1)
    return np.ascontiguousarray(out.reshape(P, 4, V))


def radial_rows():
    side = 2 * KEEP
    y, x = np.meshgrid(np.arange(side), np.arange(side), indexing="ij")
    d = np.sqrt((x - side / 2.0) ** 2 + (y - side / 2.0) ** 2).reshape(-1)
    idx = np.argsort(d, kind="stable")
    fy, fx = idx // side - KEEP, idx % side - KEEP
    v, u = np.abs(fy), np.where(fy < 0, -fx, fx)
    place = lambda f: (f % 2) * NE + f // 2
    row = (place(v) * 2 + (u < 0)) * V + place(np.abs(u))
    row = row.reshape(BINS // 2, 2, JC, P).transpose(3, 0, 2, 1)
    return np.ascontiguousarray(row.reshape(P, BINS * JC).astype(np.int32))


def position_code():
    pos = np.arange(S)[:, None].astype(np.float32)
    div = np.exp(np.arange(0, E, 2).astype(np.float32) * (-np.log(10000.0) / E))
    pe = np.zeros((S, E), np.float32)
    pe[:, 0::2], pe[:, 1::2] = np.sin(pos * div), np.cos(pos * div)
    return np.ascontiguousarray(pe.T.reshape(2, EH, S).transpose(1, 0, 2))


def dft_phase(nc, d, scratch, weight, rows, ident, spare):
    LB = IMAGES * NL // P
    PRE = 3
    XB = 4
    assert LB % PRE == 0 and IMAGES % XB == 0 and STAGE % XB == 0
    STEPS = STAGE // XB
    STAGES = IMAGES // STAGE
    PARTS = 2 * V // NE
    EARLY = 8
    assert STAGES % 2 == 0 and PARTS < EARLY
    with ExitStack() as ctx:
        sb = lambda n, s: ctx.enter_context(nc.sbuf_tensor(n, s, F32))
        ps = lambda n: ctx.enter_context(nc.psum_tensor(n, [P, 512], F32))
        sem = lambda n: ctx.enter_context(nc.semaphore(n))
        image = sb("image", [P, XB, 4, 512])
        fold_y = sb("fold_y", [P, 2, 4, 512])
        high = sb("high", [P, 2, 2 * U])
        fold_x = sb("fold_x", [P, 2, 4, U])
        second = sb("second", [V, 2, U])
        parts, squares = [spare[0:V, 4 * U * i:4 * U * (i + 1)].rearrange("p (i w u) -> p i w u", i=2, w=2)
                          for i in range(2)]
        power2 = sb("power2", [V, 2, 2 * V])
        mags = sb("mags", [P, 2 * V, 2 * STAGE])
        ktab = sb("ktab", [P, 4, V])
        full = sb("full", [P, 4, U])
        left = sb("left", [NL, U])
        low = sb("low", [2 * NL, XB, 2, U])
        rest = mags[:].rearrange("p r i -> p (r i)")
        space = {}
        for name, size in (("c", 4 * P), ("r", 4 * P), ("k", P), ("o", 2 * U)):
            space[name], rest = rest[:, 0:PRE * size], rest[:, PRE * size:]
        pre_c = space["c"].rearrange("p (i q n) -> p i q n", i=PRE, q=4)
        pre_r = space["r"].rearrange("p (i q n) -> p i q n", i=PRE, q=4)
        pre_k = space["k"].rearrange("p (i n) -> p i n", i=PRE)[0:NL]
        pre_o = space["o"].rearrange("p (i a u) -> p i a u", i=PRE, a=2)
        rows_ps = [[ps(f"rows{i}{h}") for h in range(2)] for i in range(2)]
        cols_ps = [ps(f"cols{i}") for i in range(2)]
        pre_ps = [ps(f"pre{i}") for i in range(2)]

        full_in, tables_in = sem("full_in"), sem("tables_in")
        pre_in = [sem(f"pre_in{i}") for i in range(PRE)]
        pre_done = sem("pre_done")
        pre_copied = sem("pre_copied")
        pre_out = [sem(f"pre_out{i}") for i in range(PRE)]
        image_in = [sem(f"image_in{i}") for i in range(XB)]
        low_in = [sem(f"low_in{i}") for i in range(XB)]
        folded_y = sem("folded_y")
        rows_high = sem("rows_high")
        rows_low = sem("rows_low")
        high_copied = sem("high_copied")
        folded_x = sem("folded_x")
        cols_done = sem("cols_done")
        second_copied = sem("second_copied")
        parts_done = sem("parts_done")
        squared = sem("squared")
        added = sem("added")
        rooted = sem("rooted")
        preloaded = sem("preloaded")
        stage_out = [sem(f"stage_out{i}") for i in range(2)]
        block = ctx.enter_context(nc.Block())

        @block.sync
        def _(sp):
            def load_pre(m, i):
                sp.dma_start(pre_c[:, i], d["x_cols"][m]).then_inc(pre_in[i], 16)
                sp.dma_start(pre_r[:, i], d["x_rows"][m]).then_inc(pre_in[i], 16)
                sp.dma_start(pre_k[:, i], d["x_corner"][m]).then_inc(pre_in[i], 16)

            def load_image(n, i):
                sp.dma_start(image[:, i], d["x"][n]).then_inc(image_in[i], 16)

            def load_low(n, i):
                rows = bass.ds(n, 1) if not isinstance(n, int) else slice(n, n + 1)
                sp.dma_start(low[0:NL, i, 0, :], scratch["left_cols"][rows].rearrange("a l u -> (a l) u"))\
                    .then_inc(low_in[i], 16)
                sp.dma_start(low[NL:, i, 1, :], scratch["left_rows"][rows].rearrange("a l u -> (a l) u"))\
                    .then_inc(low_in[i], 16)

            sp.dma_start(full[:], d["full"]).then_inc(full_in, 16)
            load_pre(0, 0)
            sp.dma_start(left[:], d["left"]).then_inc(full_in, 16)
            for i in range(1, PRE):
                load_pre(i, i)
            sp.dma_start(ktab[:], d["ktab"]).then_inc(tables_in, 16)
            for m in range(LB):
                i = m % PRE
                sp.wait_ge(pre_copied, m + 1)
                for side, name in enumerate(("left_cols", "left_rows")):
                    sp.dma_start(scratch[name].rearrange("a l u -> (a l) u")[m * P:(m + 1) * P],
                                 pre_o[:, i, side]).then_inc(pre_out[i], 16)
                if m + PRE < LB:
                    load_pre(m + PRE, i)
                if m < XB:
                    load_image(m, m)
                    sp.dma_start(low[NL:, m, 0, :], d["left"]).then_inc(tables_in, 16)
                    sp.dma_start(low[0:NL, m, 1, :], d["left"]).then_inc(tables_in, 16)
            for i in range(PRE):
                sp.wait_ge(pre_out[i], 32 * (LB // PRE))
            for i in range(XB):
                load_low(i, i)

            def flush(s, k, some=slice(0, STAGE)):
                part = bass.ds((k - 1) * NE, NE)
                first = s % 2 * STAGE
                power = scratch["power"].rearrange("(v r) (s i) -> s v r i", v=V, i=STAGE)
                sp.dma_start(power[s][:, part, some],
                             mags[0:V, part, first + some.start:first + some.stop])\
                    .then_inc(stage_out[s % 2], 16)

            for dst, src in ((rows, "rows"), (ident, "ident")):
                sp.dma_start(dst[:], d[src]).then_inc(preloaded, 16)
            piece = JC * C * E // STEPS
            for s in range(STAGES):
                def refill(k, s=s):
                    for i in range(XB):
                        n = k * XB + (s * STAGE + i + XB)
                        done = k * XB + (s * STAGE + i + 1)
                        if not isinstance(k, int):
                            n, done = sp.snap(n), sp.snap(done)
                        one = bass.ds(n, 1) if not isinstance(n, int) else slice(n, n + 1)
                        sp.wait_ge(folded_y, done)
                        sp.dma_start(image[:, i], d["x"][one].rearrange("a p r x -> (a p) r x"))\
                            .then_inc(image_in[i], 16)
                        sp.wait_ge(cols_done, done)
                        load_low(n, i)
                    if s == 0:
                        part = bass.ds(k * piece, piece)
                        sp.dma_start(weight[:].rearrange("p j c e -> p (j c e)")[:, part],
                                     d["tok_w"].rearrange("p j c e -> p (j c e)")[:, part])\
                            .then_inc(preloaded, 16)

                refill(0)
                if s:
                    sp.wait_ge(rooted, s * STAGE)
                with sp.Fori(1, PARTS + 1) as k:
                    if s:
                        flush(s - 1, k)
                    refill(k)
                if s < STAGES - 1:
                    with sp.Fori(PARTS + 1, STEPS) as k:
                        refill(k)
            with sp.Fori(PARTS + 1, EARLY + 1) as k:
                refill(k)
            sp.wait_ge(rooted, (STAGES - 1) * STAGE + EARLY * XB)
            for k in range(PARTS):
                flush(STAGES - 1, k + 1, slice(0, EARLY * XB))
                if EARLY + 1 + k < STEPS - 1:
                    refill(EARLY + 1 + k)
            sp.wait_ge(rooted, IMAGES)
            for k in range(PARTS):
                flush(STAGES - 1, k + 1, slice(EARLY * XB, STAGE))
            for i in range(2):
                sp.wait_ge(stage_out[i], 16 * PARTS * (STAGES // 2 + i))
            sp.wait_ge(preloaded, 16 * (2 + STEPS))

        @block.tensor
        def _(pe):
            pe.wait_ge(full_in, 32)
            for m in range(LB):
                i, o = m % PRE, pre_ps[m % 2]
                pe.wait_ge(pre_in[i], 48 * (m // PRE + 1))
                if m >= 2:
                    pe.wait_ge(pre_copied, m - 1)
                for q in range(4):
                    nc.tensor.matmul(o[:, 0:U], pre_c[:, i, q], full[:, q], start=q == 0, stop=q == 3)
                for q in range(4):
                    nc.tensor.matmul(o[:, U:2 * U], pre_r[:, i, q], full[:, q], start=q == 0, stop=False)
                nc.tensor.matmul(o[:, U:2 * U], pre_k[:, i], left[:], start=False, stop=True)\
                    .then_inc(pre_done, 1)

            def parity(a, g):
                return a.rearrange("p (t g f) -> p t g f", t=2, g=2)[:, :, g]

            def row_transform(n, i, peeled):
                pe.wait_ge(folded_y, n + 1)
                if not peeled:
                    pe.wait_ge(folded_x, n - 1)
                for h in (1, 0):
                    for j in range(2):
                        q = 2 * h + j
                        for g in range(2):
                            for a in range(2):
                                mm = nc.tensor.matmul(
                                    parity(rows_ps[i][h][:, j * U:(j + 1) * U], g),
                                    fold_y[:, i, 2 * g + a, q * P:(q + 1) * P], ktab[:, 2 * g + a],
                                    start=a == 0, stop=a == 1)
                    mm.then_inc(rows_high if h else rows_low, 1)

            def steps(base, peeled):
                for j in range(XB):
                    row_transform(base + j, j % 2, peeled and j < 2)
                    if peeled and j == 0:
                        continue
                    columns(base, j - 1, peeled)

            def columns(base, j, peeled):
                i, slot, n = j % 2, j % XB, base + j
                pe.wait_ge(folded_x, n + 1)
                if not peeled or j >= 2:
                    pe.wait_ge(parts_done, n - 1)
                pe.wait_ge(low_in[slot], 8 * (base + j - slot) + 32)
                for t in range(2):
                    o = cols_ps[i][0:V, t * U:(t + 1) * U]
                    part = slice(t * V, (t + 1) * V)
                    nc.tensor.matmul(o, low[:, slot, 0, part], low[:, slot, 1], start=True, stop=False,
                                     skip_group_check=True)
                    for g in range(2):
                        for a in range(2):
                            mm = nc.tensor.matmul(parity(o, g), fold_x[:, i, 2 * g + a, part],
                                                  ktab[:, 2 * g + a], start=False, stop=g == 1 and a == 1,
                                                  skip_group_check=True)
                mm.then_inc(cols_done, 1)

            pe.wait_ge(tables_in, 16 * (1 + 2 * XB))
            steps(0, True)
            with pe.Fori(XB, IMAGES, XB) as base:
                steps(base, False)
            columns(IMAGES - XB, XB - 1, False)

        @block.vector
        def _(dve):
            def fold_rows(n, j, peeled):
                i, s = j % 2, j % XB
                dve.wait_ge(image_in[s], 4 * (n - s) + 16)
                if not peeled:
                    dve.wait_ge(rows_low, n - 1)
                a, b = image[:, s, 0:2], image[:, s, 2:4]
                nc.vector.tensor_tensor(fold_y[:, i, 0:2], a, b, ALU.add)
                nc.vector.tensor_tensor(fold_y[:, i, 2:4], a, b, ALU.subtract).then_inc(folded_y, 1)

            def fold_columns(n, j, peeled):
                i = j % 2
                dve.wait_ge(rows_low, n + 1)
                dve.wait_ge(high_copied, n + 1)
                if not peeled:
                    dve.wait_ge(cols_done, n - 1)
                a, b = rows_ps[i][0][:, 0:2 * U], high[:, i]
                for k, op in ((0, ALU.add), (1, ALU.subtract)):
                    ins = nc.vector.tensor_tensor(
                        fold_x[:, i, 2 * k:2 * k + 2].rearrange("p a u -> p (a u)"), a, b, op)
                ins.then_inc(folded_x, 1)

            def combine(n, j, peeled):
                i = j % 2
                dve.wait_ge(second_copied, n + 1)
                if not peeled:
                    dve.wait_ge(squared, n - 1)
                a, b = cols_ps[i][0:V, 0:U], second[:, i]
                nc.vector.tensor_tensor(parts[:, i, 0], a, b, ALU.subtract)
                nc.vector.tensor_tensor(parts[:, i, 1], a, b, ALU.add).then_inc(parts_done, 1)

            def steps(base, peeled, last):
                for j in range(XB):
                    if not (last and j == XB - 1):
                        fold_rows(base + j + 1, j + 1, peeled and j + 1 < 2)
                    fold_columns(base + j, j, peeled and j < 2)
                    if not (peeled and j == 0):
                        combine(base + j - 1, j - 1, peeled and j - 1 < 2)

            fold_rows(0, 0, True)
            steps(0, True, False)
            with dve.Fori(XB, IMAGES - XB, XB) as base:
                steps(base, False, False)
            steps(IMAGES - XB, False, True)
            combine(IMAGES - 1, XB - 1, False)

        @block.scalar
        def _(act):
            for m in range(LB):
                i = m % PRE
                act.wait_ge(pre_done, m + 1)
                if m >= PRE:
                    act.wait_ge(pre_out[i], 32 * (m // PRE))
                nc.scalar.copy(pre_o[:, i].rearrange("p a u -> p (a u)"), pre_ps[m % 2][:, 0:2 * U])\
                    .then_inc(pre_copied, 1)

            def copy_high(n, j, peeled):
                i = j % 2
                act.wait_ge(rows_high, n + 1)
                if not peeled:
                    act.wait_ge(folded_x, n - 1)
                nc.scalar.copy(high[:, i], rows_ps[i][1][:, 0:2 * U]).then_inc(high_copied, 1)

            def copy_second(n, j, peeled):
                i = j % 2
                act.wait_ge(cols_done, n + 1)
                if not peeled:
                    act.wait_ge(parts_done, n - 1)
                src = cols_ps[i][0:V, U:2 * U].rearrange("p (t v) -> p t v", t=2)
                nc.scalar.copy(second[:, i].rearrange("p (t v) -> p t v", t=2), src[:, ::-1])\
                    .then_inc(second_copied, 1)

            def square(n, j, peeled):
                i = j % 2
                act.wait_ge(parts_done, n + 1)
                if not peeled:
                    act.wait_ge(added, n - 1)
                nc.scalar.activation(squares[:, i].rearrange("p w u -> p (w u)"),
                                     parts[:, i].rearrange("p w u -> p (w u)"), ACT.Square)\
                    .then_inc(squared, 1)

            def root(n, j, at):
                dst = mags[0:V, :, bass.ds(at, 1)] if not isinstance(at, int) else mags[0:V, :, at:at + 1]
                nc.scalar.activation(dst.rearrange("p r a -> p (r a)"), power2[:, j % 2], ACT.Sqrt)\
                    .then_inc(rooted, 1)

            def steps(base, peeled, entry=None, at=None):
                for j in range(XB):
                    if not (peeled and j < 2):
                        act.wait_ge(added, base + j - 1)
                    copy_high(base + j, j, peeled and j < 2)
                    if not (peeled and j < 2):
                        if entry is not None and j == 2 and entry >= 2:
                            act.wait_ge(stage_out[entry % 2], 16 * PARTS * (entry // 2))
                        root(base + j - 2, j - 2, at(j - 2))
                    if not (peeled and j == 0):
                        copy_second(base + j - 1, j - 1, peeled and j - 1 < 2)
                        square(base + j - 1, j - 1, peeled and j - 1 < 2)

            for s in range(STAGES):
                first = s * STAGE
                place = lambda j, f=first: (f + j) % (2 * STAGE)
                steps(first, s == 0, s, place)
                with act.Fori(1, STEPS) as k:
                    off = k * XB + (s % 2) * STAGE
                    steps(k * XB + first, False, None, lambda j, o=off: o + j)
            n = IMAGES
            act.wait_ge(added, n - 1)
            root(n - 2, 0, (n - 2) % (2 * STAGE))
            copy_second(n - 1, 1, False)
            square(n - 1, 1, False)
            act.wait_ge(added, n)
            root(n - 1, 1, (n - 1) % (2 * STAGE))

        @block.gpsimd
        def _(pool):
            def add(n, j, peeled):
                i = j % 2
                pool.wait_ge(squared, n + 1)
                if not peeled:
                    pool.wait_ge(rooted, n - 1)
                ins = nc.gpsimd.tensor_tensor(power2[:, i].rearrange("p (w v) -> p w v", w=2),
                                              squares[:, i, :, 0:V], squares[:, i, ::-1, V:U], ALU.add)
                ins.then_inc(added, 1)

            for j in range(XB):
                add(j, j, j < 2)
            with pool.Fori(XB, IMAGES, XB) as base:
                for j in range(XB):
                    add(base + j, j, False)


GB = 16
NBG = B // GB
GROUPS = 2 * NBG
HS = HH * S
GC = GB * S
QP = 32
QI = P // QP
PAIRS = BINS // 2
SLICES = 3
SJ = JC // SLICES


def head_masks():
    f, r = np.arange(EH) // HD, np.arange(HS) // S
    of_head = (f[:, None] == np.arange(HH)).astype(np.float32)
    feat_feat = (f[:, None] == f).astype(np.float32)
    row_feat = (r[:, None] == f).astype(np.float32)
    return of_head, feat_feat, row_feat


def token_attention_phase(nc, d, scratch, weight, rows, ident, tables, h1, logits):
    with ExitStack() as ctx:
        sb = lambda n, s, t=F32: ctx.enter_context(nc.sbuf_tensor(n, s, t))
        sem = lambda n: ctx.enter_context(nc.semaphore(n))
        gathered = sb("gathered", [P, JC, 2 * IMAGES])
        rows_now = sb("rows_now", [P, 2, 2 * JC], I32)
        code = sb("code", [EH, 2, S])
        tok_bias = sb("tok_bias", [EH, 2])
        cls = sb("cls", [EH, 2])
        offset = sb("offset", [EH, 2, S])
        pair_rows = sb("pair_rows", [P, E])
        tokens = sb("tokens", [EH, 2, S, B])
        down = sb("down", [EH, 3, 2, RANK])
        up = sb("up", [RANK, 3, E])
        bias = sb("bias", [EH, 3, 2])
        m_u = sb("m_u", [RM, EH])
        m_v = sb("m_v", [RM, EH])
        of_head = sb("of_head", [EH, HH])
        feat_feat = sb("feat_feat", [EH, EH])
        row_feat = sb("row_feat", [HS, EH])
        mixer = sb("mixer", [EH, EH])
        low_qk = sb("low_qk", [RANK, 2, P])
        low_v = sb("low_v", [RANK, S, B])
        q = sb("q", [EH, 2, P])
        qm = sb("qm", [EH, 2, B * S + QP])
        k = sb("k", [EH, 2, B, S])
        k_heads = sb("k_heads", [EH, 2, GB, HH, S])
        low_heads = sb("low_heads", [RANK, 2, GB, HH, S])
        v_heads = sb("v_heads", [HS, 2, GB, 2, EH])
        top = sb("top", [P, GROUPS, GB // QI, HH])
        total = sb("total", [P, GROUPS, GB // QI, HH])
        probs = sb("head_probs", [P, 2, GB // QI, HH, S])
        probs_t = sb("head_probs_t", [HS, 2, GB // QI, QI, QP])
        ones = sb("ones", [EH, EH])
        sq = sb("sq", [EH, 2, GC])
        rstd = sb("rstd", [EH, NBG, GC])
        zero = sb("zero", [P, E])
        bank = [ctx.enter_context(nc.psum_tensor(f"bank{i}", [P, 512], F32)) for i in range(8)]
        (weights_in, tables_in, zero_set, pad_set, ones_set, rows_copied, gathers_begun, chunk_used, offset_done,
         pair_copied, turn_mm, tokens_done, mixer_mm, mixer_done, low_mm, low_qk_copied, low_v_copied, up_mm,
         up_copied, qm_mm, qm_copied, k_spread, low_spread, v_mm, v_copied, score_mm, top_done, shifted,
         exp_done, summed, inverted, weights_done, turned_mm, probs_copied, out_mm, residual_done, mean_mm,
         centred, sq_done, var_mm, var_read, rooted, rstd_done, normed, logits_mm, logits_done) = [
             sem(n) for n in (
                 "weights_in tables_in zero_set pad_set ones_set rows_copied gathers_begun chunk_used offset_done "
                 "pair_copied turn_mm tokens_done mixer_mm mixer_done low_mm low_qk_copied low_v_copied up_mm up_copied "
                 "qm_mm qm_copied k_spread low_spread v_mm v_copied score_mm top_done shifted exp_done summed inverted "
                 "weights_done turned_mm probs_copied out_mm residual_done mean_mm centred sq_done var_mm var_read rooted "
                 "rstd_done normed logits_mm logits_done").split()]
        value_bank = (bank[0], bank[1], bank[6])
        chunk_in = [sem(f"chunk_in{j}") for j in range(JC)]
        loads = [(code, "code"), (tok_bias, "tok_b"), (cls, "cls"), (down, "down"), (up, "up"),
                 (bias, "bias"), (m_u, "m_u"), (m_v, "m_v"), (of_head, "of_head"),
                 (feat_feat, "feat_feat"), (row_feat, "row_feat")]
        width = lambda c: B if c == 0 else P
        at = lambda c: slice(0, 1) if c == 0 else slice(2 * c - 1, 2 * c + 1)
        flat = lambda a: a.rearrange("p s b -> p (s b)")
        wide = lambda a: a.rearrange("p (s b) -> p s b", b=B)
        images = lambda bg: slice(bg * GB, (bg + 1) * GB)
        of = lambda bg: slice(bg * GC, (bg + 1) * GC)
        block = ctx.enter_context(nc.Block())

        @block.sync
        def _(sp):
            for dst, src in loads:
                sp.dma_start(dst[:], d[src]).then_inc(weights_in, 16)
            for name, dst in tables.items():
                sp.dma_start(dst[:], d[name]).then_inc(tables_in, 16)
            sp.wait_ge(zero_set, 1)
            sp.dma_start(scratch["slots"].rearrange("(n p) e -> p n e", p=P),
                         zero[:].rearrange("p (n e) -> p n e", n=1).to_broadcast([P, NT, E]))\
                .then_inc(tables_in, 16)
            sp.wait_ge(tables_in, 16 * (len(tables) + 1))

        @block.gpsimd
        def _(pool):
            def pair(p, q, peeled):
                pool.wait_ge(rows_copied, p + 1)
                pool.sem_inc(gathers_begun, 1)
                for c in range(SLICES):
                    if not peeled:
                        pool.wait_ge(chunk_used, (p - 1) * JC + (c + 1) * SJ)
                        pool.sem_inc(gathers_begun, 1)
                    for j in range(c * SJ, (c + 1) * SJ):
                        for n in range(2):
                            at_row = rows_now[:, q, 2 * j + n:2 * j + n + 1]
                            nc.gpsimd.indirect_dma_start(
                                gathered[:, j, n * IMAGES:(n + 1) * IMAGES], None, scratch["power"],
                                bass.IndirectOffsetOnAxis(ap=at_row, axis=0)).then_inc(chunk_in[j], 16)

            pair(0, 0, True)
            pair(1, 1, False)
            with pool.Fori(1, PAIRS // 2) as step:
                for q in range(2):
                    pair(step * 2 + q, q, False)

        @block.tensor
        def _(pe):
            def multiply(p, j, acc):
                pe.wait_ge(chunk_in[j], 32 * p + 32)
                by_channel = gathered[:, j].rearrange("p (m c) -> p c m", c=C)
                for c in range(C):
                    mm = nc.tensor.matmul(acc, by_channel[:, c], weight[:, j, c], start=j == 0 and c == 0,
                                          stop=j == JC - 1 and c == C - 1)
                mm.then_inc(chunk_used, 1)
                return mm

            def turn(c):
                pe.wait_ge(pair_copied, c)
                for h in range(2):
                    mm = nc.tensor.matmul(bank[1][0:EH, h * P:(h + 1) * P], pair_rows[:, h * EH:(h + 1) * EH],
                                          ident[:], start=True, stop=True)
                mm.then_inc(turn_mm, 1)

            def low(c, first):
                n = width(0) if first else P
                pe.wait_ge(tokens_done, c + 1)
                if not first:
                    pe.wait_ge(low_v_copied, c)
                for x in range(3):
                    for h in range(2):
                        src = flat(tokens[:, h, 0:1]) if first else \
                            tokens[:, h].rearrange("p s b -> p (s b)")[:, bass.ds(c * P - B, P)]
                        mm = nc.tensor.matmul(bank[2][0:RANK, x * P:x * P + n], down[:, x, h], src,
                                              start=h == 0, stop=h == 1)
                mm.then_inc(low_mm, 1)

            def up_both(c, first):
                n = width(0) if first else P
                pe.wait_ge(low_qk_copied, c + 1)
                if not first:
                    pe.wait_ge(up_copied, c)
                for x in range(2):
                    for h in range(2):
                        mm = nc.tensor.matmul(bank[3][0:EH, (2 * x + h) * P:(2 * x + h) * P + n],
                                              up[:, x, h * EH:(h + 1) * EH], low_qk[:, x, 0:n],
                                              start=True, stop=True)
                mm.then_inc(up_mm, 1)

            def mix(c, first):
                n = width(0) if first else P
                pe.wait_ge(up_copied, c + 1)
                if not first:
                    pe.wait_ge(qm_copied, c)
                for h in range(2):
                    mm = nc.tensor.matmul(bank[4][0:EH, h * P:h * P + n], mixer[:], q[:, h, 0:n],
                                          start=True, stop=True)
                mm.then_inc(qm_mm, 1)

            def pair(p, first):
                acc = bank[0][:, 0:E]
                if not first:
                    pe.wait_ge(pair_copied, p)
                for j in range(JC):
                    mm = multiply(p, j, acc)
                    if j == 2 and not first:
                        turn(p)
                    if j == 5:
                        low(p, first)
                    if j == 8:
                        up_both(p, first)
                    if j == 11:
                        mix(p, first)

            pe.wait_ge(weights_in, 16 * len(loads))
            nc.tensor.matmul(bank[5][0:EH, 0:EH], m_u[:], m_v[:], start=True, stop=True).then_inc(mixer_mm, 1)
            pe.wait_ge(mixer_done, 1)
            pair(0, True)
            with pe.Fori(1, PAIRS) as p:
                pair(p, False)
            turn(PAIRS)
            low(PAIRS, False)
            up_both(PAIRS, False)
            mix(PAIRS, False)

            def values(v):
                bg = v // 2
                pe.wait_ge(low_spread, bg + 1)
                for i in range(v % 2 * (GB // 2), (v % 2 + 1) * (GB // 2)):
                    n = bg * (GB // 2) + i // 2
                    if i % 2 == 0 and n >= 3:
                        pe.wait_ge(v_copied, n - 2)
                    mm = nc.tensor.matmul(value_bank[n % 3][0:HS, i % 2 * E:(i % 2 + 1) * E],
                                          low_heads[:, bg % 2, i].rearrange("p h s -> p (h s)"), up[:, 2],
                                          start=True, stop=True)
                    if i % 2:
                        mm.then_inc(v_mm, 1)

            def scores(g):
                bg, h = divmod(g, 2)
                pe.wait_ge(k_spread, g + 1)
                if g:
                    pe.wait_ge(shifted, g)
                for i in range(GB):
                    at_q, at_k = i % QI * QP, i // QI * HS
                    mm = nc.tensor.matmul(bank[2][at_q:at_q + QP, at_k:at_k + HS],
                                          qm[:, h, (bg * GB + i) * S:(bg * GB + i) * S + QP],
                                          k_heads[:, g % 2, i].rearrange("p h s -> p (h s)"),
                                          start=True, stop=True)
                mm.then_inc(score_mm, 1)

            def turned(g):
                pe.wait_ge(weights_done, g + 1)
                if g:
                    pe.wait_ge(probs_copied, g)
                for c in range(GB // QI):
                    mm = nc.tensor.matmul(bank[3][0:HS, c * P:(c + 1) * P],
                                          probs[:, g % 2, c].rearrange("p h s -> p (h s)"), ident[:],
                                          start=True, stop=True)
                mm.then_inc(turned_mm, 1)

            def weighted(g):
                bg, h = divmod(g, 2)
                pe.wait_ge(v_copied, (bg + 1) * (GB // 2))
                pe.wait_ge(probs_copied, g + 1)
                if g:
                    pe.wait_ge(residual_done, g)
                for i in range(GB):
                    mm = nc.tensor.matmul(bank[4][0:EH, i * S:(i + 1) * S], v_heads[:, bg % 2, i, h],
                                          probs_t[:, g % 2, i // QI, i % QI, 0:S], start=True, stop=True)
                mm.then_inc(out_mm, 1)

            def mean(bg):
                pe.wait_ge(ones_set, 1)
                pe.wait_ge(residual_done, 2 * bg + 2)
                if bg:
                    pe.wait_ge(var_read, bg)
                for h in range(2):
                    mm = nc.tensor.matmul(bank[7][0:EH, 0:GC], ones[:],
                                          tokens[:, h, :, images(bg)].rearrange("p s b -> p b s"),
                                          start=h == 0, stop=h == 1)
                mm.then_inc(mean_mm, 1)

            def variance(bg):
                pe.wait_ge(centred, bg + 1)
                pe.wait_ge(sq_done, bg + 1)
                for h in range(2):
                    mm = nc.tensor.matmul(bank[7][0:EH, 0:GC], ones[:], sq[:, h],
                                          start=h == 0, stop=h == 1)
                mm.then_inc(var_mm, 1)

            def route(lo, hi):
                pe.wait_ge(normed, -(-min(hi * P, T) // GC))
                for t in range(lo, hi):
                    for h in range(2):
                        mm = nc.tensor.matmul(bank[5][:, t * EXPERTS:(t + 1) * EXPERTS],
                                              h1[:, h, t * P:(t + 1) * P], tables["w_router"][:, h],
                                              start=h == 0, stop=h == 1)
                mm.then_inc(logits_mm, 1)

            pe.wait_ge(pad_set, 2)
            pe.wait_ge(qm_copied, PAIRS + 1)
            scores(0)
            values(0)
            for g in range(GROUPS + 3):
                if g + 1 < GROUPS:
                    scores(g + 1)
                    values(g + 1)
                if g < GROUPS:
                    turned(g)
                if 1 <= g <= GROUPS:
                    weighted(g - 1)
                if g >= 3 and g % 2:
                    mean((g - 3) // 2)
                if g == GROUPS + 1:
                    pe.wait_ge(tables_in, 16 * (len(tables) + 1))
                    route(0, GC // P)
                if g >= 4 and g % 2 == 0:
                    variance((g - 4) // 2)
            for bg in range(1, NBG):
                route(bg * GC // P, (bg + 1) * GC // P if bg < NBG - 1 else TILES)

        @block.scalar
        def _(act):
            def square(bg):
                act.wait_ge(centred, bg + 1)
                if bg:
                    act.wait_ge(var_mm, bg)
                for h in range(2):
                    ins = nc.scalar.activation(sq[:, h], h1[:, h, of(bg)], ACT.Square)
                ins.then_inc(sq_done, 1)

            for c in range(PAIRS + 1):
                if c:
                    act.wait_ge(chunk_used, c * JC)
                    if c >= 2:
                        act.wait_ge(turn_mm, c - 1)
                    nc.scalar.copy(pair_rows[:], bank[0][:, 0:E]).then_inc(pair_copied, 1)
                n = width(c)
                act.wait_ge(low_mm, c + 1)
                if c:
                    act.wait_ge(up_mm, c)
                nc.scalar.copy(low_qk[:, :, 0:n],
                               bank[2][0:RANK, 0:2 * P].rearrange("p (x n) -> p x n", x=2)[:, :, 0:n])\
                    .then_inc(low_qk_copied, 1)
            def spread_low(bg):
                if bg >= 2:
                    act.wait_ge(v_mm, (bg - 1) * (GB // 2))
                src = low_v[:, :, images(bg)].rearrange("p (o s) b -> p b o s", o=1)
                nc.scalar.copy(low_heads[:, bg % 2], src.to_broadcast([RANK, GB, HH, S]))\
                    .then_inc(low_spread, 1)

            def exp(g):
                act.wait_ge(shifted, g + 1)
                x = probs[:, g % 2].rearrange("p c h s -> p (c h s)")
                nc.scalar.activation(x, x, ACT.Exp).then_inc(exp_done, 1)

            act.wait_ge(low_v_copied, PAIRS + 1)
            spread_low(0)
            exp(0)
            for g in range(GROUPS):
                if g + 1 < GROUPS:
                    exp(g + 1)
                act.wait_ge(turned_mm, g + 1)
                if g >= 2:
                    act.wait_ge(out_mm, g - 1)
                nc.scalar.copy(probs_t[:, g % 2].rearrange("p c a q -> p (c a q)"), bank[3][0:HS, :])\
                    .then_inc(probs_copied, 1)
                if g % 2 == 0 and g // 2 + 1 < NBG:
                    spread_low(g // 2 + 1)
                if g >= 4 and g % 2 == 0:
                    square((g - 4) // 2)
            square(NBG - 2)
            def root(bg):
                act.wait_ge(var_read, bg + 1)
                nc.scalar.activation(rstd[:, bg], rstd[:, bg], ACT.Sqrt).then_inc(rooted, 1)

            for bg in range(NBG - 1):
                root(bg)
            square(NBG - 1)
            root(NBG - 1)

        @block.vector
        def _(dve):
            V_ = nc.vector

            def copy_scratch_rows(p):
                if p >= 2:
                    dve.wait_ge(chunk_used, (p - 1) * JC)
                V_.tensor_copy(rows_now[:, p % 2], rows[:, p * 2 * JC:(p + 1) * 2 * JC]).then_inc(rows_copied, 1)

            copy_scratch_rows(0)
            copy_scratch_rows(1)
            V_.memset(ones[:], 1.0 / E).then_inc(ones_set, 1)
            V_.memset(h1[:, :, T:], 0.0).then_inc(pad_set, 1)
            V_.memset(zero[:], 0.0).then_inc(zero_set, 1)
            V_.memset(qm[:, :, B * S:], 0.0).then_inc(pad_set, 1)
            by_position = lambda a: a.rearrange("p (b s) -> p s b", s=S)
            dve.wait_ge(weights_in, 16 * len(loads))
            for h in range(2):
                V_.tensor_scalar(offset[:, h, 1:S], code[:, h, 1:S], tok_bias[:, h:h + 1], None, ALU.add)
                ins = V_.tensor_scalar(offset[:, h, 0:1], code[:, h, 0:1], cls[:, h:h + 1], None, ALU.add)
            ins.then_inc(offset_done, 1)
            dve.wait_ge(mixer_mm, 1)
            V_.scalar_tensor_tensor(out=mixer[:], in0=bank[5][0:EH, 0:EH], scalar=float(HD) ** -0.5,
                                    in1=feat_feat[:], op0=ALU.mult, op1=ALU.mult).then_inc(mixer_done, 1)
            dve.wait_ge(offset_done, 1)
            V_.tensor_copy(tokens[:, :, 0, :], offset[:, :, 0:1].to_broadcast([EH, 2, B])).then_inc(tokens_done, 1)
            for c in range(PAIRS + 1):
                n = width(c)
                if 1 <= c < PAIRS - 1:
                    copy_scratch_rows(c + 1)
                if c:
                    dve.wait_ge(turn_mm, c)
                    for h in range(2):
                        o = offset[:, h, at(c)].rearrange("p (s o) -> p s o", o=1).to_broadcast([EH, 2, B])
                        ins = V_.tensor_tensor(tokens[:, h, at(c)], wide(bank[1][0:EH, h * P:(h + 1) * P]), o,
                                               ALU.add)
                    ins.then_inc(tokens_done, 1)
                dve.wait_ge(low_qk_copied, c + 1)
                V_.tensor_copy(low_v[:, at(c)], wide(bank[2][0:RANK, 2 * P:2 * P + n])).then_inc(low_v_copied, 1)
                dve.wait_ge(up_mm, c + 1)
                if c:
                    dve.wait_ge(qm_mm, c)
                for h in range(2):
                    V_.tensor_scalar(q[:, h, 0:n], bank[3][0:EH, h * P:h * P + n], bias[:, 0, h:h + 1], None,
                                     ALU.add)
                    ins = V_.tensor_scalar(k[:, h].rearrange("p b s -> p s b")[:, at(c)],
                                           wide(bank[3][0:EH, (2 + h) * P:(2 + h) * P + n]),
                                           bias[:, 1, h:h + 1], None, ALU.add)
                ins.then_inc(up_copied, 1)
                dve.wait_ge(qm_mm, c + 1)
                for h in range(2):
                    ins = V_.tensor_copy(by_position(qm[:, h, 0:B * S])[:, at(c)],
                                         wide(bank[4][0:EH, h * P:h * P + n]))
                ins.then_inc(qm_copied, 1)

            by_head = of_head[:].rearrange("p (o h q) -> p o h q", o=1, q=1).to_broadcast([EH, GB, HH, S])

            def spread_k(g):
                bg, h = divmod(g, 2)
                if g >= 2:
                    dve.wait_ge(score_mm, g - 1)
                v = k[:, h, images(bg)].rearrange("p b (o s) -> p b o s", o=1)
                V_.tensor_tensor(k_heads[:, g % 2], v.to_broadcast([EH, GB, HH, S]), by_head, ALU.mult)\
                    .then_inc(k_spread, 1)

            per_head = [P, GB // QI, HH, S]
            along = lambda a: a.rearrange("p c (h o) -> p c h o", o=1).to_broadcast(per_head)

            def less_top(g):
                dve.wait_ge(score_mm, g + 1)
                x = bank[2][:, 0:GB // QI * HS].rearrange("p (c h s) -> p c h s", c=GB // QI, h=HH)
                V_.tensor_reduce(top[:, g], x, AXX, ALU.max).then_inc(top_done, 1)
                dve.wait_ge(top_done, g + 1)
                if g >= 2:
                    dve.wait_ge(turned_mm, g - 1)
                V_.tensor_tensor(probs[:, g % 2], x, along(top[:, g]), ALU.subtract).then_inc(shifted, 1)

            def weights(g):
                dve.wait_ge(exp_done, g + 1)
                V_.tensor_reduce(total[:, g], probs[:, g % 2], AXX, ALU.add).then_inc(summed, 1)
                dve.wait_ge(summed, g + 1)
                V_.reciprocal(total[:, g], total[:, g]).then_inc(inverted, 1)
                dve.wait_ge(inverted, g + 1)
                V_.tensor_tensor(probs[:, g % 2], probs[:, g % 2], along(total[:, g]), ALU.mult)\
                    .then_inc(weights_done, 1)

            def value_rows(v):
                bg = v // 2
                for i in range(v % 2 * (GB // 4), (v % 2 + 1) * (GB // 4)):
                    n = bg * (GB // 2) + i
                    dve.wait_ge(v_mm, n + 1)
                    if i == 0 and bg >= 2:
                        dve.wait_ge(out_mm, 2 * bg - 2)
                    mask = row_feat[:].rearrange("p (o f) -> p o f", o=1).to_broadcast([HS, 4, EH])
                    V_.tensor_tensor(v_heads[:, bg % 2, 2 * i:2 * i + 2].rearrange("p b h f -> p (b h) f"),
                                     value_bank[n % 3][0:HS, 0:2 * E].rearrange("p (a f) -> p a f", a=4),
                                     mask, ALU.mult).then_inc(v_copied, 1)

            def residual(g):
                bg, h = divmod(g, 2)
                dve.wait_ge(out_mm, g + 1)
                t = tokens[:, h, :, images(bg)].rearrange("p s b -> p b s")
                V_.scalar_tensor_tensor(out=t, in0=bank[4][0:EH, 0:GC].rearrange("p (b s) -> p b s", s=S),
                                        scalar=bias[:, 2, h:h + 1], in1=t, op0=ALU.add, op1=ALU.add)\
                    .then_inc(residual_done, 1)

            def centre(bg):
                dve.wait_ge(mean_mm, bg + 1)
                dve.wait_ge(residual_done, 2 * bg + 2)
                for h in range(2):
                    ins = V_.tensor_tensor(h1[:, h, of(bg)].rearrange("p (b s) -> p b s", s=S),
                                           tokens[:, h, :, images(bg)].rearrange("p s b -> p b s"),
                                           bank[7][0:EH, 0:GC].rearrange("p (b s) -> p b s", s=S), ALU.subtract)
                ins.then_inc(centred, 1)

            def variance(bg):
                dve.wait_ge(var_mm, bg + 1)
                V_.tensor_scalar(rstd[:, bg], bank[7][0:EH, 0:GC], EPS, None, ALU.add).then_inc(var_read, 1)

            def norm(bg):
                dve.wait_ge(rooted, bg + 1)
                dve.wait_ge(centred, bg + 1)
                V_.reciprocal(rstd[:, bg], rstd[:, bg]).then_inc(rstd_done, 1)
                dve.wait_ge(rstd_done, bg + 1)
                for h in range(2):
                    x = h1[:, h, of(bg)]
                    ins = V_.tensor_tensor(x, x, rstd[:, bg], ALU.mult)
                ins.then_inc(normed, 1)

            dve.wait_ge(qm_copied, PAIRS + 1)
            spread_k(0)
            spread_k(1)
            less_top(0)
            value_rows(0)
            weights(0)
            for g in range(GROUPS + 3):
                if 2 <= g < GROUPS + 2:
                    residual(g - 2)
                if g >= 4 and g % 2 == 0:
                    centre((g - 4) // 2)
                if g >= 5 and g % 2:
                    variance((g - 5) // 2)
                if g == GROUPS + 1:
                    norm(0)
                if g + 1 < GROUPS:
                    less_top(g + 1)
                    value_rows(g + 1)
                if g + 2 < GROUPS:
                    spread_k(g + 2)
                if g + 1 < GROUPS:
                    weights(g + 1)
            for bg in range(1, NBG):
                if bg == NBG - 1:
                    variance(bg)
                norm(bg)
            dve.wait_ge(logits_mm, NBG)
            V_.tensor_tensor(logits[:], bank[5][:, 0:TILES * EXPERTS].rearrange("p (t e) -> p t e", e=EXPERTS),
                             tables["b_router"][:], ALU.add).then_inc(logits_done, 1)
            dve.wait_ge(logits_done, 1)


NT = (2 * T - EXPERTS) // P + EXPERTS
SLOTS = NT * P
TG = 3


def routing_tables():
    before = np.triu(np.ones((P, P), np.float32), 1)
    count = np.arange(EXPERTS, dtype=np.float32)
    rows = {
        "counts": np.broadcast_to(count, (TILES, EXPERTS)),
        "limits": np.broadcast_to(P * np.arange(TILES, dtype=np.float32), (EXPERTS, TILES)),
        "upto": np.tril(np.ones((EXPERTS, EXPERTS), np.float32)),
        "tile_no": np.broadcast_to(np.arange(NT, dtype=np.float32)[:, None], (NT, EXPERTS)),
    }
    out = {n: np.ascontiguousarray(np.broadcast_to(a, (P,) + a.shape)) for n, a in rows.items()}
    valid = (np.arange(TILES)[None] * P + np.arange(P)[:, None] < T).astype(np.float32)
    out["valid"] = np.ascontiguousarray(np.repeat(valid[:, :, None], EXPERTS, 2))
    out["before"] = before
    return out


def expert_tables():
    return {
        "w_router": [EH, 2, EXPERTS], "before": [P, P], "b_proj": [EXPERTS, E],
        "b_router": [P, TILES, EXPERTS],
        "counts": [P, TILES, EXPERTS],
        "limits": [P, EXPERTS, TILES],
        "upto": [P, EXPERTS, EXPERTS],
        "tile_no": [P, NT, EXPERTS],
        "valid": [P, TILES, EXPERTS],
    }


def expert_phase(nc, d, h1, logits, ident, tables, scratch, rows, out):
    XT = 4
    assert NT % XT == 0 and TILES % TG == 0
    tile_rows = [min(P, T - t * P) for t in range(TILES)]
    RT = [P, TILES, EXPERTS]
    with ExitStack() as ctx:
        sb = lambda n, s, t=F32: ctx.enter_context(nc.sbuf_tensor(n, s, t))
        sem = lambda n: ctx.enter_context(nc.semaphore(n))
        all_ones = sb("all_ones", [P, P])
        before, b_proj = tables["before"], tables["b_proj"]
        counts, limits, upto, tile_no, valid = [tables[n] for n in "counts limits upto tile_no valid".split()]
        acc = sb("acc", [P, TILES, E])
        square = sb("square", [P, TG, E])
        results = sb("results", [P, TILES, 2, E])
        (probs, far, best_one, next_one, rest, picked, gate, slot_of, of_slot) = [sb(n, RT) for n in (
            "probs far best_one next_one rest picked gate slot_of of_slot").split()]
        ahead = sb("ahead", [P, TILES + 1, EXPERTS])
        need = sb("need", [P, EXPERTS, TILES])
        tri = sb("tri", [P, EXPERTS, EXPERTS])
        past = sb("past", [P, NT, EXPERTS])
        per_expert = sb("per_expert", [P, 3, EXPERTS])
        gate_t = sb("gate_t", [EXPERTS, TILES, P])
        stat = sb("stat", [P, 10, TILES])
        slots = sb("slots", [P, 2, TILES], I32)
        owner_f = sb("owner_f", [P, NT])
        owner = sb("owner", [P, NT], I32)
        w_fc = sb("w_fc", [EH, XT, 2, FF])
        w_proj = sb("w_proj", [P, XT, FC, E])
        b_fc = sb("b_fc", [P, XT, FC])
        slot_rows = sb("slot_rows", [P, XT, E])
        features = sb("features", [EH, 2, 2, P])
        hidden = sb("hidden", [P, 2, FC, P])
        result = sb("result", [P, XT, E])
        bank = [ctx.enter_context(nc.psum_tensor(f"ebank{i}", [P, 512], F32)) for i in range(8)]
        (rows_mm, rows_copied, exp_in, exp_done, routed, rank_mm, placed,
         turn_mm, turned, base_mm, based, scattered, feat_mm, feat_copied, fc_mm, fc_act,
         proj_mm, proj_copied, chain, std_in, std_done, out_ready, out_left, ones_set, added) = [
             sem("e_" + n) for n in (
                 "rows_mm rows_copied exp_in exp_done routed rank_mm placed "
                 "turn_mm turned base_mm based scattered feat_mm feat_copied fc_mm fc_act "
                 "proj_mm proj_copied chain std_in std_done out_ready out_left ones_set added").split()]
        w_in = [sem(f"e_w_in{i}") for i in range(XT)]
        x_in = [sem(f"e_x_in{i}") for i in range(XT)]
        y_out = [sem(f"e_y_out{i}") for i in range(XT)]
        y_in = [sem(f"e_y_in{i}") for i in range(TILES // TG)]
        block = ctx.enter_context(nc.Block())

        @block.sync
        def _(sp):
            def load(j, i):
                at = bass.ds(j, 1) if not isinstance(j, int) else slice(j, j + 1)
                e = sp.value_load(owner[0:1, at], min_val=0, max_val=EXPERTS - 1)
                one = bass.ds(e, 1)
                sp.dma_start(w_fc[:, i], d["w_fc"][one].rearrange("a p h f -> (a p) h f")).then_inc(w_in[i], 16)
                sp.dma_start(b_fc[:, i], d["b_fc"][one].rearrange("a p f -> (a p) f")).then_inc(w_in[i], 16)
                sp.dma_start(w_proj[:, i], d["w_proj"][one].rearrange("a p c f -> (a p) c f"))\
                    .then_inc(w_in[i], 16)

            def load_rows(j, i):
                at = bass.ds(j, 1) if not isinstance(j, int) else slice(j, j + 1)
                src = scratch["slots"].rearrange("(n p) e -> n p e", p=P)[at]
                sp.dma_start(slot_rows[:, i], src.rearrange("a p e -> (a p) e")).then_inc(x_in[i], 16)

            def store(j, i):
                at = bass.ds(j, 1) if not isinstance(j, int) else slice(j, j + 1)
                dst = scratch["results"].rearrange("(n p) e -> n p e", p=P)[at]
                sp.dma_start(dst.rearrange("a p e -> (a p) e"), result[:, i]).then_inc(y_out[i], 16)

            sp.wait_ge(placed, 1)
            for i in range(XT):
                load(i, i)
            sp.wait_ge(scattered, 32 * TILES)
            for i in range(XT):
                load_rows(i, i)
            with sp.Fori(0, NT // XT - 1) as k:
                for i in range(XT):
                    j = sp.snap(k * XT + i)
                    done = sp.snap(j + 1)
                    following = sp.snap(j + XT)
                    sp.wait_ge(proj_mm, done)
                    load_rows(following, i)
                    load(following, i)
                    sp.wait_ge(proj_copied, done)
                    store(j, i)
            for i in range(XT):
                sp.wait_ge(proj_copied, NT - XT + i + 1)
                store(NT - XT + i, i)
            rows_out = out.rearrange("b s e -> (b s) e")
            for t in range(TILES):
                if t % TG == 0:
                    sp.wait_ge(out_ready, t // TG + 1)
                sp.dma_start(rows_out[t * P:t * P + tile_rows[t]], acc[0:tile_rows[t], t]).then_inc(out_left, 16)
            sp.wait_ge(out_left, 16 * TILES)

        @block.gpsimd
        def _(pool):
            pool.wait_ge(placed, 1)
            for t in range(TILES):
                r = tile_rows[t]
                pool.wait_ge(rows_copied, t + 1)
                for k in range(2):
                    nc.gpsimd.indirect_dma_start(
                        scratch["slots"], bass.IndirectOffsetOnAxis(ap=slots[0:r, k, t:t + 1], axis=0),
                        rows[0:r, t], None).then_inc(scattered, 16)
            for i in range(XT):
                pool.wait_ge(y_out[i], 16 * (NT // XT))
            for t in range(TILES):
                r = tile_rows[t]
                for k in range(2):
                    nc.gpsimd.indirect_dma_start(
                        results[0:r, t, k], None, scratch["results"],
                        bass.IndirectOffsetOnAxis(ap=slots[0:r, k, t:t + 1], axis=0))\
                        .then_inc(y_in[t // TG], 16)

        @block.tensor
        def _(pe):
            for t in range(TILES):
                if t >= 2:
                    pe.wait_ge(rows_copied, t - 1)
                for h in range(2):
                    mm = nc.tensor.matmul(bank[2 + t % 2][:, h * EH:(h + 1) * EH], h1[:, h, t * P:(t + 1) * P],
                                          ident[0:EH, 0:EH], start=True, stop=True)
                mm.then_inc(rows_mm, 1)
            pe.wait_ge(ones_set, 1)
            pe.wait_ge(routed, 1)
            both = picked[:].rearrange("p t e -> p (t e)")
            nc.tensor.matmul(bank[1][:, 0:TILES * EXPERTS], before[:], both, start=True, stop=True)
            nc.tensor.matmul(bank[1][:, 256:256 + TILES * EXPERTS], all_ones[:], both, start=True, stop=True)\
                .then_inc(rank_mm, 1)
            pe.wait_ge(routed, 2)
            for t in range(TILES):
                if t >= 2:
                    pe.wait_ge(turned, t - 1)
                nc.tensor.transpose(bank[4 + t % 2][0:EXPERTS, 0:P], gate[:, t], ident[:]).then_inc(turn_mm, 1)
            for t in range(TILES):
                pe.wait_ge(turned, t + 1)
                if t >= 2:
                    pe.wait_ge(based, t - 1)
                nc.tensor.matmul(bank[6 + t % 2][:, 0:E], gate_t[:, t], b_proj[:], start=True, stop=True)\
                    .then_inc(base_mm, 1)
            pe.wait_ge(based, TILES)

            def turn(j, i, q, peeled):
                pe.wait_ge(x_in[i], 4 * (j - i) + 16)
                if not peeled:
                    pe.wait_ge(feat_copied, j - 1)
                for h in range(2):
                    mm = nc.tensor.matmul(bank[q][0:EH, h * P:(h + 1) * P], slot_rows[:, i, h * EH:(h + 1) * EH],
                                          ident[:], start=True, stop=True)
                mm.then_inc(feat_mm, 1)

            def up(j, i, q, peeled):
                pe.wait_ge(w_in[i], 12 * (j - i) + 48)
                pe.wait_ge(feat_copied, j + 1)
                if not peeled:
                    pe.wait_ge(fc_act, FC * (j - 1))
                for f in range(FC):
                    o = bank[2 + 2 * q + f // 3][:, f % 3 * P:(f % 3 + 1) * P]
                    for h in range(2):
                        mm = nc.tensor.matmul(o, w_fc[:, i, h, f * P:(f + 1) * P], features[:, q, h],
                                              start=h == 0, stop=h == 1)
                    if f % 3 == 2:
                        mm.then_inc(fc_mm, 1)

            def down(j, i, q, peeled):
                pe.wait_ge(fc_act, FC * (j + 1))
                if not peeled:
                    pe.wait_ge(proj_copied, j - 1)
                for f in range(FC):
                    mm = nc.tensor.matmul(bank[6 + q][:, 0:E], hidden[:, q, f], w_proj[:, i, f],
                                          start=f == 0, stop=f == FC - 1)
                mm.then_inc(proj_mm, 1)

            turn(0, 0, 0, True)
            for j in range(1, XT):
                up(j - 1, j - 1, (j - 1) % 2, j <= 2)
                turn(j, j, j % 2, j < 2)
                if j >= 2:
                    down(j - 2, j - 2, j % 2, True)
            with pe.Fori(1, NT // XT) as k:
                for i in range(XT):
                    j = k * XT + i
                    up(j - 1, (i - 1) % XT, (i - 1) % 2, False)
                    turn(j, i, i % 2, False)
                    down(j - 2, (i - 2) % XT, i % 2, False)
            up(NT - 1, XT - 1, 1, False)
            down(NT - 2, XT - 2, 0, False)
            down(NT - 1, XT - 1, 1, False)

        @block.scalar
        def _(act):
            act.wait_ge(exp_in, 1)
            nc.scalar.activation(probs[:], probs[:], ACT.Exp).then_inc(exp_done, 1)

            for t in range(TILES):
                act.wait_ge(rows_mm, t + 1)
                nc.scalar.copy(rows[:, t], bank[2 + t % 2][:, 0:E]).then_inc(rows_copied, 1)

            def gelu(j, i, peeled):
                q = i % 2
                if not peeled:
                    act.wait_ge(proj_mm, j - 1)
                for f in range(FC):
                    if f % 3 == 0:
                        act.wait_ge(fc_mm, 2 * j + f // 3 + 1)
                    nc.scalar.activation(hidden[:, q, f], bank[2 + 2 * q + f // 3][:, f % 3 * P:(f % 3 + 1) * P],
                                         ACT.Gelu_apprx_tanh, bias=b_fc[:, i, f:f + 1]).then_inc(fc_act, 1)

            for i in range(XT):
                gelu(i, i, i < 2)
            with act.Fori(1, NT // XT) as k:
                for i in range(XT):
                    gelu(k * XT + i, i, False)
            for g in range(TILES // TG):
                act.wait_ge(std_in, g + 1)
                v = stat[:, 8, g * TG:(g + 1) * TG]
                nc.scalar.activation(v, v, ACT.Sqrt).then_inc(std_done, 1)

        @block.vector
        def _(dve):
            step = [0]

            def then(ins):
                step[0] += 1
                ins.then_inc(chain, 1)
                dve.wait_ge(chain, step[0])

            def spread(a, n, w):
                return a.rearrange("p (t o) -> p t o", o=1).to_broadcast([P, n, w])

            def repeat(a, n, w):
                return a.rearrange("p (o t) -> p o t", o=1).to_broadcast([P, n, w])

            tok = lambda a: spread(a, TILES, EXPERTS)
            V_ = nc.vector
            V_.memset(all_ones[:], 1.0).then_inc(ones_set, 1)
            then(V_.memset(ahead[:, 0], 0.0))
            then(V_.tensor_reduce(stat[:, 0], logits[:], AXX, ALU.max))
            V_.tensor_tensor(probs[:], logits[:], tok(stat[:, 0]), ALU.subtract).then_inc(exp_in, 1)
            dve.wait_ge(exp_done, 1)
            then(V_.tensor_reduce(stat[:, 1], probs[:], AXX, ALU.add))
            then(V_.reciprocal(stat[:, 1], stat[:, 1]))
            then(V_.tensor_tensor(probs[:], probs[:], tok(stat[:, 1]), ALU.mult))

            def best(src, onehot, value):
                then(V_.tensor_reduce(value, src, AXX, ALU.max))
                then(V_.tensor_tensor(far[:], src, tok(value), ALU.is_lt))
                then(V_.scalar_tensor_tensor(out=far[:], in0=far[:], scalar=float(EXPERTS), in1=counts[:],
                                             op0=ALU.mult, op1=ALU.add))
                then(V_.tensor_reduce(stat[:, 6], far[:], AXX, ALU.min))
                then(V_.tensor_tensor(onehot[:], counts[:], tok(stat[:, 6]), ALU.is_equal))

            best(probs[:], best_one, stat[:, 2])
            then(V_.scalar_tensor_tensor(out=rest[:], in0=best_one[:], scalar=-2.0, in1=probs[:],
                                         op0=ALU.mult, op1=ALU.add))
            best(rest[:], next_one, stat[:, 3])
            then(V_.tensor_tensor(rest[:], best_one[:], next_one[:], ALU.add))
            V_.tensor_tensor(picked[:], rest[:], valid[:], ALU.mult).then_inc(routed, 1)
            then(V_.tensor_tensor(stat[:, 7], stat[:, 2], stat[:, 3], ALU.add))
            then(V_.reciprocal(stat[:, 7], stat[:, 7]))
            for k in range(2):
                then(V_.tensor_tensor(stat[:, 4 + k], stat[:, 2 + k], stat[:, 7], ALU.mult))
            then(V_.tensor_tensor(gate[:], best_one[:], tok(stat[:, 4]), ALU.mult))
            then(V_.tensor_tensor(rest[:], next_one[:], tok(stat[:, 5]), ALU.mult))
            V_.tensor_tensor(gate[:], gate[:], rest[:], ALU.add).then_inc(routed, 1)
            dve.wait_ge(rank_mm, 1)
            total = bank[1][:, 256:256 + TILES * EXPERTS].rearrange("p (t e) -> p t e", e=EXPERTS)
            for t in range(TILES):
                then(V_.tensor_tensor(ahead[:, t + 1], total[:, t], ahead[:, t], ALU.add))
            then(V_.tensor_tensor(need[:], spread(ahead[:, TILES], EXPERTS, TILES), limits[:], ALU.is_gt))
            then(V_.tensor_reduce(per_expert[:, 0], need[:], AXX, ALU.add))
            then(V_.tensor_tensor(tri[:], repeat(per_expert[:, 0], EXPERTS, EXPERTS), upto[:], ALU.mult))
            then(V_.tensor_reduce(per_expert[:, 1], tri[:], AXX, ALU.add))
            then(V_.tensor_tensor(past[:], repeat(per_expert[:, 1], NT, EXPERTS), tile_no[:], ALU.is_le))
            then(V_.tensor_reduce(owner_f[:], past[:], AXX, ALU.add))
            then(V_.tensor_scalar(owner[:], owner_f[:], float(EXPERTS - 1), None, ALU.min))
            then(V_.tensor_tensor(per_expert[:, 2], per_expert[:, 1], per_expert[:, 0], ALU.subtract))
            then(V_.tensor_scalar(per_expert[:, 2], per_expert[:, 2], float(P), None, ALU.mult))
            rank = bank[1][:, 0:TILES * EXPERTS].rearrange("p (t e) -> p t e", e=EXPERTS)
            then(V_.tensor_tensor(slot_of[:], rank, ahead[:, 0:TILES], ALU.add))
            then(V_.tensor_tensor(slot_of[:], slot_of[:], repeat(per_expert[:, 2], TILES, EXPERTS), ALU.add))
            for k, onehot in enumerate((best_one, next_one)):
                then(V_.tensor_tensor(of_slot[:], slot_of[:], onehot[:], ALU.mult))
                then(V_.tensor_reduce(stat[:, 6 + k], of_slot[:], AXX, ALU.add))
            V_.tensor_copy(slots[:], stat[:, 6:8]).then_inc(placed, 1)
            for t in range(TILES):
                dve.wait_ge(turn_mm, t + 1)
                V_.tensor_copy(gate_t[:, t], bank[4 + t % 2][0:EXPERTS, 0:P]).then_inc(turned, 1)
            for t in range(TILES):
                dve.wait_ge(base_mm, t + 1)
                dve.wait_ge(rows_copied, t + 1)
                V_.tensor_tensor(acc[:, t], bank[6 + t % 2][:, 0:E], rows[:, t], ALU.add).then_inc(based, 1)

            def copy_features(j, q, peeled):
                dve.wait_ge(feat_mm, j + 1)
                if not peeled:
                    dve.wait_ge(fc_mm, 2 * (j - 1))
                V_.tensor_copy(features[:, q].rearrange("p h n -> p (h n)"), bank[q][0:EH, 0:2 * P])\
                    .then_inc(feat_copied, 1)

            def copy_result(j, i, peeled):
                dve.wait_ge(proj_mm, j + 1)
                if not peeled:
                    dve.wait_ge(y_out[i], 4 * (j - i))
                V_.tensor_copy(result[:, i], bank[6 + i % 2][:, 0:E]).then_inc(proj_copied, 1)

            for j in range(2 * XT):
                copy_features(j, j % 2, j < 2)
                if j >= 2:
                    copy_result(j - 2, (j - 2) % XT, j - 2 < XT)
            with dve.Fori(2, NT // XT) as k:
                for i in range(XT):
                    copy_features(k * XT + i, i % 2, False)
                    copy_result(k * XT + i - 2, (i - 2) % XT, False)
            for j in (NT - 2, NT - 1):
                copy_result(j, j % XT, False)

            for g in range(TILES // TG):
                ts = slice(g * TG, (g + 1) * TG)
                a = acc[:, ts]
                wide = lambda v: spread(v[:, ts], TG, E)
                dve.wait_ge(y_in[g], 32 * TG)
                for t in range(g * TG, (g + 1) * TG):
                    r = tile_rows[t]
                    for k in range(2):
                        n = 2 * t + k
                        if k:
                            dve.wait_ge(added, n)
                        ins = V_.scalar_tensor_tensor(out=acc[0:r, t], in0=results[0:r, t, k],
                                                      scalar=stat[0:r, 4 + k, t:t + 1], in1=acc[0:r, t],
                                                      op0=ALU.mult, op1=ALU.add)
                        ins.then_inc(added, 1)
                dve.wait_ge(added, 2 * TG * (g + 1))
                then(V_.tensor_reduce(stat[:, 9, ts], a, AXX, ALU.add))
                then(V_.tensor_scalar(stat[:, 9, ts], stat[:, 9, ts], 1.0 / E, None, ALU.mult))
                then(V_.tensor_tensor(a, a, wide(stat[:, 9]), ALU.subtract))
                then(V_.tensor_tensor(square[:], a, a, ALU.mult))
                then(V_.tensor_reduce(stat[:, 8, ts], square[:], AXX, ALU.add))
                v = stat[:, 8, ts]
                V_.tensor_scalar(v, v, 1.0 / E, EPS, ALU.mult, ALU.add).then_inc(std_in, 1)
                dve.wait_ge(std_done, g + 1)
                then(V_.reciprocal(v, v))
                V_.tensor_tensor(a, a, wide(stat[:, 8]), ALU.mult).then_inc(out_ready, 1)


def vit_tower(nc, d, out):
    scratch = {
        "power": nc.dram_tensor("power", [ROWS, IMAGES], F32).ap(),
        "left_cols": nc.dram_tensor("left_cols", [IMAGES, NL, U], F32).ap(),
        "left_rows": nc.dram_tensor("left_rows", [IMAGES, NL, U], F32).ap(),
        "slots": nc.dram_tensor("slot_rows_dram", [SLOTS, E], F32).ap(),
        "results": nc.dram_tensor("results_dram", [SLOTS, E], F32).ap(),
    }
    with ExitStack() as ctx:
        sb = lambda n, s: ctx.enter_context(nc.sbuf_tensor(n, s, F32))
        ident = sb("ident", [P, P])
        h1 = sb("h1", [EH, 2, TILES * P])
        token_rows = sb("token_rows", [P, TILES, E])
        logits = sb("logits", [P, TILES, EXPERTS])
        tables = {name: sb(name + "_table", shape) for name, shape in expert_tables().items()}
        with ExitStack() as until_tokens:
            weight = until_tokens.enter_context(nc.sbuf_tensor("weight", [P, JC, C, E], F32))
            rows = until_tokens.enter_context(nc.sbuf_tensor("rows", [P, BINS * JC], I32))
            dft_phase(nc, d, scratch, weight, rows, ident, token_rows[:].rearrange("p t e -> p (t e)"))
            token_attention_phase(nc, d, scratch, weight, rows, ident, tables, h1, logits)
        expert_phase(nc, d, h1, logits, ident, tables, scratch, token_rows, out)


def layout(x, L0_tok_cls_token, L0_tok_W, L0_tok_b, **w):
    x = np.asarray(x)
    order = [((b - B // 2) % B, (c - C // 2) % C) for b in range(B) for c in range(C)]
    flat = x.reshape(B * C, N, N)
    src = np.array([b * C + c for b, c in order])
    rows = np.concatenate(FOLDED)
    main = np.empty((IMAGES, P, 4, 4 * P), np.float32)
    cols = np.empty((IMAGES, NL, 4, P), np.float32)
    for n, k in enumerate(src):
        image = flat[k]
        picked = image[rows]
        main[n] = picked[:, rows].reshape(4, P, 4 * P).transpose(1, 0, 2)
        cols[n] = picked[:, LEFT].T.reshape(NL, 4, P)
    left = flat[src][:, LEFT]
    chunks = lambda a: np.ascontiguousarray(
        a.reshape(-1, P, 4, P).transpose(0, 3, 2, 1))
    corner = left[:, :, LEFT].reshape(-1, P, NL).transpose(0, 2, 1)
    per_half = lambda a: np.ascontiguousarray(
        np.asarray(a).reshape(2, EH, -1).transpose(1, 0, 2))
    w = {name: np.asarray(a) for name, a in w.items()}
    of_head, feat_feat, row_feat = head_masks()
    tab = trig(np.concatenate(FOLDED)).reshape(4, P, U).transpose(1, 0, 2)
    return {
        "x": main,
        "x_cols": chunks(cols),
        "x_rows": chunks(left[:, :, rows].reshape(IMAGES, NL, 4, P)),
        "x_corner": np.ascontiguousarray(corner),
        "ktab": folded_trig(), "full": np.ascontiguousarray(tab), "left": trig(LEFT),
        "rows": radial_rows(), "code": position_code(),
        "tok_w": np.ascontiguousarray(np.asarray(L0_tok_W).reshape(E, C, JC, P).transpose(3, 2, 1, 0)),
        "tok_b": per_half(np.asarray(L0_tok_b))[:, :, 0],
        "cls": per_half(np.asarray(L0_tok_cls_token).reshape(E))[:, :, 0],
        "down": np.ascontiguousarray(np.stack([per_half(w["L0_attn_V_" + n]) for n in "QKV"], 1)),
        "up": np.ascontiguousarray(np.stack([w["L0_attn_U_" + n] for n in "QKV"], 1)),
        "bias": np.ascontiguousarray(np.stack([per_half(w["L0_attn_bias_" + n])[:, :, 0] for n in "qkv"], 1)),
        "m_u": np.ascontiguousarray(np.tile(np.asarray(w["L0_attn_M_U"]).T, (1, HH))),
        "m_v": np.ascontiguousarray(np.tile(w["L0_attn_M_V"], (1, HH))),
        "of_head": of_head, "feat_feat": feat_feat, "row_feat": row_feat,
        "w_router": per_half(w["L0_ffn_Wr"]),
        "b_router": np.ascontiguousarray(np.broadcast_to(np.asarray(w["L0_ffn_br"]), (P, TILES, EXPERTS))),
        "ident": np.eye(P, dtype=np.float32),
        **routing_tables(),
        "b_fc": np.ascontiguousarray(np.asarray(w["L0_ffn_bfc"]).reshape(EXPERTS, FC, P).transpose(0, 2, 1)),
        "b_proj": np.asarray(w["L0_ffn_bproj"]),
        "w_fc": np.ascontiguousarray(np.asarray(w["L0_ffn_Wfc"]).reshape(EXPERTS, 2, EH, FF).transpose(0, 2, 1, 3)),
        "w_proj": np.ascontiguousarray(
            np.asarray(w["L0_ffn_Wproj"]).reshape(EXPERTS, FC, P, E).transpose(0, 2, 1, 3)),
    }


def kernel(**inputs):
    import concourse.bacc as bacc
    from concourse.bass_utils import run_bass_kernel_spmd as run

    nc = bacc.Bacc("TRN2", target_bir_lowering=False, num_devices=1)
    arrays, aps = {}, {}
    for name, a in layout(**inputs).items():
        a = np.ascontiguousarray(a)
        arrays[f"in_{name}"] = a
        aps[name] = nc.dram_tensor(f"in_{name}", list(a.shape), mybir.dt.from_np(a.dtype),
                                   kind="ExternalInput").ap()
    out = nc.dram_tensor("tokens_out", [B, S, E], F32, kind="ExternalOutput").ap()
    vit_tower(nc, aps, out)
    return run(nc, [arrays], core_ids=[0]).results[0]["tokens_out"]
```
